# Optimizing a Trainium2 kernel written in Bass

```python
import numpy as np
import jax
import jax.numpy as jnp

def _softmax(x, axis=-1):
    return jax.nn.softmax(x, axis=axis)

def _gelu(x):
    return jax.nn.gelu(x, approximate=True)

def _silu(x):
    return jax.nn.silu(x)

def _sigmoid(x):
    return jax.nn.sigmoid(x)

def _layernorm(x, axis=-1, eps=1e-05):
    m = jnp.mean(x, axis=axis, keepdims=True)
    v = jnp.var(x, axis=axis, keepdims=True)
    return (x - m) / jnp.sqrt(v + eps)

def _scatter_add(tgt, idx, src, axis=0):
    return tgt.at[idx].add(src)

def _segment_sum(src, seg, n):
    return jax.ops.segment_sum(src, seg, n)
kernel_name = 'mk_decoder_preln_d1_seqx_r8_77fd4f'

def setup_inputs(seed: int=0):
    np.random.seed(seed)
    _w = jnp.asarray

    def _rec_inputs():
        import jax
        import jax.numpy as jnp
        _rk = jax.random.key(seed)
        x = 7.22e-05 + 1 * jax.random.normal(jax.random.fold_in(_rk, 1), (8, 128, 128), jnp.float32)
        _lenS = 128 - jax.random.randint(jax.random.fold_in(_rk, 7), (8,), 0, max(1, 128 // 4) + 1, jnp.int32)
        _lenS2 = 128 - jax.random.randint(jax.random.fold_in(_rk, 8), (8,), 0, max(1, 128 // 4) + 1, jnp.int32)
        _ctx_1024P = jax.random.normal(jax.random.fold_in(_rk, 11), (8, 16, 128), jnp.float32)
        _ctx_1024c = jax.random.dirichlet(jax.random.fold_in(_rk, 511), 0.3 * jnp.ones((16,), jnp.float32), (8, 128))
        _ctx_1024t = jnp.einsum('bsk,bkd->bsd', _ctx_1024c, _ctx_1024P)
        _ctx_1024t = _ctx_1024t * jax.lax.rsqrt(jnp.mean(jnp.square(_ctx_1024t)) + 1e-12) * 0.953939
        ctx_1024 = 4.13588e-05 + 0.999923 * (_ctx_1024t + 0.3 * jax.random.normal(jax.random.fold_in(_rk, 611), (8, 128, 128), jnp.float32))
        _validS = jnp.arange(128)[None, :] < _lenS[:, None]
        _validS2 = jnp.arange(128)[None, :] < _lenS2[:, None]
        _causal = jnp.tril(jnp.ones((128, 128), dtype=bool))
        mask_Bx1xSxS2_bk1 = jnp.broadcast_to(_validS2[:, None, None, :], (8, 1, 128, 128))
        return (x, ctx_1024, mask_Bx1xSxS2_bk1)
    x, ctx_1024, mask_Bx1xSxS2_bk1 = _rec_inputs()

    def _L0_attn_setup():
        import jax, jax.numpy as jnp
        import numpy as np
        from math import sqrt
        D, H, B, L = (128, 16, 2, 256)
        DK = D // H

        def linear(x, w, b):
            return x @ w.T + b

        def conv1d(x, w, b, padding, groups=1):
            y = jax.lax.conv_general_dilated(x, w, window_strides=(1,), padding=(padding,), dimension_numbers=('NCH', 'OIH', 'NCH'), feature_group_count=groups)
            return y + b[None, :, None]
        key = jax.random.key(seed)
        ks = jax.random.split(key, 26)

        def n(k, shape, s=0.02):
            return jax.random.normal(k, shape, jnp.float32) * s
        return {'x': jax.random.normal(ks[0], (B, L, D), jnp.float32), 'Wq_w': n(ks[1], (D, D)), 'Wq_b': n(ks[2], (D,)), 'Wk_w': n(ks[3], (D, D)), 'Wk_b': n(ks[4], (D,)), 'Wv_w': n(ks[5], (D, D)), 'Wv_b': n(ks[6], (D,)), 'convq_w': n(ks[7], (D, D, 3)), 'convq_b': n(ks[8], (D,)), 'convk_w': n(ks[9], (D, D, 3)), 'convk_b': n(ks[10], (D,)), 'qproj_w': n(ks[11], (D, 2 * D)), 'qproj_b': n(ks[12], (D,)), 'kproj_w': n(ks[13], (D, 2 * D)), 'kproj_b': n(ks[14], (D,)), 'tau1_w': n(ks[15], (2 * D, 1, 3)), 'tau1_b': n(ks[16], (2 * D,)), 'tau2_w': n(ks[17], (H, 2 * D, 1)), 'tau2_b': n(ks[18], (H,)), 'del1_w': n(ks[19], (2 * D, 1, 3)), 'del1_b': n(ks[20], (2 * D,)), 'del2_w': n(ks[21], (H, 2 * D, 1)), 'del2_b': n(ks[22], (H,)), 'out_w': n(ks[23], (D, D)), 'out_b': n(ks[24], (D,))}
    _L0_attn_all = _L0_attn_setup()
    _L0_attn_in = {k: v for k, v in _L0_attn_all.items() if k in ('Wq_w', 'Wq_b', 'Wk_w', 'Wk_b', 'Wv_w', 'Wv_b', 'convq_w', 'convq_b', 'convk_w', 'convk_b', 'qproj_w', 'qproj_b', 'kproj_w', 'kproj_b', 'tau1_w', 'tau1_b', 'tau2_w', 'tau2_b', 'del1_w', 'del1_b', 'del2_w', 'del2_b', 'out_w', 'out_b')}
    del _L0_attn_all

    def _L0_xattn_setup():
        import jax, jax.numpy as jnp
        import numpy as np
        B, S, D, H = (4, 256, 128, 16)
        HD = D // H
        key = jax.random.key(seed)
        ks = jax.random.split(key, 12)
        scale = 1.0 / np.sqrt(D)
        inp = {'queries': jax.random.normal(ks[0], (B, S, D), jnp.float32), 'keys': jax.random.normal(ks[1], (B, S, D), jnp.float32), 'values': jax.random.normal(ks[2], (B, S, D), jnp.float32), 'mask': jax.random.randint(ks[3], (B, 1, S, S), 0, 2).astype(bool), 'Wq': jax.random.normal(ks[4], (D, D), jnp.float32) * scale, 'bq': jnp.zeros((D,), jnp.float32), 'Wk': jax.random.normal(ks[5], (D, D), jnp.float32) * scale, 'bk': jnp.zeros((D,), jnp.float32), 'Wv': jax.random.normal(ks[6], (D, D), jnp.float32) * scale, 'bv': jnp.zeros((D,), jnp.float32), 'Wo': jax.random.normal(ks[7], (D, D), jnp.float32) * scale, 'bo': jnp.zeros((D,), jnp.float32)}
        return inp
    _L0_xattn_all = _L0_xattn_setup()
    _L0_xattn_in = {k: v for k, v in _L0_xattn_all.items() if k in ('Wq', 'bq', 'Wk', 'bk', 'Wv', 'bv', 'Wo', 'bo')}
    del _L0_xattn_all

    def _L0_ffn_setup():
        import jax, jax.numpy as jnp
        import numpy as np
        H = 128
        I = 64
        E = 64
        G = 8
        TOPK_GROUP = 4
        K = 8
        I_SH = 128
        SCALE = 2.5

        def _route(x, router_w, e_bias):
            T = x.shape[0]
            scores = jax.nn.sigmoid(x.astype(jnp.float32) @ router_w.T.astype(jnp.float32))
            sfc = jax.lax.stop_gradient(scores) + e_bias[None, :]
            group_scores = jax.lax.top_k(sfc.reshape(T, G, E // G), 2)[0].sum(-1)
            _, gidx = jax.lax.top_k(group_scores, TOPK_GROUP)
            gmask = jax.nn.one_hot(gidx, G, dtype=sfc.dtype).sum(1)
            smask = jnp.repeat(gmask, E // G, axis=1)
            masked = jnp.where(smask > 0, sfc, 0.0)
            _, topk_idx = jax.lax.top_k(masked, K)
            w = jnp.take_along_axis(scores, topk_idx, axis=1)
            w = w / (w.sum(-1, keepdims=True) + 1e-20)
            return (topk_idx, w * SCALE)
        key = jax.random.key(seed)
        ks = jax.random.split(key, 9)
        s = 0.02
        return {'hidden_states': jax.random.normal(ks[0], (2, 128, H), jnp.float32), 'router_w': jax.random.normal(ks[1], (E, H), jnp.float32) * s, 'e_bias': jnp.zeros((E,), jnp.float32), 'Wg': jax.random.normal(ks[2], (E, H, I), jnp.float32) * s, 'Wu': jax.random.normal(ks[3], (E, H, I), jnp.float32) * s, 'Wd': jax.random.normal(ks[4], (E, I, H), jnp.float32) * s, 'SWg': jax.random.normal(ks[5], (H, I_SH), jnp.float32) * s, 'SWu': jax.random.normal(ks[6], (H, I_SH), jnp.float32) * s, 'SWd': jax.random.normal(ks[7], (I_SH, H), jnp.float32) * s}
    _L0_ffn_all = _L0_ffn_setup()
    _L0_ffn_in = {k: v for k, v in _L0_ffn_all.items() if k in ('router_w', 'e_bias', 'Wg', 'Wu', 'Wd', 'SWg', 'SWu', 'SWd')}
    del _L0_ffn_all
    return {'x': x, 'ctx_1024': ctx_1024, 'mask_Bx1xSxS2_bk1': mask_Bx1xSxS2_bk1, 'L0_attn_Wq_w': _L0_attn_in['Wq_w'], 'L0_attn_Wq_b': _L0_attn_in['Wq_b'], 'L0_attn_Wk_w': _L0_attn_in['Wk_w'], 'L0_attn_Wk_b': _L0_attn_in['Wk_b'], 'L0_attn_Wv_w': _L0_attn_in['Wv_w'], 'L0_attn_Wv_b': _L0_attn_in['Wv_b'], 'L0_attn_convq_w': _L0_attn_in['convq_w'], 'L0_attn_convq_b': _L0_attn_in['convq_b'], 'L0_attn_convk_w': _L0_attn_in['convk_w'], 'L0_attn_convk_b': _L0_attn_in['convk_b'], 'L0_attn_qproj_w': _L0_attn_in['qproj_w'], 'L0_attn_qproj_b': _L0_attn_in['qproj_b'], 'L0_attn_kproj_w': _L0_attn_in['kproj_w'], 'L0_attn_kproj_b': _L0_attn_in['kproj_b'], 'L0_attn_tau1_w': _L0_attn_in['tau1_w'], 'L0_attn_tau1_b': _L0_attn_in['tau1_b'], 'L0_attn_tau2_w': _L0_attn_in['tau2_w'], 'L0_attn_tau2_b': _L0_attn_in['tau2_b'], 'L0_attn_del1_w': _L0_attn_in['del1_w'], 'L0_attn_del1_b': _L0_attn_in['del1_b'], 'L0_attn_del2_w': _L0_attn_in['del2_w'], 'L0_attn_del2_b': _L0_attn_in['del2_b'], 'L0_attn_out_w': _L0_attn_in['out_w'], 'L0_attn_out_b': _L0_attn_in['out_b'], 'L0_xattn_Wq': _L0_xattn_in['Wq'], 'L0_xattn_bq': _L0_xattn_in['bq'], 'L0_xattn_Wk': _L0_xattn_in['Wk'], 'L0_xattn_bk': _L0_xattn_in['bk'], 'L0_xattn_Wv': _L0_xattn_in['Wv'], 'L0_xattn_bv': _L0_xattn_in['bv'], 'L0_xattn_Wo': _L0_xattn_in['Wo'], 'L0_xattn_bo': _L0_xattn_in['bo'], 'L0_ffn_router_w': _L0_ffn_in['router_w'], 'L0_ffn_e_bias': _L0_ffn_in['e_bias'], 'L0_ffn_Wg': _L0_ffn_in['Wg'], 'L0_ffn_Wu': _L0_ffn_in['Wu'], 'L0_ffn_Wd': _L0_ffn_in['Wd'], 'L0_ffn_SWg': _L0_ffn_in['SWg'], 'L0_ffn_SWu': _L0_ffn_in['SWu'], 'L0_ffn_SWd': _L0_ffn_in['SWd']}

def reference(x, ctx_1024, mask_Bx1xSxS2_bk1, L0_attn_Wq_w, L0_attn_Wq_b, L0_attn_Wk_w, L0_attn_Wk_b, L0_attn_Wv_w, L0_attn_Wv_b, L0_attn_convq_w, L0_attn_convq_b, L0_attn_convk_w, L0_attn_convk_b, L0_attn_qproj_w, L0_attn_qproj_b, L0_attn_kproj_w, L0_attn_kproj_b, L0_attn_tau1_w, L0_attn_tau1_b, L0_attn_tau2_w, L0_attn_tau2_b, L0_attn_del1_w, L0_attn_del1_b, L0_attn_del2_w, L0_attn_del2_b, L0_attn_out_w, L0_attn_out_b, L0_xattn_Wq, L0_xattn_bq, L0_xattn_Wk, L0_xattn_bk, L0_xattn_Wv, L0_xattn_bv, L0_xattn_Wo, L0_xattn_bo, L0_ffn_router_w, L0_ffn_e_bias, L0_ffn_Wg, L0_ffn_Wu, L0_ffn_Wd, L0_ffn_SWg, L0_ffn_SWu, L0_ffn_SWd):
    import jax
    import jax.numpy as jnp

    def _L0_attn_ref(x, Wq_w, Wq_b, Wk_w, Wk_b, Wv_w, Wv_b, convq_w, convq_b, convk_w, convk_b, qproj_w, qproj_b, kproj_w, kproj_b, tau1_w, tau1_b, tau2_w, tau2_b, del1_w, del1_b, del2_w, del2_b, out_w, out_b):
        import jax, jax.numpy as jnp
        import numpy as np
        from math import sqrt
        D, H, B, L = (128, 16, 2, 256)
        DK = D // H

        def linear(x, w, b):
            return x @ w.T + b

        def conv1d(x, w, b, padding, groups=1):
            y = jax.lax.conv_general_dilated(x, w, window_strides=(1,), padding=(padding,), dimension_numbers=('NCH', 'OIH', 'NCH'), feature_group_count=groups)
            return y + b[None, :, None]
        b_, l_, _ = x.shape
        q_in = linear(x, Wq_w, Wq_b).transpose(0, 2, 1)
        Q3 = conv1d(q_in, convq_w, convq_b, (1, 1))
        Q_cat = jnp.concatenate([q_in, Q3], axis=1).transpose(0, 2, 1)
        Q = linear(Q_cat, qproj_w, qproj_b).reshape(b_, l_, H, DK).transpose(0, 2, 1, 3)
        k_in = linear(x, Wk_w, Wk_b).transpose(0, 2, 1)
        K3 = conv1d(k_in, convk_w, convk_b, (1, 1))
        K_cat = jnp.concatenate([k_in, K3], axis=1).transpose(0, 2, 1)
        K = linear(K_cat, kproj_w, kproj_b).reshape(b_, l_, H, DK).transpose(0, 2, 1, 3)
        V = linear(x, Wv_w, Wv_b).reshape(b_, l_, H, DK).transpose(0, 2, 1, 3)
        x_conv = x.transpose(0, 2, 1)
        tau = jax.nn.sigmoid(conv1d(jax.nn.gelu(conv1d(x_conv, tau1_w, tau1_b, (1, 1), groups=D), approximate=False), tau2_w, tau2_b, (0, 0)))
        delta = jax.nn.sigmoid(conv1d(jax.nn.gelu(conv1d(x_conv, del1_w, del1_b, (1, 1), groups=D), approximate=False), del2_w, del2_b, (0, 0)))
        scores = jnp.einsum('bhqd,bhkd->bhqk', Q, K) / sqrt(DK)
        scores = scores * tau[..., None] + delta[:, :, None, :]
        attn = jax.nn.softmax(scores, axis=-1)
        out = jnp.einsum('bhqk,bhkd->bhqd', attn, V)
        out = out.transpose(0, 2, 1, 3).reshape(b_, l_, D)
        return linear(out, out_w, out_b)

    def _L0_xattn_ref(queries, keys, values, mask, Wq, bq, Wk, bk, Wv, bv, Wo, bo):
        import jax, jax.numpy as jnp
        import numpy as np
        B, S, D, H = (4, 256, 128, 16)
        HD = D // H
        b, sq, d = queries.shape

        def split_heads(x):
            return x.reshape(b, x.shape[1], H, HD).transpose(0, 2, 1, 3)
        q = split_heads(queries @ Wq + bq)
        k = split_heads(keys @ Wk + bk)
        v = split_heads(values @ Wv + bv)
        scores = jnp.einsum('bhqd,bhkd->bhqk', q, k) / jnp.sqrt(jnp.float32(HD))
        scores = jnp.where(mask, jnp.float32(-1000000000000000.0), scores)
        attn = jax.nn.softmax(scores, axis=-1)
        ctx = jnp.einsum('bhqk,bhkd->bhqd', attn, v)
        ctx = ctx.transpose(0, 2, 1, 3).reshape(b, sq, d)
        return ctx @ Wo + bo

    def _L0_ffn_ref(hidden_states, router_w, e_bias, Wg, Wu, Wd, SWg, SWu, SWd):
        import jax, jax.numpy as jnp
        import numpy as np
        H = 128
        I = 64
        E = 64
        G = 8
        TOPK_GROUP = 4
        K = 8
        I_SH = 128
        SCALE = 2.5

        def _route(x, router_w, e_bias):
            T = x.shape[0]
            scores = jax.nn.sigmoid(x.astype(jnp.float32) @ router_w.T.astype(jnp.float32))
            sfc = jax.lax.stop_gradient(scores) + e_bias[None, :]
            group_scores = jax.lax.top_k(sfc.reshape(T, G, E // G), 2)[0].sum(-1)
            _, gidx = jax.lax.top_k(group_scores, TOPK_GROUP)
            gmask = jax.nn.one_hot(gidx, G, dtype=sfc.dtype).sum(1)
            smask = jnp.repeat(gmask, E // G, axis=1)
            masked = jnp.where(smask > 0, sfc, 0.0)
            _, topk_idx = jax.lax.top_k(masked, K)
            w = jnp.take_along_axis(scores, topk_idx, axis=1)
            w = w / (w.sum(-1, keepdims=True) + 1e-20)
            return (topk_idx, w * SCALE)
        orig_shape = hidden_states.shape
        x = hidden_states.reshape(-1, orig_shape[-1])
        T = x.shape[0]
        topk_idx, topk_w = _route(x, router_w, e_bias)
        coef = jnp.zeros((T, E), topk_w.dtype).at[jnp.arange(T)[:, None], topk_idx].add(topk_w)
        g = jnp.einsum('th,ehi->tei', x, Wg)
        u = jnp.einsum('th,ehi->tei', x, Wu)
        h = jax.nn.silu(g) * u * coef[:, :, None]
        moe_out = jnp.einsum('tei,eih->th', h, Wd)
        shared = jax.nn.silu(x @ SWg) * (x @ SWu) @ SWd
        return (moe_out + shared).reshape(orig_shape)
    x = x + _L0_attn_ref(_layernorm(x, axis=-1), L0_attn_Wq_w, L0_attn_Wq_b, L0_attn_Wk_w, L0_attn_Wk_b, L0_attn_Wv_w, L0_attn_Wv_b, L0_attn_convq_w, L0_attn_convq_b, L0_attn_convk_w, L0_attn_convk_b, L0_attn_qproj_w, L0_attn_qproj_b, L0_attn_kproj_w, L0_attn_kproj_b, L0_attn_tau1_w, L0_attn_tau1_b, L0_attn_tau2_w, L0_attn_tau2_b, L0_attn_del1_w, L0_attn_del1_b, L0_attn_del2_w, L0_attn_del2_b, L0_attn_out_w, L0_attn_out_b)
    x = x + _L0_xattn_ref(_layernorm(x, axis=-1), ctx_1024, ctx_1024, mask_Bx1xSxS2_bk1, L0_xattn_Wq, L0_xattn_bq, L0_xattn_Wk, L0_xattn_bk, L0_xattn_Wv, L0_xattn_bv, L0_xattn_Wo, L0_xattn_bo)
    x = x + _L0_ffn_ref(_layernorm(x, axis=-1), L0_ffn_router_w, L0_ffn_e_bias, L0_ffn_Wg, L0_ffn_Wu, L0_ffn_Wd, L0_ffn_SWg, L0_ffn_SWu, L0_ffn_SWd)
    return x

_drawn_inputs = setup_inputs


def setup_inputs(seed=0):
    import zlib

    import numpy as np

    out = dict(_drawn_inputs(seed))
    spreads = {'L0_xattn_bq': (0.0, 0.284),
     'L0_xattn_bk': (0.0, 2.0),
     'L0_xattn_bv': (0.0, 0.1),
     'L0_xattn_bo': (0.0, 0.1),
     'L0_ffn_e_bias': (0.0, 0.8)}
    factors = {'L0_attn_Wq_w': 8.0,
     'L0_attn_Wq_b': 8.0,
     'L0_attn_Wk_w': 8.0,
     'L0_attn_Wk_b': 8.0,
     'L0_attn_Wv_w': 8.0,
     'L0_attn_Wv_b': 8.0,
     'L0_attn_convq_w': 8.0,
     'L0_attn_convq_b': 8.0,
     'L0_attn_convk_w': 8.0,
     'L0_attn_convk_b': 64.0,
     'L0_attn_qproj_w': 8.0,
     'L0_attn_qproj_b': 8.0,
     'L0_attn_kproj_w': 8.0,
     'L0_attn_kproj_b': 64.0,
     'L0_attn_tau1_w': 8.0,
     'L0_attn_tau1_b': 8.0,
     'L0_attn_tau2_w': 8.0,
     'L0_attn_tau2_b': 8.0,
     'L0_attn_del1_w': 8.0,
     'L0_attn_del1_b': 64.0,
     'L0_attn_del2_w': 8.0,
     'L0_attn_del2_b': 64.0,
     'L0_attn_out_w': 8.0,
     'L0_attn_out_b': 3.333,
     'L0_ffn_router_w': 8.0,
     'L0_ffn_Wg': 8.0,
     'L0_ffn_Wu': 8.0,
     'L0_ffn_Wd': 8.0,
     'L0_ffn_SWg': 8.0,
     'L0_ffn_SWu': 8.0,
     'L0_ffn_SWd': 8.0}
    for name, (base, spread) in spreads.items():
        noise = np.random.default_rng([zlib.crc32(name.encode()), seed]).standard_normal(out[name].shape)
        drawn = base * np.exp(spread * noise) if base else spread * noise
        out[name] = jnp.asarray(drawn.astype(out[name].dtype))
    for name, factor in factors.items():
        out[name] = (out[name] * factor).astype(out[name].dtype)
    return out
```

```python
from contextlib import ExitStack

import concourse.bass as bass
from concourse import mybir

F32 = mybir.dt.float32
F32R = mybir.dt.float32r
F16 = mybir.dt.float16
BF16 = mybir.dt.bfloat16
I32 = mybir.dt.int32
U8 = mybir.dt.uint8
ALU = mybir.AluOpType
ACT = mybir.ActivationFunctionType
AX = mybir.AxisListType

P = 128
B = 8
T = B * P
H, DK = 16, 8
G = 4
J = H // G
HALF = T // 2
E, I = 64, 64
PAIRS = E * I // P
GE = 8
TOP_GROUPS, TOP_K = 4, 8
ROUTE_SCALE = 2.5
EPS = 1e-5
SCALE = DK ** -0.5
MASKED = -1e15 / SCALE
RSQRT_MAGIC = 1597463007.0

PACK_A = dict(ident=P, wqT=P, wkT=P, wvT=P, cq=3 * P, ck=3 * P, qp1T=P, qp2T=P, kp1T=P, kp2T=P,
              tau1=6, tau1b=2, del1=6, del1b=2, tau2T=32, del2T=32,
              bq=1, bk=1, cqb=1, ckb=1, qpb=1, kpb=1, tau2b=1, woT=P, bv=P, bo=P, del2b=H)
PACK_B = dict(wq=P, wk=P, wv=P, wo=P, bq=1, bk=1, bv=P, bo=P, routerT=E, e_bias=E)


def columns(pack):
    at, out = 0, {}
    for name, n in pack.items():
        out[name] = (at, at + n)
        at += n
    return out, at


def decoder_layer(nc, x, ctxT, mask, pack_a, pack_b, w3, outT):
    cols_a, n_a = columns(PACK_A)
    cols_b, n_b = columns(PACK_B)

    with ExitStack() as ctx:
        def sb(name, shape, dt=F32):
            return ctx.enter_context(nc.sbuf_tensor(name, shape, dt))

        def sem(name):
            return ctx.enter_context(nc.semaphore(name))

        bank = [ctx.enter_context(nc.psum_tensor(f"bank{i}", [P, 512], F32)) for i in range(8)]

        pa = sb("pa", [P, n_a])
        pb = sb("pb", [P, n_b])
        A = lambda name: pa[:, cols_a[name][0]:cols_a[name][1]]
        Bw = lambda name: pb[:, cols_b[name][0]:cols_b[name][1]]
        ident = A("ident")
        w3s = sb("w3s", [P, PAIRS + 2, 3, P])
        xres = sb("xres", [P, B, P])
        xn = sb("xn", [P, B, P])
        xnT = sb("xnT", [P, B, P + 2])
        qin = sb("qin", [P, B, P + 2])
        kin = sb("kin", [P, B, P + 2])
        ctxs = sb("ctxs", [P, B, P])
        masku = sb("masku", [P, B, P], U8)
        maskb = sb("maskb", [P, B, P], BF16)
        identb = sb("identb", [P, P], BF16)
        stats = sb("stats", [P, B, 6])
        mv = sb("mv", [P, B, 2])
        nwt = sb("nwt", [P, 5, B])
        foldq = sb("foldq", [P, 3, P])
        foldk = sb("foldk", [P, 3, P])
        foldb = sb("foldb", [P, 2])
        conv = sb("conv", [P, 4, B, P])
        tau2r = sb("tau2r", [P, 2, H, DK])
        edelta = sb("edelta", [P, B, H])
        qc = sb("qc", [P, B, P])
        kc = [qin[:, :, 1:1 + P], sb("kc1", [P, B, P])]
        qs = sb("qs", [P, G, B, P])
        ks = sb("ks", [P, G, B, P])
        vs = [sb(f"vs{n}", [P, B, H, DK + 1]) for n in range(2)]
        qm = sb("qm", [P, 2, G, P])
        tauT = qm[:, :, :, :].rearrange("p i g t -> p (i g) t")
        negmax = sb("negmax", [P, G, P])
        probs = conv[:, 0:2, :, :].rearrange("p a b t -> p (a b t)").rearrange("p (i j t) -> p i j t", i=4, j=J)
        oT = sb("oT", [P, G, P])
        on = sb("on", [P, H, DK])
        rec = sb("rec", [P, H])
        onT = sb("onT", [P, P])
        xhl = sb("xhl", [P, 2, T], F32R)
        def over_qs(at, n):
            return qs[:, :, :, :].rearrange("p g b t -> p (g b t)")[:, at:at + n]

        sc, masked, replaced, coef = (over_qs(B * E * i, B * E).rearrange("p (b e) -> p b e", b=B) for i in range(4))
        sfc = over_qs(4 * B * E, B * E).rearrange("p (b g e) -> p b g e", b=B, g=GE)
        gcmp = over_qs(5 * B * E, 3 * B * E).rearrange("p (i b g f) -> p i b g f", i=3, b=B, g=GE)
        tmp = conv[:, 0:3, :, :].rearrange("p a b t -> p (a b t)").rearrange("p (i n) -> p i n", i=12)
        low = sb("low", [P, GE, GE])
        top8 = sb("top8", [P, B, 8])
        chl = sb("chl", [P, B, 2, E], F16)
        identh = sb("identh", [P, P], F16)
        cT = sb("cT", [P, T], F16)
        sel = sb("sel", [P, E, I], F16)
        i2 = sb("i2", [P, E])
        whigu = sb("whigu", [P, 2, 2, P], F32R)
        wlogu = sb("wlogu", [P, 2, 2, P], F32R)
        whid = sb("whid", [P, 2, P], F32R)
        wlod = sb("wlod", [P, 2, P], F32R)
        sg, gu, hx, outs = (ks[:, g, :, :].rearrange("p (c b) t -> p c (b t)", c=2) for g in range(G))
        hhi = sb("hhi", [P, 2, 512], F32R)
        hlo = sb("hlo", [P, 2, 512], F32R)

        ld_x, ld_a, ld_b, ld_ctx, ld_mask, ld_w = (sem(f"ld_{n}") for n in ("x", "a", "b", "ctx", "mask", "w"))
        dve_step = sem("dve_step")
        pool_step = sem("pool_step")
        pads_ready = sem("pads_ready")
        xn_ready = sem("xn_ready")
        xT_done = sem("xT_done")
        xT_copied = sem("xT_copied")
        folded = sem("folded")
        fold_copied = sem("fold_copied")
        in_done = sem("in_done")
        in_copied = sem("in_copied")
        v_done = sem("v_done")
        v_copied = sem("v_copied")
        conv_part = sem("conv_part")
        conv_done = sem("conv_done")
        gelu_done = sem("gelu_done")
        tau_done = sem("tau_done")
        tau_ready = sem("tau_ready")
        delta_done = sem("delta_done")
        delta_sum = sem("delta_sum")
        delta_ready = sem("delta_ready")
        q_done = sem("q_done")
        q_ready = sem("q_ready")
        k_done = sem("k_done")
        k_ready = sem("k_ready")
        k2_done = sem("k2_done")
        k2_ready = sem("k2_ready")
        spread_q = sem("spread_q")
        spread_k = sem("spread_k")
        mask_ready = sem("mask_ready")
        const_ready = sem("const_ready")
        layer = [{n: sem(f"{n}_{i}") for n in (
            "scored", "maxed", "max_turned", "qm_ready", "scoredT", "exped", "pv_done", "o_copied",
            "o_turned", "normed", "on_turned", "on_copied", "projected", "residual")} for i in range(2)]
        logits_done = sem("logits_done")
        scores_ready = sem("scores_ready")
        coef_ready = sem("coef_ready")
        coefT_done = sem("coefT_done")
        coefT_ready = sem("coefT_ready")
        xhi_ready = sem("xhi_ready")
        xlo_ready = sem("xlo_ready")
        x3T_ready = sem("x3T_ready")
        whigu_ready = sem("whigu_ready")
        wlogu_ready = sem("wlogu_ready")
        whid_ready = sem("whid_ready")
        wlod_ready = sem("wlod_ready")
        rows_ready = sem("rows_ready")
        ones_ready = sem("ones_ready")
        sel_ready = sem("sel_ready")
        bank5_zeroed = sem("bank5_zeroed")
        values_scaled = sem("values_scaled")
        coefb_done = sem("coefb_done")
        gate_done = sem("gate_done")
        up_done = sem("up_done")
        silu_done = sem("silu_done")
        gu_done = sem("gu_done")
        h_done = sem("h_done")
        hhi_ready = sem("hhi_ready")
        hlo_ready = sem("hlo_ready")
        down_done = sem("down_done")
        out_copied = sem("out_copied")
        stored = sem("stored")

        block = ctx.enter_context(nc.Block())

        @block.sync
        def _(sp):
            sp.dma_start(xres[:, :, :], x.rearrange("(b p) d -> p b d", p=P)).then_inc(ld_x, 16)
            sp.dma_start(pa[:, :], pack_a).then_inc(ld_a, 16)
            sp.dma_start(ctxs[:, :, :], ctxT.rearrange("p (b t) -> p b t", b=B)).then_inc(ld_ctx, 16)
            sp.dma_start(pb[:, :], pack_b).then_inc(ld_b, 16)
            sp.dma_start(masku[:, :, :], mask.rearrange("b q k -> q b k")).then_inc(ld_mask, 16)

            def spread(dst, src, signal):
                for h in range(H):
                    g, j = h // J, h % J
                    sp.dma_start(dst[32 * j + 1:32 * j + 1 + DK, g, :, :],
                                 src[DK * h:DK * h + DK, :, :]).then_inc(signal, 16)

            sp.wait_ge(rows_ready, 2)
            sp.wait_ge(q_ready, 2)
            spread(qs, qc, spread_q)
            sp.wait_ge(k_ready, 2)
            spread(ks, kc[0], spread_k)
            sp.dma_start(w3s[:, 0:PAIRS + 1, :, :], w3.rearrange("p (n m c) -> p n m c", m=3, c=P)).then_inc(ld_w, 16)
            sp.wait_ge(layer[0]["scoredT"], G * B)
            sp.wait_ge(k2_ready, 2)
            spread(ks, kc[1], spread_k)
            sp.wait_ge(layer[0]["qm_ready"], B)
            sp.wait_ge(q_ready, 4)
            spread(qs, qc, spread_q)
            for c in range(2):
                sp.wait_ge(out_copied, c + 1)
                sp.dma_start(outT[:, HALF * c:HALF * c + HALF], outs[:, c, :]).then_inc(stored, 16)
            sp.wait_ge(stored, 32)

        @block.tensor
        def _(pe):
            def half(t, c, shift=1):
                return t[:, 4 * c:4 * c + 4, shift:shift + P]

            def mm(out, lhsT, rhs, start=True, stop=True):
                return pe.matmul(out, lhsT, rhs, start=start, stop=stop)

            def turn_inputs(n, banks):
                for c in range(2):
                    for b in range(4 * c, 4 * c + 4):
                        pe.wait_ge(xn_ready, B * n + b + 1)
                        last = pe.transpose(banks[c][:, P * (b % 4):P * (b % 4) + P], xn[:, b, :], ident)
                    last.then_inc(xT_done, 1)

            pe.wait_ge(ld_a, 16)
            for n, (conv_w, proj, bias) in enumerate((("cq", "qp2T", "cqb"), ("ck", "kp2T", "ckb"))):
                for k in range(3):
                    c0 = cols_a[conv_w][0] + P * k
                    mm(bank[2 + n][:, P * k:P * k + P], pa[:, c0:c0 + P], A(proj))
                mm(bank[4][:, n:n + 1], A(proj), A(bias)).then_inc(folded, 1)
            turn_inputs(0, bank)
            pe.wait_ge(ld_ctx, 16)
            pe.wait_ge(ld_b, 16)
            pe.wait_ge(pads_ready, 6)
            for c in range(2):
                pe.wait_ge(xT_copied, c + 1)
                mm(bank[5 + c][:, :], A("wqT"), half(xnT, c)).then_inc(in_done, 1)
            for c in range(2):
                mm(bank[7 - 7 * c][:, :], A("wkT"), half(xnT, c)).then_inc(in_done, 1)
            for b in range(B):
                if b == 4:
                    pe.wait_ge(fold_copied, 4)
                last = mm(bank[1 + b // 4][:, P * (b % 4):P * (b % 4) + P], xnT[:, b, 1:1 + P], A("wvT"))
                if b % 4 == 3:
                    last.then_inc(v_done, 1)
            pe.wait_ge(in_copied, 2)
            for c in range(2):
                for k in range(3):
                    last = mm(bank[5 + c][:, :], foldq[:, k, :], half(qin, c, k), k == 0, k == 2)
                last.then_inc(q_done, 1)
            pe.wait_ge(in_copied, 4)
            for c in range(2):
                for k in range(3):
                    last = mm(bank[7 - 7 * c][:, :], foldk[:, k, :], half(kin, c, k), k == 0, k == 2)
                last.then_inc(k_done, 1)
            for c in range(2):
                pe.wait_ge(v_copied, c + 1)
                mm(bank[1 + c][:, :], Bw("wk"), ctxs[:, 4 * c:4 * c + 4, :]).then_inc(k2_done, 1)
            pe.wait_ge(fold_copied, 4)
            pe.wait_ge(gelu_done, 4)
            pe.wait_ge(const_ready, 1)
            for c in range(2):
                for r in range(2):
                    last = mm(bank[3 + c][:, :], tau2r[:, r, :, :], conv[:, r, 4 * c:4 * c + 4, :], r == 0, r == 1)
                last.then_inc(tau_done, 1)
            pe.wait_ge(k_ready, 1)
            d0 = cols_a["del2T"][0]
            for b in range(B):
                for r in range(2):
                    last = mm(bank[7][:, H * b:H * b + H], conv[:, 2 + r, b, :], pa[:, d0 + H * r:d0 + H * r + H],
                              r == 0, r == 1)
            last.then_inc(delta_done, 1)
            for b in range(B):
                if b % 4 == 0:
                    pe.wait_ge(k2_ready, b // 4 + 1)
                last = mm(bank[1 + b // 4][:, P * (b % 4):P * (b % 4) + P], ctxs[:, b, :], Bw("wv"))
                if b % 4 == 3:
                    last.then_inc(v_done, 1)

            def attention(n, w_out, masked_layer):
                s = layer[n]

                def scores(b, j):
                    i = J * b + j
                    if i >= 2:
                        pe.wait_ge(s["maxed"], i - 1)
                    out = bank[i % 2]
                    if masked_layer:
                        pe.matmul(out[:, :].rearrange("p (g k) -> p g k", g=G), identb[:, :],
                                  maskb[:, b, :].unsqueeze(1).broadcast_to([P, G, P]), start=True, stop=False,
                                  skip_group_check=True)
                    for g in range(G):
                        last = pe.matmul(out[:, P * g:P * g + P], qs[32 * j:32 * j + DK + 1, g, b, :],
                                         ks[32 * j:32 * j + DK + 1, g, b, :], start=not masked_layer, stop=True,
                                         skip_group_check=masked_layer)
                    last.then_inc(s["scored"], 1)

                def turn_max(b):
                    pe.wait_ge(s["maxed"], G * b + G)
                    if b >= 1:
                        pe.wait_ge(s["qm_ready"], b)
                    for g in range(G):
                        last = pe.transpose(bank[6][:, P * g:P * g + P], negmax[:, g, :], ident)
                    last.then_inc(s["max_turned"], 1)

                def scoresT(b, j):
                    i = J * b + j
                    if j == 0:
                        pe.wait_ge(s["qm_ready"], b + 1)
                    if i >= 3:
                        pe.wait_ge(s["exped"], i - 2)
                    out = bank[2 + i % 3]
                    if masked_layer:
                        pe.matmul(out[:, :].rearrange("p (g q) -> p g q", g=G), maskb[:, b, :],
                                  identb[:, :].unsqueeze(1).broadcast_to([P, G, P]), start=True, stop=False,
                                  skip_group_check=True)
                    for g in range(G):
                        last = pe.matmul(out[:, P * g:P * g + P], ks[32 * j:32 * j + DK + 1, g, b, :],
                                         qm[32 * j:32 * j + DK + 1, b % 2, g, :], start=not masked_layer, stop=True,
                                         skip_group_check=masked_layer)
                    last.then_inc(s["scoredT"], 1)

                def pv(b, j):
                    i = J * b + j
                    pe.wait_ge(s["exped"], i + 1)
                    if j == 0 and b >= 1:
                        pe.wait_ge(s["o_copied"], b)
                    for g in range(G):
                        last = mm(bank[5][32 * j:32 * j + DK + 1, P * g:P * g + P], vs[n][:, b, J * g + j, :],
                                  probs[:, i % 4, g, :])
                    last.then_inc(s["pv_done"], 1)

                def turn_out(b):
                    pe.wait_ge(s["o_copied"], b + 1)
                    if b >= 1:
                        pe.wait_ge(s["residual"], b)
                    for g in range(G):
                        last = pe.transpose(bank[7][:, P * g:P * g + P], oT[:, g, :], ident)
                    last.then_inc(s["o_turned"], 1)

                def turn_on(b):
                    pe.wait_ge(s["normed"], b + 1)
                    pe.transpose(bank[7][:, 0:P], on[:, :, :].rearrange("p h d -> p (h d)"), ident)\
                        .then_inc(s["on_turned"], 1)

                def project(b):
                    pe.wait_ge(s["on_copied"], b + 1)
                    mm(bank[7][:, P:2 * P], onT[:, :], w_out).then_inc(s["projected"], 1)

                pe.wait_ge(spread_q, 16 * H * (n + 1))
                pe.wait_ge(spread_k, 16 * H * (n + 1))
                for g in range(G):
                    scores(0, g)
                for b in range(B):
                    turn_max(b)
                    if b >= 1:
                        turn_out(b - 1)
                    scoresT(b, 0)
                    scoresT(b, 1)
                    if b >= 1:
                        turn_on(b - 1)
                    scoresT(b, 2)
                    if b >= 1:
                        project(b - 1)
                    for g in range(G):
                        if b + 1 < B:
                            scores(b + 1, g)
                        pv(b, g)
                        if g == 0:
                            scoresT(b, 3)
                turn_out(B - 1)
                turn_on(B - 1)
                project(B - 1)

            pe.wait_ge(v_copied, 4)
            pe.wait_ge(tau_ready, 2)
            pe.wait_ge(delta_sum, 1)
            pe.wait_ge(bank5_zeroed, 1)
            pe.wait_ge(values_scaled, 1)
            attention(0, A("woT"), False)
            pe.wait_ge(layer[0]["maxed"], G * B)
            turn_inputs(1, bank)
            for c in range(2):
                pe.wait_ge(xT_copied, 3 + c)
                if c == 0:
                    pe.wait_ge(layer[0]["exped"], G * B)
                mm(bank[2 + c][:, :], Bw("wq"), half(xnT, c)).then_inc(q_done, 1)
            pe.wait_ge(q_ready, 4)
            pe.wait_ge(mask_ready, 1)
            attention(1, Bw("wo"), True)
            pe.wait_ge(layer[1]["maxed"], G * B)
            turn_inputs(2, bank)

            pe.wait_ge(layer[1]["exped"], G * B)
            pe.wait_ge(layer[1]["residual"], B)
            pe.wait_ge(x3T_ready, 2)
            r0, r1 = cols_b["routerT"]
            for b in range(B):
                last = mm(bank[6][:, E * b:E * b + E], xnT[:, b, 1:1 + P], pb[:, r0:r1])
            last.then_inc(logits_done, 1)
            for b in range(B):
                pe.matmul(bank[b // 4][:, P * (b % 4):P * (b % 4) + P], xres[:, b, :], ident,
                          start=(b % 4 == 0), stop=False, skip_group_check=True)

            def gate_up(c, w, n, gate_before, up_before):
                for m, (out, signal, before, used) in enumerate((
                        (bank[2 + c], gate_done, gate_before, silu_done), (bank[4 + c], up_done, up_before, gu_done))):
                    if before is not None:
                        pe.wait_ge(used, before)
                    xh, xl = xhl[:, 0, HALF * c:HALF * c + HALF], xhl[:, 1, HALF * c:HALF * c + HALF]
                    mm(out[:, :], whigu[:, w, m, :], xh, True, False)
                    mm(out[:, :], whigu[:, w, m, :], xl, False, False)
                    mm(out[:, :], wlogu[:, w, m, :], xh, False, True).then_inc(signal, 1)

            def down(c, w, n, pairs, stop):
                if c == 0:
                    pe.wait_ge(wlod_ready, pairs)
                pe.wait_ge(hlo_ready, n)
                acc = bank[c][:, :]
                pe.matmul(acc, whid[:, w, :], hhi[:, c, :], start=False, stop=False, skip_group_check=True)
                pe.matmul(acc, whid[:, w, :], hlo[:, c, :], start=False, stop=False, skip_group_check=True)
                pe.matmul(acc, wlod[:, w, :], hhi[:, c, :], start=False, stop=stop,
                          skip_group_check=True).then_inc(down_done, 1)

            pe.wait_ge(xhi_ready, 2)
            pe.wait_ge(xlo_ready, 2)
            pe.wait_ge(wlogu_ready, 1)
            for c in range(2):
                gate_up(c, 0, c + 1, None, None)
            pe.wait_ge(coef_ready, 1)
            for b in range(B):
                last = pe.transpose(bank[7][:, :].bitcast(F16)[:, P * b:P * b + P],
                                    chl[:, b, :, :].rearrange("p a e -> p (a e)"), identh[:, :])
            last.then_inc(coefT_done, 1)
            pe.wait_ge(coefT_ready, 1)
            pe.wait_ge(sel_ready, 1)
            with pe.Fori(0, PAIRS // 2) as it:
                for k in range(4):
                    c, w = k % 2, (1 + k // 2) % 2
                    if c == 0:
                        pe.wait_ge(wlogu_ready, 2 * it + (2 + k // 2))
                    gate_up(c, w, None, 4 * it + (k + 1), 4 * it + (k + 1))
                    pe.wait_ge(h_done, 4 * it + (k + 1))
                    pe.matmul(bank[6 + c][:, :],
                              sel[:, bass.ds(4 * it + 2 * (k // 2), 2), :].rearrange("p e i -> p (e i)"),
                              cT[:, HALF * c:HALF * c + HALF], start=True, stop=True).then_inc(coefb_done, 1)
                    down(c, 1 - w, 4 * it + (k + 1), 2 * it + (1 + k // 2), False)
            for c in range(2):
                down(c, PAIRS % 2, 2 * PAIRS + c + 1, PAIRS + 1, True)

        @block.scalar
        def _(act):
            def copy_inputs(n):
                for c in range(2):
                    act.wait_ge(xT_done, 2 * n + c + 1)
                    act.activation(xnT[:, 4 * c:4 * c + 4, 1:1 + P],
                                   bank[c][:, :].rearrange("p (b t) -> p b t", b=4), ACT.Copy).then_inc(xT_copied, 1)

            act.wait_ge(pads_ready, 6)
            copy_inputs(0)
            act.wait_ge(ld_a, 16)
            for n, (dst, bias, banks) in enumerate(((qin, "bq", (5, 6)), (kin, "bk", (7, 0)))):
                for c in range(2):
                    act.wait_ge(in_done, 2 * n + c + 1)
                    act.activation(dst[:, 4 * c:4 * c + 4, 1:1 + P],
                                   bank[banks[c]][:, :].rearrange("p (b t) -> p b t", b=4), ACT.Identity,
                                   bias=A(bias)).then_inc(in_copied, 1)
            act.wait_ge(xT_copied, 2)
            for n, (w, bias) in enumerate((("tau1", "tau1b"), ("del1", "del1b"))):
                for r in range(2):
                    w0, b0 = cols_a[w][0] + 3 * r, cols_a[bias][0] + r
                    act.activation(conv[:, 2 * n + r, :, :], xnT[:, :, 0:P], ACT.Identity,
                                   bias=pa[:, b0:b0 + 1], scale=pa[:, w0:w0 + 1]).then_inc(conv_part, 1)
            for n in range(4):
                act.wait_ge(conv_done, n + 1)
                act.activation(conv[:, n, :, :], conv[:, n, :, :], ACT.Gelu).then_inc(gelu_done, 1)
            act.wait_ge(fold_copied, 4)
            for c in range(2):
                act.wait_ge(k_done, c + 1)
                act.activation(kc[0][:, 4 * c:4 * c + 4, :],
                               bank[7 - 7 * c][:, :].rearrange("p (b t) -> p b t", b=4), ACT.Identity,
                               bias=foldb[:, 1:2]).then_inc(k_ready, 1)
            act.wait_ge(ld_b, 16)
            for c in range(2):
                act.wait_ge(k2_done, c + 1)
                act.activation(kc[1][:, 4 * c:4 * c + 4, :],
                               bank[1 + c][:, :].rearrange("p (b t) -> p b t", b=4), ACT.Identity,
                               bias=Bw("bk")).then_inc(k2_ready, 1)
            for c in range(2):
                act.wait_ge(tau_done, c + 1)
                act.activation(tauT[:, 4 * c:4 * c + 4, :], bank[3 + c][:, :].rearrange("p (b t) -> p b t", b=4),
                               ACT.Sigmoid, bias=A("tau2b")).then_inc(tau_ready, 1)
            act.wait_ge(delta_sum, 1)
            act.activation(edelta[:, :, :], edelta[:, :, :], ACT.Sigmoid).then_inc(delta_ready, 1)
            act.wait_ge(delta_ready, 1)
            act.activation(edelta[:, :, :], edelta[:, :, :], ACT.Exp).then_inc(delta_ready, 1)

            def attention(n):
                s = layer[n]

                def copy_o(b):
                    act.wait_ge(s["pv_done"], G * b + G)
                    if b >= 1:
                        act.wait_ge(s["o_turned"], b)
                    act.activation(oT[:, :, :].rearrange("p g t -> p (g t)"), bank[5][:, :], ACT.Copy)\
                        .then_inc(s["o_copied"], 1)

                def copy_on(b):
                    act.wait_ge(s["on_turned"], b + 1)
                    if b >= 1:
                        act.wait_ge(s["projected"], b)
                    act.activation(onT[:, :], bank[7][:, 0:P], ACT.Copy).then_inc(s["on_copied"], 1)

                def exponential(b, g):
                    i = G * b + g
                    act.wait_ge(s["scoredT"], i + 1)
                    if i >= 4:
                        act.wait_ge(s["pv_done"], i - 3)
                    act.activation(probs[:, i % 4, :, :].rearrange("p j t -> p (j t)"), bank[2 + i % 3][:, :],
                                   ACT.Exp, scale=SCALE).then_inc(s["exped"], 1)

                for b in range(B):
                    if b >= 1:
                        copy_o(b - 1)
                    exponential(b, 0)
                    exponential(b, 1)
                    if b >= 1:
                        copy_on(b - 1)
                    exponential(b, 2)
                    exponential(b, 3)
                copy_o(B - 1)
                copy_on(B - 1)

            attention(0)
            copy_inputs(1)
            for c in range(2):
                act.wait_ge(q_done, 3 + c)
                if c == 0:
                    act.wait_ge(spread_q, 16 * H)
                act.activation(qc[:, 4 * c:4 * c + 4, :], bank[2 + c][:, :].rearrange("p (b t) -> p b t", b=4),
                               ACT.Identity, bias=Bw("bq")).then_inc(q_ready, 1)
            attention(1)
            for c in range(2):
                act.wait_ge(xT_done, 4 + c + 1)
                src = bank[c][:, :].rearrange("p (b t) -> p b t", b=4)
                act.activation(xnT[:, 4 * c:4 * c + 4, 1:1 + P], src, ACT.Copy).then_inc(x3T_ready, 1)
                act.wait_ge(x3T_ready, c + 1)
                act.activation(xhl[:, 0, HALF * c:HALF * c + HALF].rearrange("p (b t) -> p b t", b=4),
                               xnT[:, 4 * c:4 * c + 4, 1:1 + P], ACT.Copy).then_inc(xhi_ready, 1)
            act.wait_ge(logits_done, 1)
            act.activation(sc[:, :, :].rearrange("p b e -> p (b e)"), bank[6][:, :], ACT.Sigmoid)\
                .then_inc(scores_ready, 1)

            def silu(c, gates, gu_used):
                act.wait_ge(gate_done, gates)
                if gu_used is not None:
                    act.wait_ge(gu_done, gu_used)
                act.activation(sg[:, c, :], bank[2 + c][:, :], ACT.Silu).then_inc(silu_done, 1)

            def high_part(c, hs, downs):
                act.wait_ge(h_done, hs)
                if downs is not None:
                    act.wait_ge(down_done, downs)
                act.activation(hhi[:, c, :], hx[:, c, :], ACT.Copy).then_inc(hhi_ready, 1)

            silu(0, 1, None)
            silu(1, 2, None)
            high_part(0, 1, None)
            high_part(1, 2, None)
            with act.Fori(0, PAIRS // 2) as it:
                for k in range(4):
                    silu(k % 2, 4 * it + (k + 3), 4 * it + (k + 1))
                    high_part(k % 2, 4 * it + (k + 3), 4 * it + (k + 1))
            for c in range(2):
                act.wait_ge(down_done, 2 * PAIRS + 1 + c)
                act.activation(outs[:, c, :], bank[c][:, :], ACT.Copy).then_inc(out_copied, 1)

        @block.vector
        def _(dve):
            steps = [0]

            def link(ins):
                ins.then_inc(dve_step, 1)
                steps[0] += 1
                dve.wait_ge(dve_step, steps[0])

            def stats_of(b):
                dve.bn_stats(stats[:, b, :], xres[:, b, :]).then_inc(dve_step, 1)
                steps[0] += 1
                dve.wait_ge(dve_step, steps[0])
                link(dve.bn_aggr(mv[:, b, :], stats[:, b, :]))

            def normalise(n):
                v, y, a, c2, raw = (nwt[:, i, :] for i in range(5))
                link(dve.tensor_scalar(v, mv[:, :, 1], EPS, None, ALU.add))
                link(dve.tensor_scalar(raw.bitcast(I32), v.bitcast(I32), 1, None, ALU.logical_shift_right))
                link(dve.tensor_scalar(y.bitcast(I32), raw.bitcast(I32), -1.0, RSQRT_MAGIC, ALU.mult, ALU.add))
                for _ in range(4):
                    link(dve.tensor_tensor(a, v, y, ALU.mult))
                    link(dve.tensor_tensor(c2, a, y, ALU.mult))
                    link(dve.tensor_scalar(c2, c2, -0.5, 1.5, ALU.mult, ALU.add))
                    link(dve.tensor_tensor(y, y, c2, ALU.mult))
                if n >= 1:
                    dve.wait_ge(xT_done, 2 * n)
                for b in range(B):
                    dve.tensor_scalar(xn[:, b, :], xres[:, b, :], mv[:, b, 0:1], y[:, b:b + 1],
                                      ALU.subtract, ALU.mult).then_inc(xn_ready, 1)

            dve.wait_ge(ld_x, 16)
            for b in range(B):
                stats_of(b)
            normalise(0)
            dve.wait_ge(ld_a, 16)
            link(dve.tensor_copy(identb[:, :], ident))
            link(dve.tensor_copy(identh[:, :], ident))
            t0 = cols_a["tau2T"][0]
            dve.tensor_copy(tau2r[:, :, :, :].rearrange("p r h d -> p (r h) d"),
                            pa[:, t0:t0 + 2 * H].unsqueeze(2).broadcast_to([P, 2 * H, DK])).then_inc(const_ready, 1)
            for n, (dst, proj) in enumerate(((foldq, "qp1T"), (foldk, "kp1T"))):
                dve.wait_ge(folded, n + 1)
                link(dve.tensor_copy(dst[:, :, :].rearrange("p k o -> p (k o)"), bank[2 + n][:, 0:3 * P]))
                dve.tensor_tensor(dst[:, 1, :], dst[:, 1, :], A(proj), ALU.add).then_inc(fold_copied, 1)
            for n, bias in enumerate(("qpb", "kpb")):
                dve.tensor_tensor(foldb[:, n:n + 1], bank[4][:, n:n + 1], A(bias), ALU.add).then_inc(fold_copied, 1)
            dve.wait_ge(xT_copied, 2)
            for n, w in enumerate(("tau1", "del1")):
                for r in range(2):
                    w0 = cols_a[w][0] + 3 * r
                    dve.wait_ge(conv_part, 2 * n + r + 1)
                    y = conv[:, 2 * n + r, :, :]
                    link(dve.scalar_tensor_tensor(out=y, in0=xnT[:, :, 1:1 + P], scalar=pa[:, w0 + 1:w0 + 2],
                                                  in1=y, op0=ALU.mult, op1=ALU.add))
                    dve.scalar_tensor_tensor(out=y, in0=xnT[:, :, 2:2 + P], scalar=pa[:, w0 + 2:w0 + 3],
                                             in1=y, op0=ALU.mult, op1=ALU.add).then_inc(conv_done, 1)

            def values(n, bias, base):
                for c in range(2):
                    dve.wait_ge(v_done, base + c + 1)
                    for b in range(4 * c, 4 * c + 4):
                        last = dve.tensor_tensor(
                            vs[n][:, b, :, 0:DK],
                            bank[1 + c][:, P * (b % 4):P * (b % 4) + P].rearrange("p (h d) -> p h d", h=H),
                            bias.rearrange("p (h d) -> p h d", h=H), ALU.add)
                    last.then_inc(v_copied, 1)

            values(0, A("bv"), 0)
            dve.wait_ge(fold_copied, 3)
            for c in range(2):
                dve.wait_ge(q_done, c + 1)
                dve.wait_ge(tau_ready, c + 1)
                dve.scalar_tensor_tensor(out=qc[:, 4 * c:4 * c + 4, :].rearrange("p b t -> p (b t)"),
                                         in0=bank[5 + c][:, :], scalar=foldb[:, 0:1],
                                         in1=tauT[:, 4 * c:4 * c + 4, :].rearrange("p b t -> p (b t)"),
                                         op0=ALU.add, op1=ALU.mult).then_inc(q_ready, 1)
            dve.wait_ge(delta_done, 1)
            dve.tensor_tensor(edelta[:, :, :], bank[7][:, 0:B * H].rearrange("p (b h) -> p b h", b=B),
                              A("del2b").unsqueeze(1).broadcast_to([P, B, H]), ALU.add).then_inc(delta_sum, 1)
            dve.wait_ge(ld_b, 16)
            values(1, Bw("bv"), 2)
            dve.wait_ge(ones_ready, 5)
            dve.wait_ge(delta_ready, 2)
            dve.wait_ge(v_copied, 2)
            v0 = vs[0][:, :, :, :].rearrange("p b h d -> p (b h) d")
            dve.tensor_tensor(v0, v0, edelta[:, :, :].rearrange("p b h -> p (b h)").unsqueeze(2)
                              .broadcast_to([P, B * H, DK + 1]), ALU.mult).then_inc(values_scaled, 1)
            dve.memset(bank[5][:, :], 0.0).then_inc(bank5_zeroed, 1)

            def attention(n, bias):
                s = layer[n]

                def maximum(b, j):
                    i = J * b + j
                    dve.wait_ge(s["scored"], i + 1)
                    if j == 0 and b >= 1:
                        dve.wait_ge(s["max_turned"], b)
                    dve.tensor_reduce(negmax[:, :, 32 * j:32 * j + 1],
                                      bank[i % 2][:, :].rearrange("p (g k) -> p g k", g=G), AX.X, ALU.max,
                                      negate=True).then_inc(s["maxed"], 1)

                def queries_with_max(b):
                    dve.wait_ge(s["max_turned"], b + 1)
                    if b >= 2:
                        dve.wait_ge(s["scoredT"], G * (b - 1))
                    dve.tensor_tensor(qm[:, b % 2, :, :], bank[6][:, :].rearrange("p (g t) -> p g t", g=G),
                                      qs[:, :, b, :], ALU.add).then_inc(s["qm_ready"], 1)

                def norm(b):
                    dve.wait_ge(s["o_turned"], b + 1)
                    o = bank[7][:, :].rearrange("p (h c) -> p h c", h=H)
                    link(dve.reciprocal(rec[:, :].unsqueeze(2), o[:, :, DK:DK + 1]))
                    if b >= 1:
                        dve.wait_ge(s["on_turned"], b)
                    dve.tensor_tensor(on[:, :, :], o[:, :, 0:DK], rec[:, :].unsqueeze(2).broadcast_to([P, H, DK]),
                                      ALU.mult).then_inc(s["normed"], 1)

                def residual(b):
                    dve.wait_ge(s["projected"], b + 1)
                    dve.tensor_tensor(xres[:, b, :], xres[:, b, :], bank[7][:, P:2 * P], ALU.add)\
                        .then_inc(s["residual"], 1)
                    dve.wait_ge(s["residual"], b + 1)
                    stats_of(b)

                link(dve.tensor_tensor(xres[:, :, :], xres[:, :, :], bias.unsqueeze(1).broadcast_to([P, B, P]),
                                       ALU.add))
                for g in range(G):
                    maximum(0, g)
                for b in range(B):
                    queries_with_max(b)
                    if b >= 1:
                        norm(b - 1)
                        residual(b - 1)
                    if b + 1 < B:
                        for g in range(G):
                            maximum(b + 1, g)
                norm(B - 1)
                residual(B - 1)

            dve.wait_ge(spread_q, 16 * H)
            attention(0, A("bo"))
            normalise(1)
            dve.wait_ge(ld_mask, 16)
            dve.tensor_scalar(maskb[:, :, :], masku[:, :, :], MASKED, None, ALU.mult).then_inc(mask_ready, 1)
            dve.wait_ge(spread_q, 32 * H)
            attention(1, Bw("bo"))
            normalise(2)
            for c in range(2):
                dve.wait_ge(xhi_ready, c + 1)
                dve.tensor_tensor(xhl[:, 1, HALF * c:HALF * c + HALF].rearrange("p (b t) -> p b t", b=4),
                                  xnT[:, 4 * c:4 * c + 4, 1:1 + P],
                                  xhl[:, 0, HALF * c:HALF * c + HALF].bitcast(F32).rearrange("p (b t) -> p b t", b=4),
                                  ALU.subtract).then_inc(xlo_ready, 1)

            def high_gu(w, at):
                dve.tensor_copy(whigu[:, w, :, :], w3s[:, at, 0:2, :]).then_inc(whigu_ready, 1)

            dve.wait_ge(ld_w, 16)
            dve.wait_ge(ones_ready, 5)
            high_gu(0, 0)
            dve.tensor_copy(whid[:, 0, :], w3s[:, 0, 2, :]).then_inc(whid_ready, 1)
            high_gu(1, 1)

            dve.wait_ge(scores_ready, 1)
            link(dve.tensor_tensor(sfc[:, :, :, :].rearrange("p b g e -> p b (g e)"), sc[:, :, :],
                                   Bw("e_bias").unsqueeze(1).broadcast_to([P, B, E]), ALU.add))
            NG = B * GE

            def buf(i, n):
                return tmp[:, i, 0:n]
            s8 = sfc[:, :, :, :].rearrange("p b g e -> p (b g) e")
            a4 = buf(0, NG * 4).rearrange("p (n e) -> p n e", e=4)
            b4 = buf(1, NG * 4).rearrange("p (n e) -> p n e", e=4)
            link(dve.tensor_tensor(a4, s8[:, :, 0:4], s8[:, :, 4:8], ALU.max))
            link(dve.tensor_tensor(b4, s8[:, :, 0:4], s8[:, :, 4:8], ALU.min))
            hi, lo = a4, b4
            at = 2
            for width in (2, 1):
                nh, t1, t2, nl = (buf(at + i, NG * width).rearrange("p (n e) -> p n e", e=width) for i in range(4))
                at += 4
                link(dve.tensor_tensor(nh, hi[:, :, 0:width], hi[:, :, width:2 * width], ALU.max))
                link(dve.tensor_tensor(t1, hi[:, :, 0:width], hi[:, :, width:2 * width], ALU.min))
                link(dve.tensor_tensor(t2, lo[:, :, 0:width], lo[:, :, width:2 * width], ALU.max))
                link(dve.tensor_tensor(nl, t1, t2, ALU.max))
                hi, lo = nh, nl
            gs = buf(10, NG).rearrange("p (b g) -> p b g", g=GE)
            link(dve.tensor_tensor(gs, hi[:, :, 0].rearrange("p (b g) -> p b g", g=GE),
                                   lo[:, :, 0].rearrange("p (b g) -> p b g", g=GE), ALU.add))
            flat = lambda i: gcmp[:, i, :, :, :].rearrange("p b g f -> p (b g) f")
            for b in range(B):
                other = gs[:, b, :].unsqueeze(1).broadcast_to([P, GE, GE])
                own = gs[:, b, :].unsqueeze(2).broadcast_to([P, GE, GE])
                link(dve.tensor_tensor(gcmp[:, 0, b, :, :], other, own, ALU.is_gt))
                link(dve.tensor_tensor(gcmp[:, 1, b, :, :], other, own, ALU.is_equal))
            dve.wait_ge(ones_ready, 4 + GE)
            lowb = low[:, :, :].rearrange("p g f -> p (g f)").unsqueeze(1).broadcast_to([P, B, GE * GE])
            f2 = lambda i: gcmp[:, i, :, :, :].rearrange("p b g f -> p b (g f)")
            link(dve.tensor_tensor(f2(2), f2(1), lowb, ALU.mult))
            link(dve.tensor_tensor(f2(0), f2(0), f2(2), ALU.add))
            rank = buf(11, NG)
            link(dve.tensor_reduce(rank, flat(0), AX.X, ALU.add))
            chosen = buf(2, NG)
            link(dve.tensor_scalar(chosen, rank, TOP_GROUPS - 0.5, None, ALU.is_lt))
            m3 = masked[:, :, :].rearrange("p b (g e) -> p (b g) e", g=GE)
            link(dve.tensor_tensor(m3, s8, chosen.unsqueeze(2).broadcast_to([P, NG, E // GE]), ALU.mult))
            for b in range(B):
                link(dve.max(top8[:, b, :], masked[:, b, :]))
                link(dve.match_replace(replaced[:, b, :], top8[:, b, :], masked[:, b, :], -3e38))
            link(dve.tensor_tensor(coef[:, :, :], replaced[:, :, :], masked[:, :, :], ALU.not_equal))
            link(dve.tensor_tensor(coef[:, :, :], coef[:, :, :], sc[:, :, :], ALU.mult))
            wsum = buf(3, B)
            link(dve.tensor_reduce(wsum, coef[:, :, :], AX.X, ALU.add))
            link(dve.tensor_scalar(wsum, wsum, 1e-20, None, ALU.add))
            link(dve.reciprocal(wsum, wsum))
            link(dve.tensor_scalar(wsum, wsum, ROUTE_SCALE, None, ALU.mult))
            link(dve.tensor_tensor(coef[:, :, :], coef[:, :, :], wsum.unsqueeze(2).broadcast_to([P, B, E]), ALU.mult))
            link(dve.tensor_copy(chl[:, :, 0, :], coef[:, :, :]))
            dve.tensor_tensor(chl[:, :, 1, :], coef[:, :, :], chl[:, :, 0, :], ALU.subtract).then_inc(coef_ready, 1)
            dve.wait_ge(coefT_done, 1)
            dve.tensor_copy(cT[:, :], bank[7][:, :].bitcast(F16)).then_inc(coefT_ready, 1)

            for c in range(2):
                dve.wait_ge(silu_done, c + 1)
                dve.wait_ge(up_done, c + 1)
                dve.tensor_tensor(gu[:, c, :], sg[:, c, :], bank[4 + c][:, :], ALU.mult).then_inc(gu_done, 1)
                dve.wait_ge(gu_done, c + 1)
                dve.tensor_copy(hx[:, c, :], gu[:, c, :]).then_inc(h_done, 1)
            with dve.Fori(0, PAIRS // 2) as it:
                for k in range(4):
                    c, kk = k % 2, k // 2
                    dve.wait_ge(silu_done, 4 * it + (k + 3))
                    dve.wait_ge(up_done, 4 * it + (k + 3))
                    dve.wait_ge(hlo_ready, 4 * it + (k + 1))
                    dve.tensor_tensor(gu[:, c, :], sg[:, c, :], bank[4 + c][:, :], ALU.mult).then_inc(gu_done, 1)
                    if c == 0:
                        dve.tensor_copy(whigu[:, kk, :, :].rearrange("p m c -> p (m c)"),
                                        w3s[:, bass.ds(2 * it + (kk + 2), 1), 0:2, :]
                                        .rearrange("p o m c -> p (o m c)")).then_inc(whigu_ready, 1)
                    else:
                        dve.wait_ge(down_done, 4 * it + (2 * kk + 1))
                        dve.tensor_copy(whid[:, 1 - kk, :], w3s[:, bass.ds(2 * it + (kk + 1), 1), 2, :]
                                        .rearrange("p o c -> p (o c)")).then_inc(whid_ready, 1)
                    dve.wait_ge(gu_done, 4 * it + (k + 3))
                    dve.wait_ge(coefb_done, 4 * it + (k + 1))
                    dve.tensor_tensor(hx[:, c, :], gu[:, c, :], bank[6 + c][:, :], ALU.mult).then_inc(h_done, 1)

        @block.gpsimd
        def _(pool):
            for t in (xnT, qin, kin):
                pool.memset(t[:, :, 0:1], 0.0).then_inc(pads_ready, 1)
                pool.memset(t[:, :, P + 1:P + 2], 0.0).then_inc(pads_ready, 1)
            pool.memset(qs[:, :, :, :], 0.0).then_inc(rows_ready, 1)
            pool.memset(ks[:, :, :, :], 1.0).then_inc(rows_ready, 1)
            for v in vs:
                pool.memset(v[:, :, :, DK:DK + 1], 1.0).then_inc(ones_ready, 1)
            pool.memset(negmax[:, :, :], 0.0).then_inc(ones_ready, 1)
            pool.memset(w3s[:, PAIRS + 1, :, :], 0.0).then_inc(ones_ready, 1)
            pool.memset(low[:, :, :], 0.0).then_inc(ones_ready, 1)
            pool.wait_ge(ones_ready, 5)
            for g in range(1, GE):
                pool.memset(low[:, g, 0:g], 1.0).then_inc(ones_ready, 1)
            pool.wait_ge(ld_a, 16)
            pool.tensor_tensor(i2[:, :], ident[:, 0:E], ident[:, E:2 * E], ALU.add).then_inc(pool_step, 1)
            pool.wait_ge(pool_step, 1)
            pool.tensor_copy(sel[:, :, :], i2[:, :].unsqueeze(2).broadcast_to([P, E, I])).then_inc(sel_ready, 1)

            def low_part(c, n):
                pool.wait_ge(hhi_ready, n)
                pool.tensor_tensor(hlo[:, c, :], hx[:, c, :], hhi[:, c, :].bitcast(F32), ALU.subtract)\
                    .then_inc(hlo_ready, 1)

            def low_gu(w, at, n):
                pool.wait_ge(whigu_ready, n)
                pool.tensor_tensor(wlogu[:, w, :, :], w3s[:, at, 0:2, :], whigu[:, w, :, :].bitcast(F32),
                                   ALU.subtract).then_inc(wlogu_ready, 1)

            def low_d(w, at, n):
                pool.wait_ge(whid_ready, n)
                pool.tensor_tensor(wlod[:, w, :], w3s[:, at, 2, :], whid[:, w, :].bitcast(F32),
                                   ALU.subtract).then_inc(wlod_ready, 1)

            low_gu(0, 0, 1)
            low_d(0, 0, 1)
            low_gu(1, 1, 2)
            low_part(0, 1)
            low_part(1, 2)
            with pool.Fori(0, PAIRS // 2) as it:
                for kk in range(2):
                    low_part(0, 4 * it + (2 * kk + 3))
                    pool.wait_ge(whigu_ready, 2 * it + (kk + 3))
                    pool.tensor_tensor(wlogu[:, kk, :, :].rearrange("p m c -> p (m c)"),
                                       w3s[:, bass.ds(2 * it + (kk + 2), 1), 0:2, :].rearrange("p o m c -> p (o m c)"),
                                       whigu[:, kk, :, :].rearrange("p m c -> p (m c)").bitcast(F32),
                                       ALU.subtract).then_inc(wlogu_ready, 1)
                    low_part(1, 4 * it + (2 * kk + 4))
                    pool.wait_ge(whid_ready, 2 * it + (kk + 2))
                    pool.tensor_tensor(wlod[:, 1 - kk, :],
                                       w3s[:, bass.ds(2 * it + (kk + 1), 1), 2, :].rearrange("p o c -> p (o c)"),
                                       whid[:, 1 - kk, :].bitcast(F32), ALU.subtract).then_inc(wlod_ready, 1)


def kernel(**inputs):
    import numpy as np
    import concourse.bacc as bacc
    from concourse.bass_utils import run_bass_kernel_spmd

    a = {k: np.asarray(v) for k, v in inputs.items()}
    att = lambda n: a["L0_attn_" + n]
    xat = lambda n: a["L0_xattn_" + n]
    ffn = lambda n: a["L0_ffn_" + n]
    col = lambda v: v.reshape(P, 1)
    row = lambda v: np.broadcast_to(v.reshape(1, -1), (P, v.size))
    taps = lambda w: w.transpose(0, 2, 1).reshape(P, 3 * P)
    second = lambda w: w.reshape(H, P, 2).transpose(1, 2, 0).reshape(P, 2 * H)
    part_a = dict(
        ident=np.eye(P, dtype=np.float32), wqT=att("Wq_w").T, wkT=att("Wk_w").T, wvT=att("Wv_w").T,
        cq=taps(att("convq_w")), ck=taps(att("convk_w")),
        qp1T=att("qproj_w")[:, :P].T, qp2T=att("qproj_w")[:, P:].T,
        kp1T=att("kproj_w")[:, :P].T, kp2T=att("kproj_w")[:, P:].T,
        tau1=att("tau1_w").reshape(P, 6), tau1b=att("tau1_b").reshape(P, 2),
        del1=att("del1_w").reshape(P, 6), del1b=att("del1_b").reshape(P, 2),
        tau2T=second(att("tau2_w")), del2T=second(att("del2_w")),
        bq=col(att("Wq_b")), bk=col(att("Wk_b")), cqb=col(att("convq_b")), ckb=col(att("convk_b")),
        qpb=col(att("qproj_b")), kpb=col(att("kproj_b")),
        tau2b=col(np.broadcast_to(att("tau2_b").reshape(H, 1), (H, DK))),
        woT=att("out_w").T, bv=row(att("Wv_b")), bo=row(att("out_b")), del2b=row(att("del2_b")))
    part_b = dict(wq=xat("Wq"), wk=xat("Wk"), wv=xat("Wv"), wo=xat("Wo"), bq=col(xat("bq")), bk=col(xat("bk")),
                  bv=row(xat("bv")), bo=row(xat("bo")), routerT=ffn("router_w").T, e_bias=row(ffn("e_bias")))
    gate = np.concatenate([ffn("SWg").reshape(P, 1, P), ffn("Wg").transpose(1, 0, 2).reshape(P, PAIRS, P)], 1)
    up = np.concatenate([ffn("SWu").reshape(P, 1, P), ffn("Wu").transpose(1, 0, 2).reshape(P, PAIRS, P)], 1)
    down = np.concatenate([ffn("SWd").reshape(P, 1, P), ffn("Wd").reshape(PAIRS, P, P).transpose(1, 0, 2)], 1)
    arrays = {
        "x": a["x"].reshape(T, P),
        "ctxT": a["ctx_1024"].reshape(T, P).T,
        "mask": a["mask_Bx1xSxS2_bk1"].reshape(B, P, P),
        "pack_a": np.concatenate([part_a[n] for n in PACK_A], axis=1),
        "pack_b": np.concatenate([part_b[n] for n in PACK_B], axis=1),
        "w3": np.stack([gate, up, down], axis=2).reshape(P, (PAIRS + 1) * 3 * P),
    }
    arrays = {k: np.ascontiguousarray(v) for k, v in arrays.items()}
    nc = bacc.Bacc("TRN2", target_bir_lowering=False, num_devices=1)
    args = [nc.dram_tensor(k, v.shape, mybir.dt.from_np(v.dtype), kind="ExternalInput").ap() for k, v in arrays.items()]
    outT = nc.dram_tensor("outT", (P, T), F32, kind="ExternalOutput").ap()
    decoder_layer(nc, *args, outT)
    r = run_bass_kernel_spmd(nc, [arrays], core_ids=[0])
    return np.ascontiguousarray(np.asarray(r.results[0]["outT"]).T).reshape(B, P, P)
```

```python
from contextlib import ExitStack

import concourse.bass as bass
from concourse import mybir

F32 = mybir.dt.float32
F32R = mybir.dt.float32r
F16 = mybir.dt.float16
BF16 = mybir.dt.bfloat16
I32 = mybir.dt.int32
U8 = mybir.dt.uint8
ALU = mybir.AluOpType
ACT = mybir.ActivationFunctionType
AX = mybir.AxisListType

P = 128
B = 8
T = B * P
H, DK = 16, 8
G = 4
J = H // G
HALF = T // 2
E, I = 64, 64
PAIRS = E * I // P
GE = 8
TOP_GROUPS, TOP_K = 4, 8
ROUTE_SCALE = 2.5
EPS = 1e-5
STEPS = 2 * B
S_HI, S_MID, S_LO = 2, 2 + DK, 2 + 2 * DK
UNITS = 2 * (PAIRS + 1)
LAG = 3
RING = 4
PEELED = 4
BODY = 8
TRIPS = 7
SCALE = DK ** -0.5
MASKED = -1e15 / SCALE
RSQRT_MAGIC = 1597463007.0

PACK_A = dict(ident=P, ones_rows=1, wqT=P, wkT=P, wvT=P, cq=3 * P, ck=3 * P, qp1T=P, qp2T=P, kp1T=P, kp2T=P,
              tau1=6, tau1b=2, del1=6, del1b=2, tau2T=32, del2T=32,
              bq=1, bk=1, cqb=1, ckb=1, qpb=1, kpb=1, tau2b=1, woT=P, bv=P, bo=P, del2b=H)
PACK_B = dict(wq=P, wk=P, wv=P, wo=P, bq=1, bk=1, bv=P, bo=P, routerT=E, e_bias=E)


def columns(pack):
    at, out = 0, {}
    for name, n in pack.items():
        out[name] = (at, at + n)
        at += n
    return out, at


def decoder_layer(nc, x, ctxT, mask, pack_a, pack_b, w3, outT):
    cols_a, n_a = columns(PACK_A)
    cols_b, n_b = columns(PACK_B)

    with ExitStack() as ctx:
        def sb(name, shape, dt=F32):
            return ctx.enter_context(nc.sbuf_tensor(name, shape, dt))

        def sem(name):
            return ctx.enter_context(nc.semaphore(name))

        bank = [ctx.enter_context(nc.psum_tensor(f"bank{i}", [P, 512], F32)) for i in range(8)]

        pa = sb("pa", [P, n_a])
        pb = sb("pb", [P, n_b])
        A = lambda name: pa[:, cols_a[name][0]:cols_a[name][1]]
        Bw = lambda name: pb[:, cols_b[name][0]:cols_b[name][1]]
        ident = A("ident")
        ring = sb("ring", [P, RING, 3, P])
        xres = sb("xres", [P, B, P])
        xn = sb("xn", [P, B, P])
        xnT = sb("xnT", [P, B, P + 2])
        qin = sb("qin", [P, B, P + 2])
        kin = sb("kin", [P, B, P + 2])
        ctxs = sb("ctxs", [P, B, P])
        masku = sb("masku", [P, B, P], U8)
        maskb = sb("maskb", [P, B, P], BF16)
        identb = sb("identb", [P, P], BF16)
        stats = sb("stats", [P, B, 6])
        mv = sb("mv", [P, B, 2])
        nwt = sb("nwt", [P, 5, B])
        foldq = sb("foldq", [P, 3, P])
        foldk = sb("foldk", [P, 3, P])
        foldb = sb("foldb", [P, 2])
        conv = sb("conv", [P, 4, B, P])
        probs = conv[:, :, :, :].rearrange("p a b t -> p (a b t)").rearrange("p (i j t) -> p i j t", i=8, j=J)
        tau2r = sb("tau2r", [P, 2, H, DK])
        edelta = sb("edelta", [P, B, H])
        qc = sb("qc", [P, B, P])
        kc = [qin[:, :, 1:1 + P], kin[:, :, 1:1 + P]]
        tauT = sb("tauT", [P, B, P])
        qhl = sb("qhl", [P, 2, B, P], F32R)
        khl = [sb(f"khl{n}", [P, 2, B, P], F32R) for n in range(2)]
        pick = sb("pick", [P, 4, G, P], F32R)
        qst = sb("qst", [P, G, B, P], F32R)
        kst = [sb(f"kst{n}", [P, G, B, P], F32R) for n in range(2)]
        kbd = sb("kbd", [P, 2, G, J, P], F32R)
        qbd = sb("qbd", [P, 2, G, J, P], F32R)
        vboth = sb("values", [P, 2, B, H, DK + 1])
        vs = [vboth[:, n, :, :, :] for n in range(2)]
        rawmax = sb("rawmax", [P, G, J])
        negmax = sb("negmax", [P, G, P])
        oT = sb("oT", [P, G, P])
        on = sb("on", [P, H, DK])
        rec = sb("rec", [P, H])
        onT = sb("onT", [P, P])
        xhl = khl[1][:, :, :, :].rearrange("p a b t -> p a (b t)")

        def over(at, n):
            return conv[:, :, :, :].rearrange("p a b t -> p (a b t)")[:, at:at + n]

        BE = B * E
        sc, masked, replaced, coef = (over(BE * i, BE).rearrange("p (b e) -> p b e", b=B) for i in range(4))
        sfc = over(4 * BE, BE).rearrange("p (b g e) -> p b g e", b=B, g=GE)
        gcmp = over(5 * BE, 3 * BE).rearrange("p (i b g f) -> p i b g f", i=3, b=B, g=GE)
        low = sb("low", [P, GE, GE])
        top8 = sb("top8", [P, B, 8])
        chl = sb("chl", [P, B, 2, E], F16)
        identh = sb("identh", [P, P], F16)
        cT = sb("cT", [P, T], F16)
        sel = vboth[:, :, :, :, :].rearrange("p n b h d -> p (n b h d)").bitcast(F16)[:, 0:E * I]\
            .rearrange("p (e i) -> p e i", e=E)
        i2 = sb("i2", [P, E])
        parts = khl[0][:, :, :, :].rearrange("p a b t -> p (a b) t")
        whigu, wlogu = (parts[:, 4 * i:4 * i + 4, :].rearrange("p (k m) c -> p k m c", k=2) for i in range(2))
        whid, wlod = (parts[:, 8 + 2 * i:10 + 2 * i, :] for i in range(2))
        sg = qin[:, :, 0:P]
        gu = kin[:, :, 0:P]
        hx = ctxs[:, :, :]
        outs = qc[:, :, :].rearrange("p (c b) t -> p c (b t)", c=2)
        hhi = qbd[:, 0, :, :, :].rearrange("p g j t -> p g (j t)")
        hlo = qbd[:, 1, :, :, :].rearrange("p g j t -> p g (j t)")

        ld_x, ld_a, ld_b, ld_ctx, ld_mask = (sem(f"ld_{n}") for n in ("x", "a", "b", "ctx", "mask"))
        ld_w = [sem(f"ld_w{i}") for i in range(RING)]
        dve_step = sem("dve_step")
        pool_step = sem("pool_step")
        pads_ready = sem("pads_ready")
        xn_ready = sem("xn_ready")
        xT_done = sem("xT_done")
        xT_copied = sem("xT_copied")
        folded = sem("folded")
        fold_copied = sem("fold_copied")
        in_done = sem("in_done")
        in_copied = sem("in_copied")
        v_done = sem("v_done")
        v_copied = sem("v_copied")
        conv_part = sem("conv_part")
        conv_done = sem("conv_done")
        gelu_done = sem("gelu_done")
        tau_done = sem("tau_done")
        tau_ready = sem("tau_ready")
        delta_done = sem("delta_done")
        delta_sum = sem("delta_sum")
        delta_ready = sem("delta_ready")
        q_done = sem("q_done")
        q_ready = sem("q_ready")
        k_done = sem("k_done")
        k_ready = sem("k_ready")
        k2_done = sem("k2_done")
        k2_ready = sem("k2_ready")
        khi_ready = sem("khi_ready")
        klo_ready = sem("klo_ready")
        qhi_ready = sem("qhi_ready")
        qlo_ready = sem("qlo_ready")
        q_stacked = sem("q_stacked")
        k_stacked = sem("k_stacked")
        qst_ready = sem("qst_ready")
        kst_ready = sem("kst_ready")
        kbd_ready = [sem(f"kbd_ready{i}") for i in range(2)]
        picks_ready = sem("picks_ready")
        mask_ready = sem("mask_ready")
        const_ready = sem("const_ready")
        (scored, maxed, max_split, max_turned, qbd_ready, scoredT, exped, pv_done, o_copied, o_turned, normed,
         on_turned, on_copied, projected, residual) = (sem(n) for n in (
             "scored", "maxed", "max_split", "max_turned", "qbd_ready", "scoredT", "exped", "pv_done", "o_copied",
             "o_turned", "normed", "on_turned", "on_copied", "projected", "residual"))
        logits_done = sem("logits_done")
        scores_ready = sem("scores_ready")
        coef_ready = sem("coef_ready")
        coefT_done = sem("coefT_done")
        coefT_ready = sem("coefT_ready")
        xhi_ready = sem("xhi_ready")
        xlo_ready = sem("xlo_ready")
        x3T_ready = sem("x3T_ready")
        whigu_ready = sem("whigu_ready")
        wlogu_ready = sem("wlogu_ready")
        whid_ready = sem("whid_ready")
        wlod_ready = sem("wlod_ready")
        rows_ready = sem("rows_ready")
        ones_ready = sem("ones_ready")
        sel_ready = sem("sel_ready")
        bank4_zeroed = sem("bank4_zeroed")
        values_scaled = sem("values_scaled")
        coefb_done = sem("coefb_done")
        gate_done = sem("gate_done")
        up_done = sem("up_done")
        silu_done = sem("silu_done")
        gu_done = sem("gu_done")
        h_done = sem("h_done")
        hhi_ready = sem("hhi_ready")
        hlo_ready = sem("hlo_ready")
        down_done = sem("down_done")
        out_copied = sem("out_copied")
        stored = sem("stored")

        block = ctx.enter_context(nc.Block())

        def wait(eng, signal, value):
            if not isinstance(value, int) or value > 0:
                eng.wait_ge(signal, value)

        def loaded(pair, k):
            return 16 * (pair // RING) + 16 if isinstance(pair, int) else 4 * (pair - k) + 16 * (k // RING) + 16

        def over_units(eng, body, last):
            for n in range(PEELED):
                body(0, n)
            with eng.Fori(0, TRIPS) as it:
                for k in range(PEELED, PEELED + BODY):
                    body(it, k)
            for n in range(PEELED + BODY * TRIPS, last):
                body(0, n)

        @block.sync
        def _(sp):
            sp.dma_start(xres[:, :, :], x.rearrange("(b p) d -> p b d", p=P)).then_inc(ld_x, 16)
            sp.dma_start(pa[:, :], pack_a).then_inc(ld_a, 16)
            sp.dma_start(ctxs[:, :, :], ctxT.rearrange("p (b t) -> p b t", b=B)).then_inc(ld_ctx, 16)
            sp.dma_start(pb[:, :], pack_b).then_inc(ld_b, 16)
            sp.dma_start(masku[:, :, :], mask.rearrange("b q k -> q b k")).then_inc(ld_mask, 16)
            w3v = w3.rearrange("p (n m c) -> p n m c", m=3, c=P)
            for pair in range(RING):
                sp.dma_start(ring[:, pair, :, :], w3v[:, pair, :, :]).then_inc(ld_w[pair], 16)

            sp.wait_ge(rows_ready, 3)
            for s in range(STEPS):
                n, b = s // B, s % B
                sp.wait_ge(kst_ready, G * (2 * n + b // 4 + 1))
                wait(sp, scored, G * (s - 1))
                for j in range(J):
                    sp.dma_start(kbd[32 * j:32 * j + 32, s % 2, :, j, :].bitcast(F32),
                                 kst[n][32 * j:32 * j + 32, :, b, :].bitcast(F32)).then_inc(kbd_ready[s % 2], 16)

            def load(pair, slot):
                sp.wait_ge(wlogu_ready, pair + (1 - RING))
                sp.wait_ge(wlod_ready, pair + (1 - RING))
                src = w3v[:, pair, :, :] if isinstance(pair, int) else w3v[:, bass.ds(pair, 1), :, :]\
                    .rearrange("p o m c -> p (o m) c")
                sp.dma_start(ring[:, slot, :, :], src).then_inc(ld_w[slot], 16)

            with sp.Fori(0, (PAIRS - RING) // RING) as it:
                for k in range(RING):
                    load(RING * it + (RING + k), k)
            load(PAIRS, PAIRS % RING)
            for c in range(2):
                sp.wait_ge(out_copied, c + 1)
                sp.dma_start(outT[:, HALF * c:HALF * c + HALF], outs[:, c, :]).then_inc(stored, 16)
            sp.wait_ge(stored, 32)

        @block.tensor
        def _(pe):
            def half(t, c, shift=1):
                return t[:, 4 * c:4 * c + 4, shift:shift + P]

            def mm(out, lhsT, rhs, start=True, stop=True):
                return pe.matmul(out, lhsT, rhs, start=start, stop=stop)

            def turn_inputs(n, c, out):
                for b in range(4 * c, 4 * c + 4):
                    pe.wait_ge(xn_ready, B * n + b + 1)
                    last = pe.transpose(out[:, P * (b % 4):P * (b % 4) + P], xn[:, b, :], ident)
                last.then_inc(xT_done, 1)

            def stack(out, m, hl, c, g, signal):
                mm(out[:, :], pick[:, m, g, :], hl[:, 0, 4 * c:4 * c + 4, :], True, False)
                mm(out[:, :], pick[:, m + 1, g, :], hl[:, 1, 4 * c:4 * c + 4, :], False, True).then_inc(signal, 1)

            pe.wait_ge(ld_a, 16)
            for n, (conv_w, proj, bias) in enumerate((("cq", "qp2T", "cqb"), ("ck", "kp2T", "ckb"))):
                for k in range(3):
                    c0 = cols_a[conv_w][0] + P * k
                    mm(bank[2 + n][:, P * k:P * k + P], pa[:, c0:c0 + P], A(proj))
                mm(bank[4][:, n:n + 1], A(proj), A(bias)).then_inc(folded, 1)
            for c in range(2):
                turn_inputs(0, c, bank[c])
            pe.wait_ge(ld_ctx, 16)
            pe.wait_ge(ld_b, 16)
            pe.wait_ge(pads_ready, 6)
            for c in range(2):
                pe.wait_ge(xT_copied, c + 1)
                mm(bank[5 + c][:, :], A("wqT"), half(xnT, c)).then_inc(in_done, 1)
            for c in range(2):
                mm(bank[7 - 7 * c][:, :], A("wkT"), half(xnT, c)).then_inc(in_done, 1)
            pe.wait_ge(fold_copied, 4)
            pe.wait_ge(in_copied, 2)
            for c in range(2):
                for k in range(3):
                    last = mm(bank[5 + c][:, :], foldq[:, k, :], half(qin, c, k), k == 0, k == 2)
                last.then_inc(q_done, 1)
            pe.wait_ge(in_copied, 4)
            for c in range(2):
                for k in range(3):
                    last = mm(bank[7 - 7 * c][:, :], foldk[:, k, :], half(kin, c, k), k == 0, k == 2)
                last.then_inc(k_done, 1)
            for c in range(2):
                mm(bank[1 + c][:, :], Bw("wk"), ctxs[:, 4 * c:4 * c + 4, :]).then_inc(k2_done, 1)
            pe.wait_ge(gelu_done, 2)
            pe.wait_ge(const_ready, 1)
            for c in range(2):
                for r in range(2):
                    last = mm(bank[3 + c][:, :], tau2r[:, r, :, :], conv[:, r, 4 * c:4 * c + 4, :], r == 0, r == 1)
                last.then_inc(tau_done, 1)
            for b in range(B):
                if b % 4 == 0:
                    pe.wait_ge(khi_ready, 3 + b // 4)
                last = mm(bank[1 + b // 4][:, P * (b % 4):P * (b % 4) + P], xnT[:, b, 1:1 + P], A("wvT"))
                if b % 4 == 3:
                    last.then_inc(v_done, 1)
            pe.wait_ge(picks_ready, 1)

            def stacks(c):
                for g in range(G):
                    i = G * c + g
                    if g == 0:
                        pe.wait_ge(qlo_ready, c + 1)
                        pe.wait_ge(klo_ready, c + 1)
                        pe.wait_ge(q_ready, 2)
                        pe.wait_ge(khi_ready, 2)
                    wait(pe, qst_ready, i - 1)
                    stack(bank[5 + i % 2], 0, qhl, c, g, q_stacked)
                    wait(pe, kst_ready, i - 1)
                    stack(bank[7 - 7 * (i % 2)], 2, khl[0], c, g, k_stacked)

            stacks(0)
            pe.wait_ge(gelu_done, 4)
            pe.wait_ge(tau_ready, 2)
            d0 = cols_a["del2T"][0]
            for b in range(B):
                for r in range(2):
                    last = mm(bank[3][:, H * b:H * b + H], conv[:, 2 + r, b, :], pa[:, d0 + H * r:d0 + H * r + H],
                              r == 0, r == 1)
            last.then_inc(delta_done, 1)
            for b in range(B):
                if b % 4 == 0:
                    pe.wait_ge(v_copied, b // 4 + 1)
                last = mm(bank[1 + b // 4][:, P * (b % 4):P * (b % 4) + P], ctxs[:, b, :], Bw("wv"))
                if b % 4 == 3:
                    last.then_inc(v_done, 1)
            stacks(1)
            pe.wait_ge(klo_ready, 4)
            for c in range(2):
                for g in range(G):
                    i = G * (2 + c) + g
                    pe.wait_ge(kst_ready, i - 1)
                    stack(bank[7 - 7 * (i % 2)], 2, khl[1], c, g, k_stacked)

            def scores(s, g):
                n, b = s // B, s % B
                i = G * s + g
                if g == 0:
                    pe.wait_ge(kbd_ready[s % 2], 16 * J * (s // 2 + 1))
                    if n == 0 or b % 4 == 0:
                        pe.wait_ge(qst_ready, G * (2 * n + b // 4 + 1))
                wait(pe, maxed, i - 1)
                out = bank[i % 2]
                if n == 1:
                    pe.matmul(out[:, :].rearrange("p (g k) -> p g k", g=J), identb[:, :],
                              maskb[:, b, :].unsqueeze(1).broadcast_to([P, J, P]), start=True, stop=False)
                mm(out[:, :], qst[:, g, b, :], kbd[:, s % 2, g, :, :], n == 0, True).then_inc(scored, 1)

            def turn_max(s):
                pe.wait_ge(max_split, s + 1)
                wait(pe, qbd_ready, s)
                for g in range(G):
                    last = pe.transpose(bank[5][:, P * g:P * g + P], negmax[:, g, :], ident)
                last.then_inc(max_turned, 1)

            def scoresT(s, g):
                n, b = s // B, s % B
                i = G * s + g
                if g == 0:
                    pe.wait_ge(qbd_ready, s + 1)
                wait(pe, exped, i - 1)
                out = bank[2 + i % 2]
                if n == 1:
                    pe.matmul(out[:, :].rearrange("p (g q) -> p g q", g=J), maskb[:, b, :],
                              identb[:, :].unsqueeze(1).broadcast_to([P, J, P]), start=True, stop=False)
                mm(out[:, :], kst[n][:, g, b, :], qbd[:, s % 2, g, :, :], n == 0, True).then_inc(scoredT, 1)

            def pv(s, g):
                i = G * s + g
                pe.wait_ge(exped, i + 1)
                if g == 0:
                    wait(pe, o_copied, s)
                for j in range(J):
                    last = mm(bank[4][32 * j:32 * j + DK + 1, P * g:P * g + P], vs[s // B][:, s % B, J * g + j, :],
                              probs[:, i % 8, j, :])
                last.then_inc(pv_done, 1)

            def turn_out(s):
                pe.wait_ge(o_copied, s + 1)
                wait(pe, residual, s)
                for g in range(G):
                    last = pe.transpose(bank[6][:, P * g:P * g + P], oT[:, g, :], ident)
                last.then_inc(o_turned, 1)

            def turn_on(s):
                pe.wait_ge(normed, s + 1)
                pe.transpose(bank[6][:, 0:P], on[:, :, :].rearrange("p h d -> p (h d)"), ident)\
                    .then_inc(on_turned, 1)

            def project(s):
                pe.wait_ge(on_copied, s + 1)
                mm(bank[6][:, P:2 * P], onT[:, :], A("woT") if s < B else Bw("wo")).then_inc(projected, 1)

            def second_inputs(c):
                pe.wait_ge(qst_ready, G * (2 + c))
                turn_inputs(1, c, bank[7])

            def second_queries(c):
                pe.wait_ge(xT_copied, 3 + c)
                mm(bank[7][:, :], Bw("wq"), half(xnT, c)).then_inc(q_done, 1)

            def second_stack(c, g):
                pe.wait_ge(qlo_ready, 3 + c)
                wait(pe, qst_ready, G * (2 + c) + g)
                stack(bank[7], 0, qhl, c, g, q_stacked)

            pe.wait_ge(kst_ready, 4 * G)
            pe.wait_ge(v_copied, 4)
            pe.wait_ge(delta_sum, 1)
            pe.wait_ge(bank4_zeroed, 1)
            pe.wait_ge(values_scaled, 1)
            for g in range(G):
                scores(0, g)
            for s in range(STEPS + 1):
                now, ahead = s < STEPS, s + 1 < STEPS
                if s == B - 1:
                    pe.wait_ge(mask_ready, 1)
                second = {6: 0, 10: 1}.get(s)
                if now:
                    turn_max(s)
                if second is not None:
                    second_inputs(second)
                if s >= 2:
                    project(s - 2)
                if s >= 1:
                    for g in range(G):
                        pv(s - 1, g)
                if second is not None:
                    second_queries(second)
                if now:
                    scoresT(s, 0)
                    scoresT(s, 1)
                if ahead:
                    scores(s + 1, 0)
                if now:
                    scoresT(s, 2)
                if ahead:
                    scores(s + 1, 1)
                if now:
                    scoresT(s, 3)
                if s >= 1:
                    turn_out(s - 1)
                if ahead:
                    scores(s + 1, 2)
                    scores(s + 1, 3)
                if second is not None:
                    for g in range(G):
                        second_stack(second, g)
                if s >= 1:
                    turn_on(s - 1)
            project(STEPS - 1)

            for c in range(2):
                turn_inputs(2, c, bank[2 + c])
            pe.wait_ge(x3T_ready, 2)
            r0, r1 = cols_b["routerT"]
            for b in range(B):
                last = mm(bank[6][:, E * b:E * b + E], xnT[:, b, 1:1 + P], pb[:, r0:r1])
            last.then_inc(logits_done, 1)
            pe.wait_ge(residual, STEPS)
            for b in range(B):
                pe.matmul(bank[b // 4][:, P * (b % 4):P * (b % 4) + P], xres[:, b, :], ident,
                          start=(b % 4 == 0), stop=False, skip_group_check=True)
            pe.wait_ge(xhi_ready, 2)
            pe.wait_ge(xlo_ready, 2)

            def unit(it, k):
                n, pair = BODY * it + k, BODY // 2 * it + k // 2
                peeled = isinstance(it, int)
                c, w = k % 2, k // 2 % 2
                if not peeled or n < UNITS:
                    if peeled and n == 2:
                        pe.wait_ge(coef_ready, 1)
                        for b in range(B):
                            last = pe.transpose(bank[7][:, :].bitcast(F16)[:, P * b:P * b + P],
                                                chl[:, b, :, :].rearrange("p a e -> p (a e)"), identh[:, :])
                        last.then_inc(coefT_done, 1)
                    xh, xl = xhl[:, 0, HALF * c:HALF * c + HALF], xhl[:, 1, HALF * c:HALF * c + HALF]
                    if c == 0:
                        pe.wait_ge(wlogu_ready, pair + 1)
                    for m, (out, signal, used) in enumerate((
                            (bank[2 + c], gate_done, silu_done), (bank[4 + c], up_done, gu_done))):
                        wait(pe, used, n + (-1))
                        mm(out[:, :], whigu[:, w, m, :], xh, True, False)
                        mm(out[:, :], whigu[:, w, m, :], xl, False, False)
                        mm(out[:, :], wlogu[:, w, m, :], xh, False, True).then_inc(signal, 1)
                    if peeled and n == 2:
                        pe.wait_ge(coefT_ready, 1)
                        pe.wait_ge(sel_ready, 1)
                    if not peeled or n >= 2:
                        wait(pe, h_done, n + (-1))
                        e0 = BODY * it + (2 * (k // 2) - 2)
                        pe.matmul(bank[6 + c][:, :], sel[:, bass.ds(e0, 2), :].rearrange("p e i -> p (e i)"),
                                  cT[:, HALF * c:HALF * c + HALF], start=True, stop=True).then_inc(coefb_done, 1)
                if not peeled or n >= LAG:
                    d, kd = BODY * it + (k - LAG), k - LAG
                    c, w = kd % 2, kd // 2 % 2
                    if c == 0:
                        pe.wait_ge(wlod_ready, BODY // 2 * it + (kd // 2 + 1))
                    pe.wait_ge(hlo_ready, BODY * it + (kd + 1))
                    acc, stop = bank[c][:, :], peeled and d >= UNITS - 2
                    pe.matmul(acc, whid[:, w, :], hhi[:, kd % 4, :], start=False, stop=False, skip_group_check=True)
                    pe.matmul(acc, whid[:, w, :], hlo[:, kd % 4, :], start=False, stop=False, skip_group_check=True)
                    pe.matmul(acc, wlod[:, w, :], hhi[:, kd % 4, :], start=False, stop=stop,
                              skip_group_check=True).then_inc(down_done, 1)

            over_units(pe, unit, UNITS + LAG)

        @block.scalar
        def _(act):
            def half(t, c, shift=0):
                return t[:, 4 * c:4 * c + 4, shift:shift + P]

            def four(b):
                return bank[b][:, :].rearrange("p (b t) -> p b t", b=4)

            def copy_inputs(n, c, b):
                act.wait_ge(xT_done, 2 * n + c + 1)
                act.activation(half(xnT, c, 1), four(b), ACT.Copy).then_inc(xT_copied, 1)

            act.wait_ge(pads_ready, 6)
            copy_inputs(0, 0, 0)
            copy_inputs(0, 1, 1)

            def first_taps(n, w, bias):
                for r in range(2):
                    w0, b0 = cols_a[w][0] + 3 * r, cols_a[bias][0] + r
                    act.activation(conv[:, 2 * n + r, :, :], xnT[:, :, 0:P], ACT.Identity,
                                   bias=pa[:, b0:b0 + 1], scale=pa[:, w0:w0 + 1]).then_inc(conv_part, 1)

            def gelu(n):
                for r in range(2):
                    act.wait_ge(conv_done, 2 * n + r + 1)
                    act.activation(conv[:, 2 * n + r, :, :], conv[:, 2 * n + r, :, :], ACT.Gelu).then_inc(gelu_done, 1)

            def biased(dst, n, bias, banks):
                for c in range(2):
                    act.wait_ge(in_done, 2 * n + c + 1)
                    act.activation(half(dst, c, 1), four(banks[c]), ACT.Identity, bias=A(bias)).then_inc(in_copied, 1)

            def keys(n, c, b, bias):
                act.activation(half(kc[n], c), four(b), ACT.Identity, bias=bias).then_inc(k_ready, 1)
                act.activation(half(khl[n][:, 0, :, :], c), four(b), ACT.Identity, bias=bias).then_inc(khi_ready, 1)

            def stacked_keys(n, c, g):
                i = G * (2 * n + c) + g
                act.wait_ge(k_stacked, i + 1)
                act.activation(half(kst[n][:, g, :, :], c), four(7 - 7 * (i % 2)), ACT.Identity,
                               bias=A("ones_rows")).then_inc(kst_ready, 1)

            act.wait_ge(ld_a, 16)
            biased(qin, 0, "bq", (5, 6))
            first_taps(0, "tau1", "tau1b")
            biased(kin, 1, "bk", (7, 0))
            first_taps(1, "del1", "del1b")
            act.wait_ge(q_done, 2)
            for c in range(2):
                act.wait_ge(k_done, c + 1)
                keys(0, c, 7 - 7 * c, foldb[:, 1:2])
            gelu(0)
            act.wait_ge(ld_b, 16)
            for c in range(2):
                act.wait_ge(k2_done, c + 1)
                keys(1, c, 1 + c, Bw("bk"))
            gelu(1)
            for c in range(2):
                act.wait_ge(tau_done, c + 1)
                act.activation(half(tauT, c), four(3 + c), ACT.Sigmoid, bias=A("tau2b")).then_inc(tau_ready, 1)

            def high_queries(c):
                act.wait_ge(q_ready, c + 1)
                act.activation(half(qhl[:, 0, :, :], c), half(qc, c), ACT.Copy).then_inc(qhi_ready, 1)

            high_queries(0)
            high_queries(1)
            for g in range(G):
                stacked_keys(0, 0, g)
            act.wait_ge(delta_sum, 1)
            act.activation(edelta[:, :, :], edelta[:, :, :], ACT.Sigmoid).then_inc(delta_ready, 1)
            act.wait_ge(delta_ready, 1)
            act.activation(edelta[:, :, :], edelta[:, :, :], ACT.Exp).then_inc(delta_ready, 1)
            for n, c in ((0, 1), (1, 0), (1, 1)):
                for g in range(G):
                    stacked_keys(n, c, g)

            def copy_o(s):
                act.wait_ge(pv_done, G * s + G)
                wait(act, o_turned, s)
                act.activation(oT[:, :, :].rearrange("p g t -> p (g t)"), bank[4][:, :], ACT.Copy)\
                    .then_inc(o_copied, 1)

            def copy_on(s):
                act.wait_ge(on_turned, s + 1)
                wait(act, projected, s)
                act.activation(onT[:, :], bank[6][:, 0:P], ACT.Copy).then_inc(on_copied, 1)

            def exponential(s, g):
                i = G * s + g
                act.wait_ge(scoredT, i + 1)
                wait(act, pv_done, i - 7)
                act.activation(probs[:, i % 8, :, :].rearrange("p j t -> p (j t)"), bank[2 + i % 2][:, :],
                               ACT.Exp, scale=SCALE).then_inc(exped, 1)

            for s in range(STEPS + 1):
                second = {6: 0, 10: 1}.get(s)
                if second is not None:
                    copy_inputs(1, second, 7)
                if s >= 1:
                    copy_o(s - 1)
                if second is not None:
                    act.wait_ge(q_done, 3 + second)
                    act.wait_ge(q_stacked, G * (2 + second))
                    act.activation(half(qc, second), four(7), ACT.Identity, bias=Bw("bq")).then_inc(q_ready, 1)
                    act.activation(half(qhl[:, 0, :, :], second), four(7), ACT.Identity, bias=Bw("bq"))\
                        .then_inc(qhi_ready, 1)
                if s < STEPS:
                    for g in range(G):
                        exponential(s, g)
                if second is not None:
                    for g in range(G):
                        act.wait_ge(q_stacked, G * (2 + second) + g + 1)
                        act.activation(half(qst[:, g, :, :], second), four(7), ACT.Copy).then_inc(qst_ready, 1)
                if s >= 1:
                    copy_on(s - 1)

            for c in range(2):
                act.wait_ge(xT_done, 4 + c + 1)
                act.activation(half(xnT, c, 1), four(2 + c), ACT.Copy).then_inc(x3T_ready, 1)
                act.activation(xhl[:, 0, HALF * c:HALF * c + HALF].rearrange("p (b t) -> p b t", b=4),
                               four(2 + c), ACT.Copy).then_inc(xhi_ready, 1)
            act.wait_ge(logits_done, 1)
            act.activation(sc[:, :, :].rearrange("p b e -> p (b e)"), bank[6][:, :], ACT.Sigmoid)\
                .then_inc(scores_ready, 1)

            def high_gate_up(pair, k):
                act.wait_ge(ld_w[k % RING], loaded(pair, k))
                act.activation(whigu[:, k % 2, :, :], ring[:, k % RING, 0:2, :], ACT.Copy).then_inc(whigu_ready, 1)

            def unit(it, k):
                n, pair, c = BODY * it + k, BODY // 2 * it + k // 2, k % 2
                act.wait_ge(gate_done, n + 1)
                wait(act, gu_done, n + (-1))
                act.activation(sg[:, 4 * c:4 * c + 4, :], four(2 + c), ACT.Silu).then_inc(silu_done, 1)
                if c == 0 and (not isinstance(it, int) or pair < PAIRS):
                    wait(act, up_done, n)
                    high_gate_up(pair + 1, k // 2 + 1)
                act.wait_ge(h_done, n + 1)
                wait(act, down_done, n + (-3))
                act.activation(hhi[:, k % 4, :].rearrange("p (b t) -> p b t", b=4), hx[:, 4 * c:4 * c + 4, :],
                               ACT.Copy).then_inc(hhi_ready, 1)

            high_gate_up(0, 0)
            over_units(act, unit, UNITS)
            for c in range(2):
                act.wait_ge(down_done, UNITS - 1 + c)
                act.activation(outs[:, c, :], bank[c][:, :], ACT.Copy).then_inc(out_copied, 1)

        @block.vector
        def _(dve):
            steps = [0]

            def link(ins):
                ins.then_inc(dve_step, 1)
                steps[0] += 1
                dve.wait_ge(dve_step, steps[0])

            def stats_of(b):
                dve.bn_stats(stats[:, b, :], xres[:, b, :]).then_inc(dve_step, 1)
                steps[0] += 1
                dve.wait_ge(dve_step, steps[0])
                link(dve.bn_aggr(mv[:, b, :], stats[:, b, :]))

            def half(t, c, shift=0):
                return t[:, 4 * c:4 * c + 4, shift:shift + P]

            def four(b):
                return bank[b][:, :].rearrange("p (b t) -> p b t", b=4)

            def normalise(n, lo, hi):
                v, y, a, c2, raw = (nwt[:, i, lo:hi] for i in range(5))
                link(dve.tensor_scalar(v, mv[:, lo:hi, 1], EPS, None, ALU.add))
                link(dve.tensor_scalar(raw.bitcast(I32), v.bitcast(I32), 1, None, ALU.logical_shift_right))
                link(dve.tensor_scalar(y.bitcast(I32), raw.bitcast(I32), -1.0, RSQRT_MAGIC, ALU.mult, ALU.add))
                for _ in range(4):
                    link(dve.tensor_tensor(a, v, y, ALU.mult))
                    link(dve.tensor_tensor(c2, a, y, ALU.mult))
                    link(dve.tensor_scalar(c2, c2, -0.5, 1.5, ALU.mult, ALU.add))
                    link(dve.tensor_tensor(y, y, c2, ALU.mult))
                wait(dve, xT_done, 2 * n)
                for b in range(lo, hi):
                    dve.tensor_scalar(xn[:, b, :], xres[:, b, :], mv[:, b, 0:1], nwt[:, 1, b:b + 1],
                                      ALU.subtract, ALU.mult).then_inc(xn_ready, 1)

            def add_bias(bias, lo, hi, done):
                dve.wait_ge(xn_ready, done)
                link(dve.tensor_tensor(xres[:, lo:hi, :], xres[:, lo:hi, :],
                                       bias.unsqueeze(1).broadcast_to([P, hi - lo, P]), ALU.add))

            dve.wait_ge(ld_x, 16)
            for b in range(B):
                stats_of(b)
            normalise(0, 0, B)
            dve.wait_ge(ld_a, 16)
            add_bias(A("bo"), 0, B, B)
            t0 = cols_a["tau2T"][0]
            dve.tensor_copy(tau2r[:, :, :, :].rearrange("p r h d -> p (r h) d"),
                            pa[:, t0:t0 + 2 * H].unsqueeze(2).broadcast_to([P, 2 * H, DK])).then_inc(const_ready, 1)
            for n, (dst, proj) in enumerate(((foldq, "qp1T"), (foldk, "kp1T"))):
                dve.wait_ge(folded, n + 1)
                link(dve.tensor_copy(dst[:, :, :].rearrange("p k o -> p (k o)"), bank[2 + n][:, 0:3 * P]))
                dve.tensor_tensor(dst[:, 1, :], dst[:, 1, :], A(proj), ALU.add).then_inc(fold_copied, 1)
            for n, bias in enumerate(("qpb", "kpb")):
                dve.tensor_tensor(foldb[:, n:n + 1], bank[4][:, n:n + 1], A(bias), ALU.add).then_inc(fold_copied, 1)
            def later_taps(n, w):
                for r in range(2):
                    w0 = cols_a[w][0] + 3 * r
                    dve.wait_ge(conv_part, 2 * n + r + 1)
                    y = conv[:, 2 * n + r, :, :]
                    link(dve.scalar_tensor_tensor(out=y, in0=xnT[:, :, 1:1 + P], scalar=pa[:, w0 + 1:w0 + 2],
                                                  in1=y, op0=ALU.mult, op1=ALU.add))
                    dve.scalar_tensor_tensor(out=y, in0=xnT[:, :, 2:2 + P], scalar=pa[:, w0 + 2:w0 + 3],
                                             in1=y, op0=ALU.mult, op1=ALU.add).then_inc(conv_done, 1)

            dve.wait_ge(xT_copied, 2)
            later_taps(0, "tau1")
            later_taps(1, "del1")
            for m, at in ((0, S_HI), (0, S_LO), (1, S_MID), (2, S_HI), (2, S_MID), (3, S_LO)):
                rows = pick[:, m, :, :].rearrange("p g r -> p (g r)").rearrange("p (h r) -> p h r", h=H)
                dve.wait_ge(rows_ready, 3)
                last = dve.tensor_copy(rows[:, :, at:at + DK], ident.rearrange("p (h d) -> p h d", h=H))
            last.then_inc(picks_ready, 1)
            dve.tensor_copy(identh[:, :], ident).then_inc(dve_step, 1)
            dve.tensor_copy(identb[:, :], ident).then_inc(dve_step, 1)
            steps[0] += 2

            def values(n, bias, base):
                for c in range(2):
                    dve.wait_ge(v_done, base + c + 1)
                    for b in range(4 * c, 4 * c + 4):
                        last = dve.tensor_tensor(
                            vs[n][:, b, :, 0:DK],
                            bank[1 + c][:, P * (b % 4):P * (b % 4) + P].rearrange("p (h d) -> p h d", h=H),
                            bias.rearrange("p (h d) -> p h d", h=H), ALU.add)
                    last.then_inc(v_copied, 1)

            for c in range(2):
                dve.wait_ge(q_done, c + 1)
                dve.wait_ge(tau_ready, c + 1)
                dve.scalar_tensor_tensor(out=half(qc, c), in0=four(5 + c), scalar=foldb[:, 0:1], in1=half(tauT, c),
                                         op0=ALU.add, op1=ALU.mult).then_inc(q_ready, 1)

            def low_queries(n, c):
                dve.wait_ge(qhi_ready, 2 * n + c + 1)
                dve.tensor_tensor(half(qhl[:, 1, :, :], c), half(qc, c), half(qhl[:, 0, :, :], c).bitcast(F32),
                                  ALU.subtract).then_inc(qlo_ready, 1)

            def stacked_queries(c, g):
                i = G * c + g
                dve.wait_ge(q_stacked, i + 1)
                dve.tensor_copy(half(qst[:, g, :, :], c), four(5 + i % 2)).then_inc(qst_ready, 1)

            low_queries(0, 0)
            low_queries(0, 1)
            for g in range(G):
                stacked_queries(0, g)
            values(0, A("bv"), 0)
            dve.wait_ge(delta_done, 1)
            dve.tensor_tensor(edelta[:, :, :], bank[3][:, 0:B * H].rearrange("p (b h) -> p b h", b=B),
                              A("del2b").unsqueeze(1).broadcast_to([P, B, H]), ALU.add).then_inc(delta_sum, 1)
            dve.wait_ge(ld_b, 16)
            values(1, Bw("bv"), 2)
            for g in range(G):
                stacked_queries(1, g)
            dve.wait_ge(ones_ready, 3)
            dve.wait_ge(delta_ready, 2)
            dve.wait_ge(v_copied, 2)
            v0 = vs[0][:, :, :, :].rearrange("p b h d -> p (b h) d")
            dve.tensor_tensor(v0, v0, edelta[:, :, :].rearrange("p b h -> p (b h)").unsqueeze(2)
                              .broadcast_to([P, B * H, DK + 1]), ALU.mult).then_inc(values_scaled, 1)
            dve.wait_ge(tau_ready, 2)
            dve.memset(bank[4][:, :], 0.0).then_inc(bank4_zeroed, 1)

            def maximum(s, g):
                i = G * s + g
                dve.wait_ge(scored, i + 1)
                dve.tensor_reduce(rawmax[:, g, :].unsqueeze(2), bank[i % 2][:, :].rearrange("p (j k) -> p j k", j=J),
                                  AX.X, ALU.max, negate=True).then_inc(maxed, 1)

            def split_max(s):
                dve.wait_ge(maxed, G * s + G)
                wait(dve, max_turned, s)
                cols = negmax[:, :, :].rearrange("p g (j c) -> p g j c", j=J)
                link(dve.tensor_copy(cols[:, :, :, 0:1].bitcast(F32R), rawmax[:, :, :].unsqueeze(3)))
                dve.tensor_tensor(cols[:, :, :, 1:2], rawmax[:, :, :].unsqueeze(3), cols[:, :, :, 0:1],
                                  ALU.subtract).then_inc(max_split, 1)

            def queries_with_max(s):
                dve.wait_ge(max_turned, s + 1)
                wait(dve, scoredT, G * (s - 1))
                for j in range(J):
                    r = slice(32 * j, 32 * j + 32)
                    last = dve.tensor_tensor(qbd[r, s % 2, :, j, :], bank[5][r, :].rearrange("p (g t) -> p g t", g=G),
                                             qst[r, :, s % B, :].bitcast(F32), ALU.add)
                last.then_inc(qbd_ready, 1)

            def norm(s):
                dve.wait_ge(o_turned, s + 1)
                o = bank[6][:, :].rearrange("p (h c) -> p h c", h=H)
                link(dve.reciprocal(rec[:, :].unsqueeze(2), o[:, :, DK:DK + 1]))
                wait(dve, on_turned, s)
                dve.tensor_tensor(on[:, :, :], o[:, :, 0:DK], rec[:, :].unsqueeze(2).broadcast_to([P, H, DK]),
                                  ALU.mult).then_inc(normed, 1)

            def add_residual(s):
                b = s % B
                dve.wait_ge(projected, s + 1)
                dve.tensor_tensor(xres[:, b, :], xres[:, b, :], bank[6][:, P:2 * P], ALU.add).then_inc(residual, 1)
                dve.wait_ge(residual, s + 1)
                stats_of(b)

            dve.wait_ge(rows_ready, 3)
            dve.wait_ge(ones_ready, 3)
            for g in range(G):
                maximum(0, g)
            for s in range(STEPS + 1):
                if s == 2:
                    dve.wait_ge(ld_mask, 16)
                    dve.tensor_scalar(maskb[:, :, :], masku[:, :, :], MASKED, None, ALU.mult).then_inc(mask_ready, 1)
                if s < STEPS:
                    split_max(s)
                    queries_with_max(s)
                if s >= 2:
                    add_residual(s - 2)
                if s in (5, 9):
                    c = (s - 5) // 4
                    normalise(1, 4 * c, 4 * c + 4)
                if s + 1 < STEPS:
                    maximum(s + 1, 0)
                    maximum(s + 1, 1)
                if s in (6, 10):
                    c = (s - 6) // 4
                    add_bias(Bw("bo"), 4 * c, 4 * c + 4, B + 4 * c + 4)
                    low_queries(1, c)
                if s >= 1:
                    norm(s - 1)
                if s + 1 < STEPS:
                    maximum(s + 1, 2)
                    maximum(s + 1, 3)
            add_residual(STEPS - 1)
            normalise(2, 0, B)
            for c in range(2):
                dve.wait_ge(xhi_ready, c + 1)
                dve.wait_ge(x3T_ready, c + 1)
                dve.tensor_tensor(xhl[:, 1, HALF * c:HALF * c + HALF].rearrange("p (b t) -> p b t", b=4),
                                  xnT[:, 4 * c:4 * c + 4, 1:1 + P],
                                  xhl[:, 0, HALF * c:HALF * c + HALF].bitcast(F32).rearrange("p (b t) -> p b t", b=4),
                                  ALU.subtract).then_inc(xlo_ready, 1)

            def low_gate_up(pair, k):
                dve.wait_ge(whigu_ready, pair + 1)
                dve.tensor_tensor(wlogu[:, k % 2, :, :], ring[:, k % RING, 0:2, :], whigu[:, k % 2, :, :].bitcast(F32),
                                  ALU.subtract).then_inc(wlogu_ready, 1)

            def down_weights(pair, k):
                dve.wait_ge(ld_w[k % RING], loaded(pair, k))
                dve.tensor_copy(whid[:, k % 2, :], ring[:, k % RING, 2, :]).then_inc(whid_ready, 1)
                dve.wait_ge(whid_ready, pair + 1)
                dve.tensor_tensor(wlod[:, k % 2, :], ring[:, k % RING, 2, :], whid[:, k % 2, :].bitcast(F32),
                                  ALU.subtract).then_inc(wlod_ready, 1)

            low_gate_up(0, 0)
            low_gate_up(1, 1)
            down_weights(0, 0)

            dve.wait_ge(scores_ready, 1)
            link(dve.tensor_tensor(sfc[:, :, :, :].rearrange("p b g e -> p b (g e)"), sc[:, :, :],
                                   Bw("e_bias").unsqueeze(1).broadcast_to([P, B, E]), ALU.add))
            NG = B * GE

            def buf(i, n):
                at = (0, 256, 512, 640, 768, 896)
                return tauT[:, :, :].rearrange("p b t -> p (b t)")[:, at[i]:at[i] + n] if i < 6 \
                    else xn[:, i - 6, 0:n]
            s8 = sfc[:, :, :, :].rearrange("p b g e -> p (b g) e")
            a4 = buf(0, NG * 4).rearrange("p (n e) -> p n e", e=4)
            b4 = buf(1, NG * 4).rearrange("p (n e) -> p n e", e=4)
            link(dve.tensor_tensor(a4, s8[:, :, 0:4], s8[:, :, 4:8], ALU.max))
            link(dve.tensor_tensor(b4, s8[:, :, 0:4], s8[:, :, 4:8], ALU.min))
            hi, lo = a4, b4
            at = 2
            for width in (2, 1):
                nh, t1, t2, nl = (buf(at + i, NG * width).rearrange("p (n e) -> p n e", e=width) for i in range(4))
                at += 4
                link(dve.tensor_tensor(nh, hi[:, :, 0:width], hi[:, :, width:2 * width], ALU.max))
                link(dve.tensor_tensor(t1, hi[:, :, 0:width], hi[:, :, width:2 * width], ALU.min))
                link(dve.tensor_tensor(t2, lo[:, :, 0:width], lo[:, :, width:2 * width], ALU.max))
                link(dve.tensor_tensor(nl, t1, t2, ALU.max))
                hi, lo = nh, nl
            gs = buf(10, NG).rearrange("p (b g) -> p b g", g=GE)
            link(dve.tensor_tensor(gs, hi[:, :, 0].rearrange("p (b g) -> p b g", g=GE),
                                   lo[:, :, 0].rearrange("p (b g) -> p b g", g=GE), ALU.add))
            flat = lambda i: gcmp[:, i, :, :, :].rearrange("p b g f -> p (b g) f")
            other = gs.unsqueeze(2).broadcast_to([P, B, GE, GE])
            own = gs.unsqueeze(3).broadcast_to([P, B, GE, GE])
            link(dve.tensor_tensor(gcmp[:, 0, :, :, :], other, own, ALU.is_gt))
            link(dve.tensor_tensor(gcmp[:, 1, :, :, :], other, own, ALU.is_equal))
            dve.wait_ge(ones_ready, 3 + GE)
            lowb = low[:, :, :].rearrange("p g f -> p (g f)").unsqueeze(1).broadcast_to([P, B, GE * GE])
            f2 = lambda i: gcmp[:, i, :, :, :].rearrange("p b g f -> p b (g f)")
            link(dve.tensor_tensor(f2(2), f2(1), lowb, ALU.mult))
            link(dve.tensor_tensor(f2(0), f2(0), f2(2), ALU.add))
            rank = buf(11, NG)
            link(dve.tensor_reduce(rank, flat(0), AX.X, ALU.add))
            chosen = buf(2, NG)
            link(dve.tensor_scalar(chosen, rank, TOP_GROUPS - 0.5, None, ALU.is_lt))
            m3 = masked[:, :, :].rearrange("p b (g e) -> p (b g) e", g=GE)
            link(dve.tensor_tensor(m3, s8, chosen.unsqueeze(2).broadcast_to([P, NG, E // GE]), ALU.mult))
            for b in range(B):
                dve.max(top8[:, b, :], masked[:, b, :]).then_inc(dve_step, 1)
            steps[0] += B
            dve.wait_ge(dve_step, steps[0])
            for b in range(B):
                dve.match_replace(replaced[:, b, :], top8[:, b, :], masked[:, b, :], -3e38).then_inc(dve_step, 1)
            steps[0] += B
            dve.wait_ge(dve_step, steps[0])
            link(dve.tensor_tensor(coef[:, :, :], replaced[:, :, :], masked[:, :, :], ALU.not_equal))
            link(dve.tensor_tensor(coef[:, :, :], coef[:, :, :], sc[:, :, :], ALU.mult))
            wsum = buf(3, B)
            link(dve.tensor_reduce(wsum, coef[:, :, :], AX.X, ALU.add))
            link(dve.tensor_scalar(wsum, wsum, 1e-20, None, ALU.add))
            link(dve.reciprocal(wsum, wsum))
            link(dve.tensor_scalar(wsum, wsum, ROUTE_SCALE, None, ALU.mult))
            link(dve.tensor_tensor(coef[:, :, :], coef[:, :, :], wsum.unsqueeze(2).broadcast_to([P, B, E]), ALU.mult))
            link(dve.tensor_copy(chl[:, :, 0, :], coef[:, :, :]))
            dve.tensor_tensor(chl[:, :, 1, :], coef[:, :, :], chl[:, :, 0, :], ALU.subtract).then_inc(coef_ready, 1)
            dve.wait_ge(coefT_done, 1)
            dve.tensor_copy(cT[:, :], bank[7][:, :].bitcast(F16)).then_inc(coefT_ready, 1)

            def unit(it, k):
                n, pair, c = BODY * it + k, BODY // 2 * it + k // 2, k % 2
                shared = isinstance(it, int) and n < 2
                b4 = slice(4 * c, 4 * c + 4)
                dve.wait_ge(silu_done, n + 1)
                dve.wait_ge(up_done, n + 1)
                wait(dve, hlo_ready, n + (-1))
                dve.tensor_tensor(gu[:, b4, :], sg[:, b4, :], four(4 + c), ALU.mult).then_inc(gu_done, 1)
                if c == 0 and not (isinstance(it, int) and pair == 0) and (not isinstance(it, int) or pair < PAIRS):
                    low_gate_up(pair + 1, k // 2 + 1)
                if c == 1 and not (isinstance(it, int) and pair == 0):
                    wait(dve, down_done, n + (-3))
                    down_weights(pair, k // 2)
                dve.wait_ge(gu_done, n + 1)
                if shared:
                    dve.tensor_copy(hx[:, b4, :], gu[:, b4, :]).then_inc(h_done, 1)
                else:
                    dve.wait_ge(coefb_done, n + (-1))
                    dve.tensor_tensor(hx[:, b4, :], gu[:, b4, :], four(6 + c), ALU.mult).then_inc(h_done, 1)

            over_units(dve, unit, UNITS)

        @block.gpsimd
        def _(pool):
            for t in (xnT, qin, kin):
                pool.memset(t[:, :, 0:1], 0.0).then_inc(pads_ready, 1)
                pool.memset(t[:, :, P + 1:P + 2], 0.0).then_inc(pads_ready, 1)
            pool.memset(kbd[:, :, :, :, :].bitcast(F32), 0.0).then_inc(rows_ready, 1)
            pool.memset(pick[:, :, :, :].bitcast(F32), 0.0).then_inc(rows_ready, 1)
            for v in vs:
                pool.memset(v[:, :, :, DK:DK + 1], 1.0).then_inc(ones_ready, 1)
            pool.memset(negmax[:, :, :], 0.0).then_inc(ones_ready, 1)
            pool.memset(qbd[:, :, :, :, :].bitcast(F32), 0.0).then_inc(rows_ready, 1)
            pool.memset(low[:, :, :], 0.0).then_inc(ones_ready, 1)
            pool.wait_ge(ones_ready, 4)
            for g in range(1, GE):
                pool.memset(low[:, g, 0:g], 1.0).then_inc(ones_ready, 1)
            for n in range(2):
                for c in range(2):
                    pool.wait_ge(k_ready, 2 * n + c + 1)
                    pool.wait_ge(khi_ready, 2 * n + c + 1)
                    b4 = slice(4 * c, 4 * c + 4)
                    pool.tensor_tensor(khl[n][:, 1, b4, :], kc[n][:, b4, :], khl[n][:, 0, b4, :].bitcast(F32),
                                       ALU.subtract).then_inc(klo_ready, 1)
            pool.wait_ge(ld_a, 16)
            pool.wait_ge(pv_done, G * STEPS)
            pool.tensor_tensor(i2[:, :], ident[:, 0:E], ident[:, E:2 * E], ALU.add).then_inc(pool_step, 1)
            pool.wait_ge(pool_step, 1)
            pool.tensor_copy(sel[:, :, :], i2[:, :].unsqueeze(2).broadcast_to([P, E, I])).then_inc(sel_ready, 1)

            def unit(it, k):
                c = k % 2
                pool.wait_ge(hhi_ready, BODY * it + (k + 1))
                pool.tensor_tensor(hlo[:, k % 4, :].rearrange("p (b t) -> p b t", b=4), hx[:, 4 * c:4 * c + 4, :],
                                   hhi[:, k % 4, :].bitcast(F32).rearrange("p (b t) -> p b t", b=4),
                                   ALU.subtract).then_inc(hlo_ready, 1)

            over_units(pool, unit, UNITS)


def kernel(**inputs):
    import numpy as np
    import concourse.bacc as bacc
    from concourse.bass_utils import run_bass_kernel_spmd

    a = {k: np.asarray(v) for k, v in inputs.items()}
    att = lambda n: a["L0_attn_" + n]
    xat = lambda n: a["L0_xattn_" + n]
    ffn = lambda n: a["L0_ffn_" + n]
    col = lambda v: v.reshape(P, 1)
    row = lambda v: np.broadcast_to(v.reshape(1, -1), (P, v.size))
    taps = lambda w: w.transpose(0, 2, 1).reshape(P, 3 * P)
    second = lambda w: w.reshape(H, P, 2).transpose(1, 2, 0).reshape(P, 2 * H)
    part_a = dict(
        ident=np.eye(P, dtype=np.float32),
        ones_rows=col(np.float32(np.arange(P) % 32 < 2)), wqT=att("Wq_w").T, wkT=att("Wk_w").T, wvT=att("Wv_w").T,
        cq=taps(att("convq_w")), ck=taps(att("convk_w")),
        qp1T=att("qproj_w")[:, :P].T, qp2T=att("qproj_w")[:, P:].T,
        kp1T=att("kproj_w")[:, :P].T, kp2T=att("kproj_w")[:, P:].T,
        tau1=att("tau1_w").reshape(P, 6), tau1b=att("tau1_b").reshape(P, 2),
        del1=att("del1_w").reshape(P, 6), del1b=att("del1_b").reshape(P, 2),
        tau2T=second(att("tau2_w")), del2T=second(att("del2_w")),
        bq=col(att("Wq_b")), bk=col(att("Wk_b")), cqb=col(att("convq_b")), ckb=col(att("convk_b")),
        qpb=col(att("qproj_b")), kpb=col(att("kproj_b")),
        tau2b=col(np.broadcast_to(att("tau2_b").reshape(H, 1), (H, DK))),
        woT=att("out_w").T, bv=row(att("Wv_b")), bo=row(att("out_b")), del2b=row(att("del2_b")))
    part_b = dict(wq=xat("Wq"), wk=xat("Wk"), wv=xat("Wv"), wo=xat("Wo"), bq=col(xat("bq")), bk=col(xat("bk")),
                  bv=row(xat("bv")), bo=row(xat("bo")), routerT=ffn("router_w").T, e_bias=row(ffn("e_bias")))
    gate = np.concatenate([ffn("SWg").reshape(P, 1, P), ffn("Wg").transpose(1, 0, 2).reshape(P, PAIRS, P)], 1)
    up = np.concatenate([ffn("SWu").reshape(P, 1, P), ffn("Wu").transpose(1, 0, 2).reshape(P, PAIRS, P)], 1)
    down = np.concatenate([ffn("SWd").reshape(P, 1, P), ffn("Wd").reshape(PAIRS, P, P).transpose(1, 0, 2)], 1)
    arrays = {
        "x": a["x"].reshape(T, P),
        "ctxT": a["ctx_1024"].reshape(T, P).T,
        "mask": a["mask_Bx1xSxS2_bk1"].reshape(B, P, P),
        "pack_a": np.concatenate([part_a[n] for n in PACK_A], axis=1),
        "pack_b": np.concatenate([part_b[n] for n in PACK_B], axis=1),
        "w3": np.stack([gate, up, down], axis=2).reshape(P, (PAIRS + 1) * 3 * P),
    }
    arrays = {k: np.ascontiguousarray(v) for k, v in arrays.items()}
    nc = bacc.Bacc("TRN2", target_bir_lowering=False, num_devices=1)
    args = [nc.dram_tensor(k, v.shape, mybir.dt.from_np(v.dtype), kind="ExternalInput").ap() for k, v in arrays.items()]
    outT = nc.dram_tensor("outT", (P, T), F32, kind="ExternalOutput").ap()
    decoder_layer(nc, *args, outT)
    r = run_bass_kernel_spmd(nc, [arrays], core_ids=[0])
    return np.ascontiguousarray(np.asarray(r.results[0]["outT"]).T).reshape(B, P, P)
```

```python
from contextlib import ExitStack

import concourse.bass as bass
from concourse import mybir

F32 = mybir.dt.float32
F32R = mybir.dt.float32r
F16 = mybir.dt.float16
BF16 = mybir.dt.bfloat16
I32 = mybir.dt.int32
U8 = mybir.dt.uint8
ALU = mybir.AluOpType
ACT = mybir.ActivationFunctionType
AX = mybir.AxisListType

P = 128
B = 8
T = B * P
H, DK = 16, 8
G = 4
J = H // G
HALF = T // 2
E, I = 64, 64
PAIRS = E * I // P
GE = 8
TOP_GROUPS, TOP_K = 4, 8
ROUTE_SCALE = 2.5
EPS = 1e-5
STEPS = 2 * B
S_HI, S_MID, S_LO = 2, 2 + DK, 2 + 2 * DK
PER_HALF = PAIRS + 1
UNITS = 2 * PER_HALF
LAG = 3
RING = 8
ROWS = 4
FIRST = RING - ROWS
BODY = 8
LOOPS = ((8, 3), (40, 3))
SCALE = DK ** -0.5
MASKED = -1e15 / SCALE
TAKEN = -3e38
RSQRT_MAGIC = 1597463007.0

PACK_A = dict(ident=P, woT=P, ones_rows=1, wqT=P, wkT=P, wvT=P, cq=3 * P, ck=3 * P, qp1T=P, qp2T=P, kp1T=P, kp2T=P,
              tau1=6, tau1b=2, del1=6, del1b=2, tau2T=32, del2T=32,
              bq=1, bk=1, cqb=1, ckb=1, qpb=1, kpb=1, tau2b=1, bv=P, bo=P, del2b=H)
PACK_B = dict(wq=P, wk=P, wv=P, wo=P, bq=1, bk=1, bv=P, bo=P, routerT=E, e_bias=E)


def columns(pack):
    at, out = 0, {}
    for name, n in pack.items():
        out[name] = (at, at + n)
        at += n
    return out, at


def decoder_layer(nc, x, ctxT, mask, pack_a, pack_b, w3, rowsd, outT):
    cols_a, n_a = columns(PACK_A)
    cols_b, n_b = columns(PACK_B)

    with ExitStack() as ctx:
        def sb(name, shape, dt=F32):
            return ctx.enter_context(nc.sbuf_tensor(name, shape, dt))

        def sem(name):
            return ctx.enter_context(nc.semaphore(name))

        bank = [ctx.enter_context(nc.psum_tensor(f"bank{i}", [P, 512], F32)) for i in range(8)]

        kept = cols_a["ones_rows"][1]
        SPREAD = 2 * FIRST - 2
        pa = sb("pa", [P, max(n_a, kept + SPREAD * I // 2)])
        pb = sb("pb", [P, n_b])
        A = lambda name: pa[:, cols_a[name][0]:cols_a[name][1]]
        Bw = lambda name: pb[:, cols_b[name][0]:cols_b[name][1]]
        ident = A("ident")
        ring = sb("ring", [P, RING, 3, P])
        xres = sb("xres", [P, B, P])
        xnT = sb("xnT", [P, B, P + 2])
        qin = sb("qin", [P, B, P + 2])
        kin = sb("kin", [P, B, P + 2])
        ctxs = sb("ctxs", [P, B, P])
        xn = sb("xn", [P, B, P])
        masku = sb("masku", [P, B, P], U8)
        maskb = sb("maskb", [P, B, P], BF16)
        identb = sb("identb", [P, P], BF16)
        identr = sb("identr", [P, P], F32R)
        warm = sb("warm", [P, 1])
        stats = sb("stats", [P, B, 6])
        mv = sb("mv", [P, B, 2])
        nwt = sb("nwt", [P, 4, B])
        oT = sb("oT", [P, G, P])
        foldq = oT[:, 0:3, :]
        foldk = sb("foldk", [P, 3, P])
        foldb = sb("foldb", [P, 2])
        conv = sb("conv", [P, 4, B, P])
        probs = conv[:, :, :, :].rearrange("p a b t -> p (a b t)").rearrange("p (i j t) -> p i j t", i=8, j=J)
        tau2r = sb("tau2r", [P, 2, H, DK])
        edelta = sb("edelta", [P, B, H])
        qc = sb("qc", [P, B, P])
        kc = [qin[:, :, 1:1 + P], kin[:, :, 1:1 + P]]
        tauT = sb("tauT", [P, B, P])
        qhl = sb("qhl", [P, 2, B, P], F32R)
        khl = [sb(f"khl{n}", [P, 2, B, P], F32R) for n in range(2)]
        pick = sb("pick", [P, 4, G, P], F32R)
        qst = sb("qst", [P, G, B, P], F32R)
        kst = [sb(f"kst{n}", [P, G, B, P], F32R) for n in range(2)]
        kbd = sb("kbd", [P, 2, G, J, P], F32R)
        qbd = sb("qbd", [P, 2, G, J, P], F32R)
        vs = [sb(f"vs{n}", [P, B, H, DK + 1]) for n in range(2)]
        rawmax = sb("rawmax", [P, 2, G, J])
        negmax = sb("negmax", [P, G, P])
        on = sb("on", [P, H, DK])
        rec = sb("rec", [P, H])
        onT = sb("onT", [P, P])
        xhl = khl[1][:, :, :, :].rearrange("p a b t -> p a (b t)")

        flat_tau, flat_q = (t[:, :, :].rearrange("p b t -> p (b t)") for t in (tauT, qc))
        flat_k = kin[:, :, :].rearrange("p b t -> p (b t)")
        HB, HE = B // 2, B // 2 * E
        sc = flat_tau[:, 0:2 * HE].rearrange("p (b e) -> p b e", b=B)
        masked, replaced = (flat_tau[:, HE * i:HE * i + HE].rearrange("p (b e) -> p b e", b=HB) for i in (2, 3))
        gcmp = flat_q[:, 0:3 * HE].rearrange("p (i b g f) -> p i b g f", i=3, b=HB, g=GE)
        coef = flat_q[:, 3 * HE:4 * HE].rearrange("p (b e) -> p b e", b=HB)
        sfc = flat_k[:, 0:HE].rearrange("p (b g e) -> p b g e", b=HB, g=GE)
        low = sb("low", [P, GE, GE])
        top8 = sb("top8", [P, B, 8])
        halves = conv[:, :, :, :].rearrange("p a b t -> p (a b t)").bitcast(F16)
        chl = halves[:, 2 * T:2 * T + HALF].rearrange("p (b a e) -> p b a e", b=HB, a=2)
        identh = sb("identh", [P, P], F16)
        cT = halves[:, 3 * T:3 * T + HALF]
        sel = pa[:, kept:kept + SPREAD * I // 2].bitcast(F16).rearrange("p (e i) -> p e i", e=SPREAD)
        spread = conv[:, 2:4, :, :].rearrange("p a b t -> p (a b) t").rearrange("p (u b) t -> p u b t", u=ROWS)
        coef_rows = ctxs[0:E, :, :].rearrange("p b t -> p (b t)").rearrange("p (c t) -> p c t", c=2)
        i2 = sb("i2", [P, E])
        parts = kst[0][:, :, :, :].rearrange("p g b t -> p (g b) t")
        whigu, wlogu = (parts[:, 8 * i:8 * i + 8, :].rearrange("p (k m) c -> p k m c", k=4) for i in range(2))
        whid, wlod = (parts[:, 16 + 4 * i:20 + 4 * i, :] for i in range(2))
        sg = qin[:, :, 0:P]
        gu = conv[:, 0, :, :]
        hx = [vs[i // 2][:, :, :, :].rearrange("p b h d -> p (b h d)")[:, HALF * (i % 2):HALF * (i % 2) + HALF]
              .rearrange("p (b t) -> p b t", b=4) for i in range(4)]
        outs = qc[:, :, :].rearrange("p (c b) t -> p c (b t)", c=2)
        hhi = qbd[:, 0, :, :, :].rearrange("p g j t -> p g (j t)")
        hlo = qbd[:, 1, :, :, :].rearrange("p g j t -> p g (j t)")

        ld_x, ld_a, ld_b, ld_ctx, ld_mask = (sem(f"ld_{n}") for n in ("x", "a", "b", "ctx", "mask"))
        ld_w = [sem(f"ld_w{i}") for i in range(RING)]
        dve_step = sem("dve_step")
        pool_step = sem("pool_step")
        warmed = sem("warmed")
        pads_ready = sem("pads_ready")
        xn_ready = sem("xn_ready")
        stats_ready = sem("stats_ready")
        bias_added = sem("bias_added")
        xT_done = sem("xT_done")
        xT_copied = sem("xT_copied")
        folded = sem("folded")
        fold_copied = sem("fold_copied")
        in_done = sem("in_done")
        in_copied = sem("in_copied")
        v_done = sem("v_done")
        v_copied = sem("v_copied")
        conv_part = sem("conv_part")
        conv_done = sem("conv_done")
        gelu_done = sem("gelu_done")
        tau_done = sem("tau_done")
        tau_ready = sem("tau_ready")
        delta_done = sem("delta_done")
        delta_sum = sem("delta_sum")
        delta_ready = sem("delta_ready")
        q_done = sem("q_done")
        q_ready = sem("q_ready")
        k_done = sem("k_done")
        k2_done = sem("k2_done")
        khi_ready = sem("khi_ready")
        klo_ready = sem("klo_ready")
        qhi_ready = sem("qhi_ready")
        qlo_ready = sem("qlo_ready")
        q_stacked = sem("q_stacked")
        k_stacked = sem("k_stacked")
        qst_ready = sem("qst_ready")
        qst_odd = sem("qst_odd")
        kst_ready = sem("kst_ready")
        kbd_ready = [sem(f"kbd_ready{i}") for i in range(2)]
        picks_ready = sem("picks_ready")
        kbd_first_high = sem("kbd_first_high")
        kbd_first = sem("kbd_first")
        mask_ready = sem("mask_ready")
        const_ready = sem("const_ready")
        (scored, maxed, max_split, max_turned, qbd_high, qbd_ready, scoredT, exped, pv_done, o_copied, o_turned, normed,
         on_turned, on_copied, projected, residual) = (sem(n) for n in (
             "scored", "maxed", "max_split", "max_turned", "qbd_high", "qbd_ready", "scoredT", "exped", "pv_done", "o_copied",
             "o_turned", "normed", "on_turned", "on_copied", "projected", "residual"))
        logits_done = sem("logits_done")
        scores_ready = sem("scores_ready")
        coef_ready = sem("coef_ready")
        rows_stored = sem("rows_stored")
        chl_ready = sem("chl_ready")
        rowsT_done = sem("rowsT_done")
        rowsT_copied = sem("rowsT_copied")
        ld_c = [sem(f"ld_c{i}") for i in range(ROWS)]
        coefT_done = sem("coefT_done")
        coefT_ready = sem("coefT_ready")
        xhi_ready = sem("xhi_ready")
        xlo_ready = sem("xlo_ready")
        x3T_ready = sem("x3T_ready")
        whigu_ready = sem("whigu_ready")
        wlogu_ready = sem("wlogu_ready")
        whid_ready = sem("whid_ready")
        wlod_ready = sem("wlod_ready")
        rows_ready = sem("rows_ready")
        ones_ready = sem("ones_ready")
        sel_ready = sem("sel_ready")
        bank4_zeroed = sem("bank4_zeroed")
        values_scaled = sem("values_scaled")
        coefb_done = sem("coefb_done")
        gate_done = sem("gate_done")
        up_done = sem("up_done")
        silu_done = sem("silu_done")
        gu_done = sem("gu_done")
        h_done = sem("h_done")
        hhi_ready = sem("hhi_ready")
        hlo_ready = sem("hlo_ready")
        down_done = sem("down_done")
        last_wlod = sem("last_wlod")
        last_hlo = sem("last_hlo")
        out_copied = sem("out_copied")
        stored = sem("stored")

        block = ctx.enter_context(nc.Block())

        def chain(eng, step):
            count = [0]

            def link(ins):
                ins.then_inc(step, 1)
                count[0] += 1
                eng.wait_ge(step, count[0])
            return link, count

        def normalise(eng, link, n, lo, hi, fused):
            v, y, a, vh = (nwt[:, i, lo:hi] for i in range(4))
            eng.wait_ge(stats_ready, B * n + hi)
            link(eng.tensor_scalar(v, mv[:, lo:hi, 1], EPS, None, ALU.add))
            link(eng.tensor_scalar(vh, v, -0.5, None, ALU.mult))
            link(eng.tensor_scalar(y.bitcast(I32), v.bitcast(I32), -0.5, RSQRT_MAGIC, ALU.mult, ALU.add))
            for _ in range(3):
                link(eng.tensor_tensor(a, vh, y, ALU.mult))
                link(eng.tensor_tensor(a, a, y, ALU.mult))
                if fused:
                    link(eng.scalar_tensor_tensor(out=y, in0=a, scalar=1.5, in1=y, op0=ALU.add, op1=ALU.mult))
                else:
                    link(eng.tensor_scalar(a, a, 1.5, None, ALU.add))
                    link(eng.tensor_tensor(y, y, a, ALU.mult))
            if n > 0:
                eng.wait_ge(xT_done, 2 * n - 1 + lo // 4)
            for b in range(lo, hi):
                eng.tensor_scalar(xn[:, b, :], xres[:, b, :], mv[:, b, 0:1], nwt[:, 1, b:b + 1],
                                  ALU.subtract, ALU.mult).then_inc(xn_ready, 1)

        def add_bias(eng, bias, lo, hi, done):
            eng.wait_ge(xn_ready, done)
            eng.tensor_tensor(xres[:, lo:hi, :], xres[:, lo:hi, :],
                              bias.unsqueeze(1).broadcast_to([P, hi - lo, P]), ALU.add).then_inc(bias_added, 1)

        def wait(eng, signal, value):
            if not isinstance(value, int) or value > 0:
                eng.wait_ge(signal, value)

        LATER = [(what, 0, 1, g) for g in range(G) for what in "qk"] + [("k", 1, c, g) for c in range(2) for g in range(G)]
        LATER[8:8], LATER[11:11] = [("v", 1, 0, 0)], [("v", 1, 1, 0)]
        PLACES = [(0, 0), (0, 1), (0, 2), (0, 3), (1, 0), (1, 1), (1, 2), (1, 3), (2, 0), (2, 1), (2, 3),
                  (3, 0), (3, 1), (3, 3), (4, 0), (4, 3), (5, 0), (5, 3)]

        def loaded(it, k):
            return 16 * it + (16 * (k // RING) + 16)

        def spread_in(it, k):
            before = k // ROWS - 1 - (1 if k > PER_HALF and k % ROWS == PER_HALF % ROWS else 0)
            return 16 * (BODY // ROWS) * it + (16 * before + 16)

        def over_units(eng, body, last, first=0):
            n = first
            for start, trips in LOOPS:
                if n <= start:
                    for k in range(n, start):
                        body(0, k)
                    with eng.Fori(0, trips) as it:
                        for k in range(start, start + BODY):
                            body(it, k)
                    n = start + BODY * trips
            for k in range(n, last):
                body(0, k)

        @block.sync
        def _(sp):
            sp.dma_start(xres[:, :, :], x.rearrange("(b p) d -> p b d", p=P)).then_inc(ld_x, 16)
            sp.dma_start(pa[:, 0:n_a], pack_a).then_inc(ld_a, 16)
            sp.dma_start(ctxs[:, :, :], ctxT.rearrange("p (b t) -> p b t", b=B)).then_inc(ld_ctx, 16)
            sp.dma_start(pb[:, :], pack_b).then_inc(ld_b, 16)
            sp.dma_start(masku[:, :, :], mask.rearrange("b q k -> q b k")).then_inc(ld_mask, 16)
            w3v = w3.rearrange("p (n m c) -> p n m c", m=3, c=P)
            for pair in range(RING):
                sp.dma_start(ring[:, pair, :, :], w3v[:, pair, :, :]).then_inc(ld_w[pair], 16)

            sp.wait_ge(rows_ready, 3)
            for s in range(1, STEPS):
                n, b = s // B, s % B
                sp.wait_ge(kst_ready, G * (2 * n + b // 4 + 1))
                wait(sp, scored, G * (s - 1))
                for j in range(J):
                    sp.dma_start(kbd[32 * j:32 * j + 32, s % 2, :, j, :].bitcast(F32),
                                 kst[n][32 * j:32 * j + 32, :, b, :].bitcast(F32)).then_inc(kbd_ready[s % 2], 16)

            def load(it, k):
                n, pair = BODY * it + k, BODY * it + k % PER_HALF
                if not isinstance(it, int) or n < UNITS:
                    sp.wait_ge(wlogu_ready, n + (1 - RING))
                    sp.wait_ge(wlod_ready, n + (1 - RING))
                    src = w3v[:, pair, :, :] if isinstance(it, int) else w3v[:, bass.ds(pair, 1), :, :]\
                        .rearrange("p o m c -> p (o m) c")
                    sp.dma_start(ring[:, k % RING, :, :], src).then_inc(ld_w[k % RING], 16)
                kc = k - ROWS
                c = kc // PER_HALF
                if kc == PER_HALF + 1:
                    rows_out(1)
                if kc != PER_HALF:
                    sp.wait_ge(h_done, BODY * it + (kc + 1 - ROWS))
                    e0 = 2 * BODY * it + (2 * (kc - PER_HALF * c) - 2)
                    src = rowsd[c, bass.ds(e0, 2), :] if not isinstance(it, int) else rowsd[c, e0:e0 + 2, :]
                    sp.dma_start(spread[:, kc % ROWS, :, :].rearrange("p b t -> p (b t)"),
                                 src.unsqueeze(1).broadcast_to([2, I, HALF])).then_inc(ld_c[kc % ROWS], 16)

            def rows_out(c):
                sp.wait_ge(rowsT_copied, c + 1)
                sp.dma_start(rowsd[c, :, :], coef_rows[:, c, :]).then_inc(rows_stored, 16)
                sp.wait_ge(rows_stored, 16 * (c + 1))

            rows_out(0)
            over_units(sp, load, UNITS + ROWS, RING)
            for c in range(2):
                sp.wait_ge(out_copied, c + 1)
                sp.dma_start(outT[:, HALF * c:HALF * c + HALF], outs[:, c, :]).then_inc(stored, 16)
            sp.wait_ge(stored, 32)

        @block.tensor
        def _(pe):
            def half(t, c, shift=1):
                return t[:, 4 * c:4 * c + 4, shift:shift + P]

            def mm(out, lhsT, rhs, start=True, stop=True):
                return pe.matmul(out, lhsT, rhs, start=start, stop=stop)

            def turn_inputs(n, c, out):
                for b in range(4 * c, 4 * c + 4):
                    pe.wait_ge(xn_ready, B * n + b + 1)
                    last = pe.transpose(out[:, P * (b % 4):P * (b % 4) + P], xn[:, b, :], ident)
                last.then_inc(xT_done, 1)

            def stack(out, m, hl, c, g, signal):
                mm(out[:, :], pick[:, m, g, :], hl[:, 0, 4 * c:4 * c + 4, :], True, False)
                mm(out[:, :], pick[:, m + 1, g, :], hl[:, 1, 4 * c:4 * c + 4, :], False, True).then_inc(signal, 1)

            pe.wait_ge(ld_a, 16)
            for n, (conv_w, proj, bias) in enumerate((("cq", "qp2T", "cqb"), ("ck", "kp2T", "ckb"))):
                for k in range(3):
                    c0 = cols_a[conv_w][0] + P * k
                    mm(bank[2 + n][:, P * k:P * k + P], pa[:, c0:c0 + P], A(proj))
                mm(bank[4][:, n:n + 1], A(proj), A(bias)).then_inc(folded, 1)
            for c in range(2):
                turn_inputs(0, c, bank[c])
            pe.wait_ge(ld_ctx, 16)
            pe.wait_ge(ld_b, 16)
            pe.wait_ge(pads_ready, 6)
            for c in range(2):
                pe.wait_ge(xT_copied, c + 1)
                mm(bank[5 + c][:, :], A("wqT"), half(xnT, c)).then_inc(in_done, 1)
            for c in range(2):
                mm(bank[7 - 7 * c][:, :], A("wkT"), half(xnT, c)).then_inc(in_done, 1)
            pe.wait_ge(fold_copied, 4)
            pe.wait_ge(in_copied, 2)
            for c in range(2):
                for k in range(3):
                    last = mm(bank[5 + c][:, :], foldq[:, k, :], half(qin, c, k), k == 0, k == 2)
                last.then_inc(q_done, 1)
            pe.wait_ge(gelu_done, 2)
            pe.wait_ge(const_ready, 1)
            for c in range(2):
                for r in range(2):
                    last = mm(bank[3 + c][:, :], tau2r[:, r, :, :], conv[:, r, 4 * c:4 * c + 4, :], r == 0, r == 1)
                last.then_inc(tau_done, 1)
            pe.wait_ge(in_copied, 4)
            for c in range(2):
                for k in range(3):
                    last = mm(bank[7 - 7 * c][:, :], foldk[:, k, :], half(kin, c, k), k == 0, k == 2)
                last.then_inc(k_done, 1)
            for c in range(2):
                mm(bank[1 + c][:, :], Bw("wk"), ctxs[:, 4 * c:4 * c + 4, :]).then_inc(k2_done, 1)
            def values(n, c, out):
                for b in range(4 * c, 4 * c + 4):
                    last = mm(out[:, P * (b % 4):P * (b % 4) + P], xnT[:, b, 1:1 + P] if n == 0 else ctxs[:, b, :],
                              A("wvT") if n == 0 else Bw("wv"))
                last.then_inc(v_done, 1)

            pe.wait_ge(picks_ready, 1)
            pe.wait_ge(q_ready, 2)
            pe.wait_ge(khi_ready, 2)
            pe.wait_ge(qlo_ready, 1)
            pe.wait_ge(klo_ready, 2)
            for g in range(G):
                wait(pe, qst_ready, g - 1)
                stack(bank[5 + g % 2], 0, qhl, 0, g, q_stacked)
                wait(pe, kst_ready, g - 1)
                stack(bank[7 - 7 * (g % 2)], 2, khl[0], 0, g, k_stacked)
            pe.wait_ge(tau_ready, 2)
            pe.wait_ge(gelu_done, 4)
            d0 = cols_a["del2T"][0]
            for b in range(B):
                for r in range(2):
                    last = mm(bank[3][:, H * b:H * b + H], conv[:, 2 + r, b, :], pa[:, d0 + H * r:d0 + H * r + H],
                              r == 0, r == 1)
            last.then_inc(delta_done, 1)

            def later_stack(what, n, c, g):
                i = LATER.index((what, n, c, g))
                if i == 0:
                    pe.wait_ge(qlo_ready, 2)
                    pe.wait_ge(klo_ready, 4)
                else:
                    what_, n_, c_, g_ = LATER[i - 1]
                    if what_ == "v":
                        pe.wait_ge(v_copied, 2 * n_ + c_ + 1)
                    else:
                        pe.wait_ge(qst_ready if what_ == "q" else kst_ready, G * (2 * n_ + c_) + g_ + 1)
                if what == "v":
                    values(n, c, bank[7])
                elif what == "q":
                    stack(bank[7], 0, qhl, c, g, q_stacked)
                else:
                    stack(bank[7], 2, khl[n], c, g, k_stacked)

            def later(s, place):
                if (s, place) in PLACES:
                    later_stack(*LATER[PLACES.index((s, place))])

            def scores(s, g):
                n, b = s // B, s % B
                i = G * s + g
                if g == 0 and s == 0:
                    pe.wait_ge(kbd_first_high, 1)
                    pe.wait_ge(kbd_first, 1)
                elif g == 0:
                    pe.wait_ge(kbd_ready[s % 2], 16 * J * ((s + 1) // 2))
                    if n == 0:
                        pe.wait_ge(qst_ready, G * (b // 4 + 1))
                if n == 1 and b % 4 == 0:
                    pe.wait_ge(qst_odd if g % 2 else qst_ready, (0 if g % 2 else 2 * G) + 2 * (b // 4) + g // 2 + 1)
                wait(pe, maxed, i - 1)
                out = bank[i % 2]
                if n == 1:
                    pe.matmul(out[:, :].rearrange("p (g k) -> p g k", g=J), identb[:, :],
                              maskb[:, b, :].unsqueeze(1).broadcast_to([P, J, P]), start=True, stop=False)
                mm(out[:, :], qst[:, g, b, :], kbd[:, s % 2, g, :, :], n == 0, True).then_inc(scored, 1)

            def turn_max(s):
                wait(pe, qbd_high, s)
                wait(pe, qbd_ready, s)
                wait(pe, qst_odd, {8: 2, 12: 4}.get(s, 0))
                pe.matmul(bank[5][:, :], identr[:, :], qst[:, :, s % B, :], start=True, stop=False,
                          skip_group_check=True)
                pe.wait_ge(max_split, s + 1)
                for g in range(G):
                    last = pe.matmul(bank[5][:, P * g:P * g + P], negmax[:, g, :], ident, start=False,
                                     stop=(g == G - 1), skip_group_check=True)
                last.then_inc(max_turned, 1)

            def scoresT(s, g):
                n, b = s // B, s % B
                i = G * s + g
                if g == 0:
                    pe.wait_ge(qbd_high, s + 1)
                    pe.wait_ge(qbd_ready, s + 1)
                wait(pe, exped, i - 1)
                out = bank[2 + i % 2]
                if n == 1:
                    pe.matmul(out[:, :].rearrange("p (g q) -> p g q", g=J), maskb[:, b, :],
                              identb[:, :].unsqueeze(1).broadcast_to([P, J, P]), start=True, stop=False)
                mm(out[:, :], kst[n][:, g, b, :], qbd[:, s % 2, g, :, :], n == 0, True).then_inc(scoredT, 1)

            def pv(s, g):
                i = G * s + g
                pe.wait_ge(exped, i + 1)
                if g == 0:
                    wait(pe, o_copied, s)
                for j in range(J):
                    last = mm(bank[4][32 * j:32 * j + DK + 1, P * g:P * g + P], vs[s // B][:, s % B, J * g + j, :],
                              probs[:, i % 8, j, :])
                last.then_inc(pv_done, 1)

            def turn_out(s):
                pe.wait_ge(o_copied, s + 1)
                wait(pe, residual, s)
                for g in range(G):
                    last = pe.transpose(bank[6][:, P * g:P * g + P], oT[:, g, :], ident)
                last.then_inc(o_turned, 1)

            def turn_on(s):
                pe.wait_ge(normed, s + 1)
                pe.transpose(bank[6][:, 0:P], on[:, :, :].rearrange("p h d -> p (h d)"), ident)\
                    .then_inc(on_turned, 1)

            def project(s):
                pe.wait_ge(on_copied, s + 1)
                mm(bank[6][:, P:2 * P], onT[:, :], A("woT") if s < B else Bw("wo")).then_inc(projected, 1)

            def second_inputs(c):
                pe.wait_ge(kst_ready, 4 * G)
                pe.wait_ge(qst_ready, 2 * G + 2 * c)
                turn_inputs(1, c, bank[7])

            def second_queries(c):
                pe.wait_ge(xT_copied, 3 + c)
                mm(bank[7][:, :], Bw("wq"), half(xnT, c)).then_inc(q_done, 1)

            def second_stack(c, g):
                pe.wait_ge(qlo_ready, 3 + c)
                if g == 2:
                    pe.wait_ge(qst_ready, 2 * G + 2 * c + 1)
                if g == 3:
                    pe.wait_ge(qst_odd, 2 * c + 1)
                stack(bank[7 - 2 * (g % 2)], 0, qhl, c, g, q_stacked)

            r0, r1 = cols_b["routerT"]
            def router_scores(c, out):
                pe.wait_ge(x3T_ready, c + 1)
                for b in range(4 * c, 4 * c + 4):
                    last = mm(out[:, E * (b % 4):E * (b % 4) + E], xnT[:, b, 1:1 + P], pb[:, r0:r1])
                last.then_inc(logits_done, 1)

            pe.wait_ge(kst_ready, G)
            pe.wait_ge(klo_ready, 3)
            pe.wait_ge(khi_ready, 3)
            scores(0, 0)
            scores(0, 1)
            pe.wait_ge(qst_ready, G)
            for c in range(2):
                values(0, c, bank[6 - 2 * c])
            scores(0, 2)
            scores(0, 3)
            for s in range(STEPS + 1):
                now, ahead = s < STEPS, s + 1 < STEPS
                inputs, making = {6: 0, 10: 1}.get(s), {7: 0, 11: 1}.get(s)
                early = ahead and making is None
                if early:
                    scores(s + 1, 0)
                if now:
                    turn_max(s)
                if early:
                    scores(s + 1, 1)
                later(s, 0)
                if making is not None:
                    second_queries(making)
                if s == STEPS - 1:
                    pe.wait_ge(xhi_ready, 1)
                    router_scores(0, bank[7])
                if s >= 2 and now:
                    project(s - 2)
                if s == 0:
                    pe.wait_ge(klo_ready, 4)
                    pe.wait_ge(khi_ready, 4)
                    pe.wait_ge(delta_sum, 1)
                if s == 1:
                    pe.wait_ge(v_copied, 1)
                    pe.wait_ge(bank4_zeroed, 1)
                    pe.wait_ge(values_scaled, 1)
                if s == B - 2:
                    pe.wait_ge(mask_ready, 1)
                if s >= 1:
                    pv(s - 1, 0)
                    pv(s - 1, 1)
                    if early:
                        scores(s + 1, 2)
                    pv(s - 1, 2)
                    pv(s - 1, 3)
                    if not now:
                        project(s - 2)
                elif early:
                    scores(s + 1, 2)
                later(s, 1)
                if now:
                    scoresT(s, 0)
                    scoresT(s, 1)
                if early:
                    scores(s + 1, 3)
                if s >= 1 and making is None:
                    turn_out(s - 1)
                later(s, 2)
                if making is not None:
                    second_stack(making, 0)
                    second_stack(making, 1)
                if now:
                    scoresT(s, 2)
                if making is not None:
                    scores(s + 1, 0)
                    second_stack(making, 2)
                    scores(s + 1, 1)
                if now:
                    scoresT(s, 3)
                if making is not None:
                    second_stack(making, 3)
                if making is not None:
                    turn_out(s - 1)
                if making is not None:
                    scores(s + 1, 2)
                    scores(s + 1, 3)
                later(s, 3)
                if inputs is not None:
                    second_inputs(inputs)
                if s == STEPS - 2:
                    turn_inputs(2, 0, bank[7])
                if 1 <= s < STEPS:
                    turn_on(s - 1)

            def accumulate_residual(b):
                pe.wait_ge(residual, B + b + 1)
                pe.matmul(bank[b // 4][:, P * (b % 4):P * (b % 4) + P], xres[:, b, :], ident,
                          start=(b % 4 == 0), stop=False, skip_group_check=True)

            def products(it, k, of=(0, 1)):
                n, c, w, p = BODY * it + k, k // PER_HALF, k % 4, k % 2
                xh, xl = xhl[:, 0, HALF * c:HALF * c + HALF], xhl[:, 1, HALF * c:HALF * c + HALF]
                pe.wait_ge(wlogu_ready, n + 1)
                for m in of:
                    out, signal, used = ((bank[2 + p], gate_done, silu_done), (bank[4 + p], up_done, gu_done))[m]
                    wait(pe, used, n + (-1))
                    mm(out[:, :], whigu[:, w, m, :], xh, True, False)
                    mm(out[:, :], whigu[:, w, m, :], xl, False, False)
                    mm(out[:, :], wlogu[:, w, m, :], xh, False, True).then_inc(signal, 1)

            def turn_coefficients(c):
                pe.wait_ge(coef_ready, c + 1)
                for b in range(4):
                    last = pe.transpose(bank[6 - 5 * c][0:E, P * b:P * b + P], coef[:, b, :], ident)
                last.then_inc(rowsT_done, 1)

            def turn_parts():
                pe.wait_ge(chl_ready, 1)
                for b in range(4):
                    last = pe.transpose(bank[1][:, :].bitcast(F16)[:, P * b:P * b + P],
                                        chl[:, b, :, :].rearrange("p a e -> p (a e)"), identh[:, :])
                last.then_inc(coefT_done, 1)

            pe.wait_ge(xhi_ready, 1)
            pe.wait_ge(xlo_ready, 1)
            pe.wait_ge(exped, G * STEPS)
            pe.wait_ge(o_copied, STEPS)
            products(0, 0)
            turn_on(STEPS - 1)
            products(0, 1)
            project(STEPS - 1)
            pe.wait_ge(maxed, G * STEPS)
            for b in range(4):
                accumulate_residual(b)

            def unit(it, k):
                n, p = BODY * it + k, k % 2
                peeled = isinstance(it, int)
                if peeled and n == 1:
                    products(0, 2, of=(0,))
                    pe.wait_ge(residual, STEPS)
                    turn_coefficients(0)
                    turn_parts()
                    products(0, 2, of=(1,))
                if peeled and n == PER_HALF - 1:
                    pe.wait_ge(scores_ready, 2)
                    turn_coefficients(1)
                if peeled and n == PER_HALF:
                    pe.wait_ge(xlo_ready, 2)
                if not peeled or LAG <= n < UNITS:
                    products(it, k)
                if peeled and n == 1:
                    pe.wait_ge(coefT_ready, 1)
                    pe.wait_ge(sel_ready, 1)
                    pe.wait_ge(scores_ready, 1)
                if peeled and n == 2:
                    pe.wait_ge(rowsT_copied, 1)
                if peeled and n == PER_HALF + 1:
                    pe.wait_ge(rowsT_copied, 2)
                    for b in range(4, B):
                        accumulate_residual(b)
                if peeled and 1 <= n < FIRST:
                    wait(pe, h_done, n - 1)
                    pe.matmul(bank[6 + p][:, :], sel[:, 2 * n - 2:2 * n, :].rearrange("p e i -> p (e i)"),
                              cT, start=True, stop=True).then_inc(coefb_done, 1)
                if not peeled or n >= LAG:
                    kd = k - LAG
                    w = kd % 4
                    if peeled and kd >= UNITS - 2:
                        pe.wait_ge(last_wlod, kd - (UNITS - 3))
                    else:
                        pe.wait_ge(wlod_ready, BODY * it + (kd + 1))
                    if peeled and kd == UNITS - 1:
                        pe.wait_ge(last_hlo, 1)
                    else:
                        pe.wait_ge(hlo_ready, BODY * it + (kd + 1))
                    acc, stop = bank[kd // PER_HALF][:, :], peeled and kd % PER_HALF == PER_HALF - 1
                    pe.matmul(acc, whid[:, w, :], hhi[:, w, :], start=False, stop=False, skip_group_check=True)
                    pe.matmul(acc, whid[:, w, :], hlo[:, w, :], start=False, stop=False, skip_group_check=True)
                    pe.matmul(acc, wlod[:, w, :], hhi[:, w, :], start=False, stop=stop,
                              skip_group_check=True).then_inc(down_done, 1)
                if peeled and n == 4:
                    turn_inputs(2, 1, bank[1])
                if peeled and n == 6:
                    pe.wait_ge(xhi_ready, 2)
                    router_scores(1, bank[1])

            over_units(pe, unit, UNITS + LAG)

        @block.scalar
        def _(act):
            def half(t, c, shift=0):
                return t[:, 4 * c:4 * c + 4, shift:shift + P]

            def four(b):
                return bank[b][:, :].rearrange("p (b t) -> p b t", b=4)

            def copy_inputs(n, c, b):
                act.wait_ge(xT_done, 2 * n + c + 1)
                act.activation(half(xnT, c, 1), four(b), ACT.Copy).then_inc(xT_copied, 1)

            act.wait_ge(pads_ready, 6)
            act.activation(warm[:, :], xnT[:, 0, 0:1], ACT.Gelu).then_inc(warmed, 1)
            copy_inputs(0, 0, 0)
            copy_inputs(0, 1, 1)

            def first_taps(n, w, bias):
                for r in range(2):
                    w0, b0 = cols_a[w][0] + 3 * r, cols_a[bias][0] + r
                    act.activation(conv[:, 2 * n + r, :, :], xnT[:, :, 0:P], ACT.Identity,
                                   bias=pa[:, b0:b0 + 1], scale=pa[:, w0:w0 + 1]).then_inc(conv_part, 1)

            def gelu(n):
                for r in range(2):
                    act.wait_ge(conv_done, 2 * n + r + 1)
                    act.activation(conv[:, 2 * n + r, :, :], conv[:, 2 * n + r, :, :], ACT.Gelu).then_inc(gelu_done, 1)

            def biased(dst, n, bias, banks):
                for c in range(2):
                    act.wait_ge(in_done, 2 * n + c + 1)
                    act.activation(half(dst, c, 1), four(banks[c]), ACT.Identity, bias=A(bias)).then_inc(in_copied, 1)

            def high_keys(n, c, b, bias):
                act.activation(half(khl[n][:, 0, :, :], c), four(b), ACT.Identity, bias=bias).then_inc(khi_ready, 1)

            def stacked_keys(n, c, g, b=7):
                act.wait_ge(k_stacked, G * (2 * n + c) + g + 1)
                act.activation(half(kst[n][:, g, :, :], c), four(b), ACT.Identity,
                               bias=A("ones_rows")).then_inc(kst_ready, 1)

            act.wait_ge(ld_a, 16)
            act.wait_ge(xT_copied, 2)
            first_taps(0, "tau1", "tau1b")
            biased(qin, 0, "bq", (5, 6))
            first_taps(1, "del1", "del1b")
            biased(kin, 1, "bk", (7, 0))
            gelu(0)
            gelu(1)
            for c in range(2):
                act.wait_ge(tau_done, c + 1)
                act.activation(half(tauT, c), four(3 + c), ACT.Sigmoid, bias=A("tau2b")).then_inc(tau_ready, 1)

            def high_queries(c):
                act.wait_ge(q_ready, c + 1)
                act.activation(half(qhl[:, 0, :, :], c), half(qc, c), ACT.Copy).then_inc(qhi_ready, 1)

            act.wait_ge(k_done, 1)
            act.wait_ge(fold_copied, 4)
            high_keys(0, 0, 7, foldb[:, 1:2])
            high_queries(0)
            act.wait_ge(k_done, 2)
            high_keys(0, 1, 0, foldb[:, 1:2])
            act.wait_ge(ld_b, 16)
            for c in range(2):
                act.wait_ge(k2_done, c + 1)
                high_keys(1, c, 1 + c, Bw("bk"))
            for g in range(G):
                stacked_keys(0, 0, g, 7 - 7 * (g % 2))
            act.wait_ge(rows_ready, 3)
            act.wait_ge(kst_ready, G)
            for j in range(2):
                r = slice(32 * j, 32 * j + 32)
                last = act.activation(kbd[r, 0, :, j, :], kst[0][r, :, 0, :].bitcast(F32), ACT.Copy)
            last.then_inc(kbd_first_high, 1)
            high_queries(1)
            act.wait_ge(delta_sum, 1)
            act.activation(edelta[:, :, :], edelta[:, :, :], ACT.Sigmoid).then_inc(delta_ready, 1)
            act.wait_ge(delta_ready, 1)
            act.activation(edelta[:, :, :], edelta[:, :, :], ACT.Exp).then_inc(delta_ready, 1)

            def copy_o(s):
                act.wait_ge(pv_done, G * s + G)
                wait(act, o_turned, s)
                act.activation(oT[:, :, :].rearrange("p g t -> p (g t)"), bank[4][:, :], ACT.Copy)\
                    .then_inc(o_copied, 1)

            def copy_on(s):
                act.wait_ge(on_turned, s + 1)
                wait(act, projected, s)
                act.activation(onT[:, :], bank[6][:, 0:P], ACT.Copy).then_inc(on_copied, 1)

            def exponential(s, g):
                i = G * s + g
                act.wait_ge(scoredT, i + 1)
                wait(act, pv_done, i - 7)
                act.activation(probs[:, i % 8, :, :].rearrange("p j t -> p (j t)"), bank[2 + i % 2][:, :],
                               ACT.Exp, scale=SCALE).then_inc(exped, 1)

            def queries_with_max(s):
                act.wait_ge(max_turned, s + 1)
                wait(act, scoredT, G * (s - 1))
                for j in range(2):
                    r = slice(32 * j, 32 * j + 32)
                    last = act.activation(qbd[r, s % 2, :, j, :], bank[5][r, :].rearrange("p (g t) -> p g t", g=G),
                                          ACT.Copy)
                last.then_inc(qbd_high, 1)

            def expert_inputs(c, b):
                act.wait_ge(xT_done, 4 + c + 1)
                act.activation(half(xnT, c, 1), four(b), ACT.Copy).then_inc(x3T_ready, 1)
                act.activation(xhl[:, 0, HALF * c:HALF * c + HALF].rearrange("p (b t) -> p b t", b=4),
                               four(b), ACT.Copy).then_inc(xhi_ready, 1)

            def router_scores(c):
                act.wait_ge(logits_done, c + 1)
                act.activation(sc[:, 4 * c:4 * c + 4, :].rearrange("p b e -> p (b e)"), bank[7 - 6 * c][:, 0:HE],
                               ACT.Sigmoid).then_inc(scores_ready, 1)

            def high_gate_up(it, k):
                act.wait_ge(ld_w[k % RING], loaded(it, k))
                act.activation(whigu[:, k % 4, :, :], ring[:, k % RING, 0:2, :], ACT.Copy).then_inc(whigu_ready, 1)

            def high_down(it, k):
                act.wait_ge(ld_w[k % RING], loaded(it, k))
                act.activation(whid[:, k % 4, :], ring[:, k % RING, 2, :], ACT.Copy).then_inc(whid_ready, 1)

            def second_stacked(c, g):
                act.wait_ge(q_stacked, G * (2 + c) + g + 1)
                act.activation(half(qst[:, g, :, :], c), four(7), ACT.Copy).then_inc(qst_ready, 1)

            def later_stacked(what, n, c, g):
                if what == "q":
                    act.wait_ge(q_stacked, G * c + g + 1)
                    act.activation(half(qst[:, g, :, :], c), four(7), ACT.Copy).then_inc(qst_ready, 1)
                elif what == "k":
                    stacked_keys(n, c, g)

            def later(s, place):
                if (s, place) in PLACES:
                    later_stacked(*LATER[PLACES.index((s, place))])

            for s in range(STEPS + 1):
                inputs, making = {6: 0, 10: 1}.get(s), {7: 0, 11: 1}.get(s)
                if s < STEPS:
                    queries_with_max(s)
                later(s, 0)
                if making is not None:
                    act.wait_ge(q_done, 3 + making)
                    act.activation(half(qhl[:, 0, :, :], making), four(7), ACT.Identity, bias=Bw("bq"))\
                        .then_inc(qhi_ready, 1)
                if s == STEPS - 1:
                    act.wait_ge(logits_done, 1)
                    act.activation(sc[:, 0:HB, :], bank[7][:, 0:HE].rearrange("p (b e) -> p b e", b=HB), ACT.Exp,
                                   scale=-1.0).then_inc(scores_ready, 1)
                if s >= 1:
                    copy_o(s - 1)
                later(s, 1)
                if s < STEPS:
                    exponential(s, 0)
                    exponential(s, 1)
                later(s, 2)
                if making is not None:
                    second_stacked(making, 0)
                if s < STEPS:
                    exponential(s, 2)
                if making is not None:
                    second_stacked(making, 2)
                if s < STEPS:
                    exponential(s, 3)
                later(s, 3)
                if inputs is not None:
                    copy_inputs(1, inputs, 7)
                if s == STEPS - 2:
                    expert_inputs(0, 7)
                if s >= 1:
                    copy_on(s - 1)

            def unit(it, k):
                n, p = BODY * it + k, k % 2
                peeled = isinstance(it, int)
                act.wait_ge(gate_done, n + 1)
                wait(act, gu_done, n + (-1))
                act.activation(sg[:, 4 * p:4 * p + 4, :], four(2 + p), ACT.Silu).then_inc(silu_done, 1)
                if not peeled or 1 <= n < UNITS - 2:
                    wait(act, up_done, n + (-1))
                    high_gate_up(it, k + 2)
                if not peeled or n >= LAG:
                    wait(act, down_done, n + (-3))
                    high_down(it, k)
                if peeled and n == 1:
                    copy_rows(0, 6)
                    act.wait_ge(coefT_done, 1)
                    act.activation(cT, bank[1][:, :].bitcast(F16)[:, 0:HALF], ACT.Copy).then_inc(coefT_ready, 1)
                if not peeled or n > 0:
                    high_product(it, k - 1)
                if peeled and n == PER_HALF - 1:
                    copy_rows(1, 1)
                if peeled and n == 4:
                    expert_inputs(1, 1)
                if peeled and n == 6:
                    router_scores(1)
                if peeled and n == UNITS - 1:
                    high_product(it, k)

            def copy_rows(c, b):
                act.wait_ge(rowsT_done, c + 1)
                act.activation(coef_rows[:, c, :], bank[b][0:E, :], ACT.Copy).then_inc(rowsT_copied, 1)

            def high_product(it, k):
                act.wait_ge(h_done, BODY * it + (k + 1))
                wait(act, down_done, BODY * it + (k - 3))
                act.activation(hhi[:, k % 4, :].rearrange("p (b t) -> p b t", b=4), hx[k % 4],
                               ACT.Copy).then_inc(hhi_ready, 1)

            over_units(act, unit, UNITS)
            for c in range(2):
                act.wait_ge(down_done, PER_HALF * (c + 1))
                act.activation(outs[:, c, :], bank[c][:, :], ACT.Copy).then_inc(out_copied, 1)

        @block.vector
        def _(dve):
            link, steps = chain(dve, dve_step)

            def stats_of(b):
                link(dve.bn_stats(stats[:, b, :], xres[:, b, :]))
                dve.bn_aggr(mv[:, b, :], stats[:, b, :]).then_inc(stats_ready, 1)

            def half(t, c, shift=0):
                return t[:, 4 * c:4 * c + 4, shift:shift + P]

            def four(b):
                return bank[b][:, :].rearrange("p (b t) -> p b t", b=4)

            dve.wait_ge(ld_x, 16)
            for b in range(B):
                dve.bn_stats(stats[:, b, :], xres[:, b, :]).then_inc(dve_step, 1)
            steps[0] += B
            dve.wait_ge(dve_step, steps[0])
            for b in range(B):
                dve.bn_aggr(mv[:, b, :], stats[:, b, :]).then_inc(stats_ready, 1)
            normalise(dve, link, 0, 0, B, True)
            dve.wait_ge(ld_a, 16)
            t0 = cols_a["tau2T"][0]
            dve.tensor_copy(tau2r[:, :, :, :].rearrange("p r h d -> p (r h) d"),
                            pa[:, t0:t0 + 2 * H].unsqueeze(2).broadcast_to([P, 2 * H, DK])).then_inc(const_ready, 1)
            for n, (dst, proj) in enumerate(((foldq, "qp1T"), (foldk, "kp1T"))):
                dve.wait_ge(folded, n + 1)
                link(dve.tensor_copy(dst[:, :, :].rearrange("p k o -> p (k o)"), bank[2 + n][:, 0:3 * P]))
                dve.tensor_tensor(dst[:, 1, :], dst[:, 1, :], A(proj), ALU.add).then_inc(fold_copied, 1)
            for n, bias in enumerate(("qpb", "kpb")):
                dve.tensor_tensor(foldb[:, n:n + 1], bank[4][:, n:n + 1], A(bias), ALU.add).then_inc(fold_copied, 1)
            def later_taps(n, w):
                for r in range(2):
                    w0 = cols_a[w][0] + 3 * r
                    dve.wait_ge(conv_part, 2 * n + r + 1)
                    y = conv[:, 2 * n + r, :, :]
                    link(dve.scalar_tensor_tensor(out=y, in0=xnT[:, :, 1:1 + P], scalar=pa[:, w0 + 1:w0 + 2],
                                                  in1=y, op0=ALU.mult, op1=ALU.add))
                    dve.scalar_tensor_tensor(out=y, in0=xnT[:, :, 2:2 + P], scalar=pa[:, w0 + 2:w0 + 3],
                                             in1=y, op0=ALU.mult, op1=ALU.add).then_inc(conv_done, 1)

            dve.wait_ge(xT_copied, 2)
            later_taps(0, "tau1")
            later_taps(1, "del1")
            for m, at in ((0, S_HI), (0, S_LO), (1, S_MID), (2, S_HI), (2, S_MID), (3, S_LO)):
                rows = pick[:, m, :, :].rearrange("p g r -> p (g r)").rearrange("p (h r) -> p h r", h=H)
                dve.wait_ge(rows_ready, 3)
                last = dve.tensor_copy(rows[:, :, at:at + DK], ident.rearrange("p (h d) -> p h d", h=H))
            last.then_inc(picks_ready, 1)
            dve.tensor_copy(identh[:, :], ident).then_inc(dve_step, 1)
            dve.tensor_copy(identb[:, :], ident).then_inc(dve_step, 1)
            dve.tensor_copy(identr[:, :], ident).then_inc(dve_step, 1)
            steps[0] += 3

            def values(n, c, bias, b0):
                dve.wait_ge(v_done, 2 * n + c + 1)
                for b in range(4 * c, 4 * c + 4):
                    last = dve.tensor_tensor(
                        vs[n][:, b, :, 0:DK],
                        bank[b0][:, P * (b % 4):P * (b % 4) + P].rearrange("p (h d) -> p h d", h=H),
                        bias.rearrange("p (h d) -> p h d", h=H), ALU.add)
                last.then_inc(v_copied, 1)

            for c in range(2):
                dve.wait_ge(q_done, c + 1)
                dve.wait_ge(tau_ready, c + 1)
                dve.scalar_tensor_tensor(out=half(qc, c), in0=four(5 + c), scalar=foldb[:, 0:1], in1=half(tauT, c),
                                         op0=ALU.add, op1=ALU.mult).then_inc(q_ready, 1)

            def low_queries(n, c):
                dve.wait_ge(qhi_ready, 2 * n + c + 1)
                dve.tensor_tensor(half(qhl[:, 1, :, :], c), half(qc, c), half(qhl[:, 0, :, :], c).bitcast(F32),
                                  ALU.subtract).then_inc(qlo_ready, 1)

            def low_keys(n, c, b, bias):
                dve.wait_ge(khi_ready, 2 * n + c + 1)
                dve.scalar_tensor_tensor(out=half(khl[n][:, 1, :, :], c), in0=four(b), scalar=bias,
                                         in1=half(khl[n][:, 0, :, :], c).bitcast(F32), op0=ALU.add,
                                         op1=ALU.subtract).then_inc(klo_ready, 1)

            dve.wait_ge(fold_copied, 4)
            low_keys(0, 0, 7, foldb[:, 1:2])
            low_queries(0, 0)
            low_keys(0, 1, 0, foldb[:, 1:2])
            dve.wait_ge(ld_b, 16)
            low_keys(1, 0, 1, Bw("bk"))
            for g in range(G):
                dve.wait_ge(q_stacked, g + 1)
                dve.tensor_copy(half(qst[:, g, :, :], 0), four(5 + g % 2)).then_inc(qst_ready, 1)
            low_keys(1, 1, 2, Bw("bk"))
            dve.wait_ge(kst_ready, G)
            for j in range(2, J):
                r = slice(32 * j, 32 * j + 32)
                last = dve.tensor_copy(kbd[r, 0, :, j, :], kst[0][r, :, 0, :].bitcast(F32))
            last.then_inc(kbd_first, 1)
            low_queries(0, 1)

            def maximum(s, g):
                i = G * s + g
                dve.wait_ge(scored, i + 1)
                dve.tensor_reduce(rawmax[:, s % 2, g, :].unsqueeze(2), bank[i % 2][:, :].rearrange("p (j k) -> p j k", j=J),
                                  AX.X, ALU.max, negate=True).then_inc(maxed, 1)

            def split_max(s):
                dve.wait_ge(maxed, G * s + G)
                wait(dve, max_turned, s)
                cols = negmax[:, :, :].rearrange("p g (j c) -> p g j c", j=J)
                link(dve.tensor_copy(cols[:, :, :, 0:1].bitcast(F32R), rawmax[:, s % 2, :, :].unsqueeze(3)))
                dve.tensor_tensor(cols[:, :, :, 1:2], rawmax[:, s % 2, :, :].unsqueeze(3), cols[:, :, :, 0:1],
                                  ALU.subtract).then_inc(max_split, 1)

            def queries_with_max(s):
                dve.wait_ge(max_turned, s + 1)
                wait(dve, scoredT, G * (s - 1))
                for j in range(2, J):
                    r = slice(32 * j, 32 * j + 32)
                    last = dve.tensor_copy(qbd[r, s % 2, :, j, :], bank[5][r, :].rearrange("p (g t) -> p g t", g=G))
                last.then_inc(qbd_ready, 1)

            def norm(s):
                dve.wait_ge(o_turned, s + 1)
                o = bank[6][:, :].rearrange("p (h c) -> p h c", h=H)
                link(dve.reciprocal(rec[:, :].unsqueeze(2), o[:, :, DK:DK + 1]))
                wait(dve, on_turned, s)
                dve.tensor_tensor(on[:, :, :], o[:, :, 0:DK], rec[:, :].unsqueeze(2).broadcast_to([P, H, DK]),
                                  ALU.mult).then_inc(normed, 1)

            def add_residual(s):
                b = s % B
                dve.wait_ge(projected, s + 1)
                dve.wait_ge(bias_added, 1 if s < B else 2 + b // 4)
                dve.tensor_tensor(xres[:, b, :], xres[:, b, :], bank[6][:, P:2 * P], ALU.add).then_inc(residual, 1)
                dve.wait_ge(residual, s + 1)
                stats_of(b)

            def low_gate_up(it, k):
                dve.wait_ge(whigu_ready, BODY * it + (k + 1))
                dve.tensor_tensor(wlogu[:, k % 4, :, :], ring[:, k % RING, 0:2, :], whigu[:, k % 4, :, :].bitcast(F32),
                                  ALU.subtract).then_inc(wlogu_ready, 1)

            def note(ins):
                ins.then_inc(dve_step, 1)
                steps[0] += 1

            NG = HB * GE
            taken = [HE]

            def scratch(n):
                taken[0] += n
                return flat_k[:, taken[0] - n:taken[0]]

            pairs = lambda w: scratch(NG * w).rearrange("p (n e) -> p n e", e=w)
            a4, b4 = pairs(4), pairs(4)
            rounds = [(w, [pairs(w) for _ in range(4)]) for w in (2, 1)]
            gs, rank, wsum = scratch(NG).rearrange("p (b g) -> p b g", g=GE), scratch(NG), scratch(HB)

            half_of = lambda c: slice(HB * c, HB * c + HB)

            def first_sigmoids():
                dve.wait_ge(scores_ready, 1)
                link(dve.tensor_scalar(sc[:, 0:HB, :], sc[:, 0:HB, :], 1.0, None, ALU.add))
                link(dve.reciprocal(sc[:, 0:HB, :], sc[:, 0:HB, :]))

            def score_with_bias(c):
                dve.wait_ge(scores_ready, c + 1)
                link(dve.tensor_tensor(sfc[:, :, :, :].rearrange("p b g e -> p b (g e)"), sc[:, half_of(c), :],
                                       Bw("e_bias").unsqueeze(1).broadcast_to([P, HB, E]), ALU.add))

            s8 = sfc[:, :, :, :].rearrange("p b g e -> p (b g) e")

            def first_round(c):
                note(dve.tensor_tensor(a4, s8[:, :, 0:4], s8[:, :, 4:8], ALU.max))
                link(dve.tensor_tensor(b4, s8[:, :, 0:4], s8[:, :, 4:8], ALU.min))

            def later_round(i):
                hi, lo = (a4, b4) if i == 0 else (rounds[0][1][0], rounds[0][1][3])
                width, (nh, t1, t2, nl) = rounds[i]
                note(dve.tensor_tensor(t1, hi[:, :, 0:width], hi[:, :, width:2 * width], ALU.min))
                note(dve.tensor_tensor(t2, lo[:, :, 0:width], lo[:, :, width:2 * width], ALU.max))
                link(dve.tensor_tensor(nh, hi[:, :, 0:width], hi[:, :, width:2 * width], ALU.max))
                link(dve.tensor_tensor(nl, t1, t2, ALU.max))

            def last_round():
                later_round(1)
                hi, lo = rounds[1][1][0], rounds[1][1][3]
                link(dve.tensor_tensor(gs, hi[:, :, 0].rearrange("p (b g) -> p b g", g=GE),
                                       lo[:, :, 0].rearrange("p (b g) -> p b g", g=GE), ALU.add))

            def last_rounds(c):
                later_round(0)
                last_round()

            f2 = lambda i: gcmp[:, i, :, :, :].rearrange("p b g f -> p b (g f)")

            def compare_groups(c):
                other = gs.unsqueeze(2).broadcast_to([P, HB, GE, GE])
                own = gs.unsqueeze(3).broadcast_to([P, HB, GE, GE])
                note(dve.tensor_tensor(gcmp[:, 0, :, :, :], other, own, ALU.is_gt))
                link(dve.tensor_tensor(gcmp[:, 1, :, :, :], other, own, ALU.is_equal))

            def rank_groups(c):
                dve.wait_ge(ones_ready, 3 + GE)
                lowb = low[:, :, :].rearrange("p g f -> p (g f)").unsqueeze(1).broadcast_to([P, HB, GE * GE])
                link(dve.tensor_tensor(f2(2), f2(1), lowb, ALU.mult))
                link(dve.tensor_tensor(f2(0), f2(0), f2(2), ALU.add))

            def mask_groups(c):
                link(dve.tensor_reduce(rank, gcmp[:, 0, :, :, :].rearrange("p b g f -> p (b g) f"), AX.X, ALU.add))
                link(dve.scalar_tensor_tensor(out=masked[:, :, :].rearrange("p b (g e) -> p (b g) e", g=GE),
                                              in0=rank.unsqueeze(2).broadcast_to([P, NG, E // GE]),
                                              scalar=TOP_GROUPS - 0.5, in1=s8, op0=ALU.is_lt, op1=ALU.mult))

            def pick_eight(c):
                for b in range(HB):
                    dve.max(top8[:, b, :], masked[:, b, :]).then_inc(dve_step, 1)
                steps[0] += HB
                dve.wait_ge(dve_step, steps[0])
                for b in range(HB):
                    dve.match_replace(replaced[:, b, :], top8[:, b, :], masked[:, b, :], TAKEN).then_inc(dve_step, 1)
                steps[0] += HB
                dve.wait_ge(dve_step, steps[0])

            def keep_scores(c):
                wait(dve, rowsT_done, c)
                link(dve.scalar_tensor_tensor(out=coef[:, :, :], in0=replaced[:, :, :], scalar=TAKEN / 2,
                                              in1=sc[:, half_of(c), :], op0=ALU.is_lt, op1=ALU.mult))

            def sum_scores(c):
                link(dve.tensor_reduce(wsum, coef[:, :, :], AX.X, ALU.add))
                link(dve.tensor_scalar(wsum, wsum, 1e-20, None, ALU.add))
                link(dve.reciprocal(wsum, wsum))

            def coefficients(c):
                dve.scalar_tensor_tensor(out=coef[:, :, :], in0=coef[:, :, :], scalar=ROUTE_SCALE,
                                         in1=wsum.unsqueeze(2).broadcast_to([P, HB, E]), op0=ALU.mult,
                                         op1=ALU.mult).then_inc(coef_ready, 1)
                dve.wait_ge(coef_ready, c + 1)
                if c == 0:
                    link(dve.tensor_copy(chl[:, :, 0, :], coef[:, :, :]))
                    dve.tensor_tensor(chl[:, :, 1, :], coef[:, :, :], chl[:, :, 0, :], ALU.subtract)\
                        .then_inc(chl_ready, 1)

            def second_stacked(c, g):
                dve.wait_ge(q_stacked, G * (2 + c) + g + 1)
                dve.tensor_copy(half(qst[:, g, :, :], c), four(5)).then_inc(qst_odd, 1)

            dve.wait_ge(rows_ready, 3)
            dve.wait_ge(ones_ready, 3)
            dve.wait_ge(delta_done, 1)
            dve.tensor_tensor(edelta[:, :, :], bank[3][:, 0:B * H].rearrange("p (b h) -> p b h", b=B),
                              A("del2b").unsqueeze(1).broadcast_to([P, B, H]), ALU.add).then_inc(delta_sum, 1)
            maximum(0, 0)
            maximum(0, 1)
            values(0, 0, A("bv"), 6)
            maximum(0, 2)
            maximum(0, 3)
            values(0, 1, A("bv"), 4)
            dve.wait_ge(v_copied, 2)
            dve.memset(bank[4][:, :], 0.0).then_inc(bank4_zeroed, 1)
            for s in range(STEPS + 1):
                ahead = s + 1 < STEPS
                early = ahead and s not in (7, 11)
                if s < STEPS:
                    split_max(s)
                if early:
                    maximum(s + 1, 0)
                if s < STEPS:
                    queries_with_max(s)
                if early:
                    maximum(s + 1, 1)
                if s in (2, 3):
                    values(1, s - 2, Bw("bv"), 7)
                if ahead and not early:
                    c = 0 if s == 7 else 1
                    dve.wait_ge(qhi_ready, 3 + c)
                    dve.scalar_tensor_tensor(out=half(qhl[:, 1, :, :], c), in0=four(7), scalar=Bw("bq"),
                                             in1=half(qhl[:, 0, :, :], c).bitcast(F32), op0=ALU.add,
                                             op1=ALU.subtract).then_inc(qlo_ready, 1)
                if s >= 2:
                    add_residual(s - 2)
                if early:
                    maximum(s + 1, 2)
                    maximum(s + 1, 3)
                elif ahead:
                    second_stacked(c, 1)
                    maximum(s + 1, 0)
                    maximum(s + 1, 1)
                    second_stacked(c, 3)
                if s == STEPS - 1:
                    first_sigmoids()
                if s == STEPS:
                    last_round()
                if s >= 1:
                    norm(s - 1)
                if s == STEPS - 1:
                    score_with_bias(0)
                    first_round(0)
                    later_round(0)
                if ahead and not early:
                    maximum(s + 1, 2)
                    maximum(s + 1, 3)
            compare_groups(0)
            rank_groups(0)
            mask_groups(0)
            add_residual(STEPS - 1)
            pick_eight(0)
            keep_scores(0)
            sum_scores(0)
            coefficients(0)
            def gate_times_up(it, k):
                n, p = BODY * it + k, k % 2
                dve.wait_ge(silu_done, n + 1)
                dve.wait_ge(up_done, n + 1)
                dve.tensor_tensor(gu[:, 4 * p:4 * p + 4, :], sg[:, 4 * p:4 * p + 4, :], four(4 + p), ALU.mult)\
                    .then_inc(gu_done, 1)
                if not isinstance(it, int) or 1 <= n < UNITS - 2:
                    low_gate_up(it, k + 2)

            def unit(it, k):
                n, p = BODY * it + k, k % 2
                peeled = isinstance(it, int)
                if not peeled or n != 1:
                    gate_times_up(it, k)
                dve.wait_ge(gu_done, n + 1)
                wait(dve, hlo_ready, n + (-3))
                if peeled and n % PER_HALF == 0:
                    dve.tensor_copy(hx[k % 4], gu[:, 4 * p:4 * p + 4, :]).then_inc(h_done, 1)
                else:
                    if peeled and n < FIRST:
                        dve.wait_ge(coefb_done, n)
                        factor = four(6 + p)
                    else:
                        dve.wait_ge(ld_c[k % ROWS], spread_in(it, k))
                        factor = spread[:, k % ROWS, :, :]
                    dve.tensor_tensor(hx[k % 4], gu[:, 4 * p:4 * p + 4, :], factor, ALU.mult).then_inc(h_done, 1)
                if peeled and n >= UNITS - 2:
                    dve.wait_ge(whid_ready, n + 1)
                    dve.tensor_tensor(wlod[:, k % 4, :], ring[:, k % RING, 2, :], whid[:, k % 4, :].bitcast(F32),
                                      ALU.subtract).then_inc(last_wlod, 1)
                if peeled and n == UNITS - 1:
                    dve.wait_ge(hhi_ready, UNITS)
                    dve.tensor_tensor(hlo[:, k % 4, :].rearrange("p (b t) -> p b t", b=4), hx[k % 4],
                                      hhi[:, k % 4, :].bitcast(F32).rearrange("p (b t) -> p b t", b=4),
                                      ALU.subtract).then_inc(last_hlo, 1)
                if peeled and n == 0:
                    gate_times_up(0, 1)

            SECOND_ROUTER = {8: score_with_bias, 10: first_round, 12: last_rounds, 14: compare_groups, 16: rank_groups,
                             18: mask_groups, 20: pick_eight, 22: keep_scores, 24: sum_scores, 26: coefficients}
            for k in range(PER_HALF - 1):
                unit(0, k)
                if k in SECOND_ROUTER:
                    SECOND_ROUTER[k](1)
            over_units(dve, unit, UNITS, PER_HALF - 1)

        @block.gpsimd
        def _(pool):
            for t in (xnT, qin, kin):
                pool.memset(t[:, :, 0:1], 0.0).then_inc(pads_ready, 1)
                pool.memset(t[:, :, P + 1:P + 2], 0.0).then_inc(pads_ready, 1)
            pool.memset(kbd[:, :, :, :, :].bitcast(F32), 0.0).then_inc(rows_ready, 1)
            pool.memset(pick[:, :, :, :].bitcast(F32), 0.0).then_inc(rows_ready, 1)
            for v in vs:
                pool.memset(v[:, :, :, DK:DK + 1], 1.0).then_inc(ones_ready, 1)
            pool.memset(negmax[:, :, :], 0.0).then_inc(ones_ready, 1)
            pool.memset(qbd[:, :, :, :, :].bitcast(F32), 0.0).then_inc(rows_ready, 1)
            pool.memset(low[:, :, :], 0.0).then_inc(ones_ready, 1)
            pool.wait_ge(ones_ready, 4)
            for g in range(1, GE):
                pool.memset(low[:, g, 0:g], 1.0).then_inc(ones_ready, 1)
            pool.wait_ge(ld_a, 16)
            add_bias(pool, A("bo"), 0, B, B)
            pool.wait_ge(ld_mask, 16)
            pool.tensor_scalar(maskb[:, :, :], masku[:, :, :], MASKED, None, ALU.mult).then_inc(mask_ready, 1)
            link, steps = chain(pool, pool_step)
            pool.wait_ge(delta_ready, 2)
            pool.wait_ge(v_copied, 2)
            v0 = vs[0][:, :, :, :].rearrange("p b h d -> p (b h) d")
            pool.tensor_tensor(v0, v0, edelta[:, :, :].rearrange("p b h -> p (b h)").unsqueeze(2)
                               .broadcast_to([P, B * H, DK + 1]), ALU.mult).then_inc(values_scaled, 1)
            pool.wait_ge(exped, G)
            pool.wait_ge(qbd_ready, 1)
            pool.wait_ge(bias_added, 1)
            link(pool.tensor_tensor(i2[:, :], ident[:, 0:E], ident[:, E:2 * E], ALU.add))
            pool.tensor_copy(sel[:, :, :], i2[:, 0:SPREAD].unsqueeze(2).broadcast_to([P, SPREAD, I])).then_inc(sel_ready, 1)
            pool.wait_ge(ld_b, 16)
            for c in range(2):
                normalise(pool, link, 1, 4 * c, 4 * c + 4, False)
                add_bias(pool, Bw("bo"), 4 * c, 4 * c + 4, B + 4 * c + 4)
            def low_inputs(c):
                pool.wait_ge(xhi_ready, c + 1)
                pool.wait_ge(x3T_ready, c + 1)
                pool.tensor_tensor(xhl[:, 1, HALF * c:HALF * c + HALF].rearrange("p (b t) -> p b t", b=4),
                                   xnT[:, 4 * c:4 * c + 4, 1:1 + P],
                                   xhl[:, 0, HALF * c:HALF * c + HALF].bitcast(F32).rearrange("p (b t) -> p b t", b=4),
                                   ALU.subtract).then_inc(xlo_ready, 1)

            def low_down(it, k):
                pool.wait_ge(whid_ready, BODY * it + (k + 1))
                pool.tensor_tensor(wlod[:, k % 4, :], ring[:, k % RING, 2, :], whid[:, k % 4, :].bitcast(F32),
                                   ALU.subtract).then_inc(wlod_ready, 1)

            pool.wait_ge(exped, G * B)
            for k in range(LAG):
                pool.wait_ge(ld_w[k], 16)
                pool.tensor_copy(whigu[:, k, :, :], ring[:, k, 0:2, :]).then_inc(whigu_ready, 1)
                pool.wait_ge(whigu_ready, k + 1)
                pool.tensor_tensor(wlogu[:, k, :, :], ring[:, k, 0:2, :], whigu[:, k, :, :].bitcast(F32),
                                   ALU.subtract).then_inc(wlogu_ready, 1)
                pool.tensor_copy(whid[:, k, :], ring[:, k, 2, :]).then_inc(whid_ready, 1)
                low_down(0, k)
            normalise(pool, link, 2, 0, 4, False)
            low_inputs(0)
            normalise(pool, link, 2, 4, B, False)

            def unit(it, k):
                n = BODY * it + k
                if not isinstance(it, int) or LAG <= n < UNITS - 2:
                    low_down(it, k)
                pool.wait_ge(hhi_ready, n + 1)
                pool.tensor_tensor(hlo[:, k % 4, :].rearrange("p (b t) -> p b t", b=4), hx[k % 4],
                                   hhi[:, k % 4, :].bitcast(F32).rearrange("p (b t) -> p b t", b=4),
                                   ALU.subtract).then_inc(hlo_ready, 1)
                if isinstance(it, int) and n == 5:
                    low_inputs(1)

            over_units(pool, unit, UNITS - 1)


def kernel(**inputs):
    import numpy as np
    import concourse.bacc as bacc
    from concourse.bass_utils import run_bass_kernel_spmd

    a = {k: np.asarray(v) for k, v in inputs.items()}
    att = lambda n: a["L0_attn_" + n]
    xat = lambda n: a["L0_xattn_" + n]
    ffn = lambda n: a["L0_ffn_" + n]
    col = lambda v: v.reshape(P, 1)
    row = lambda v: np.broadcast_to(v.reshape(1, -1), (P, v.size))
    taps = lambda w: w.transpose(0, 2, 1).reshape(P, 3 * P)
    second = lambda w: w.reshape(H, P, 2).transpose(1, 2, 0).reshape(P, 2 * H)
    part_a = dict(
        ident=np.eye(P, dtype=np.float32),
        ones_rows=col(np.float32(np.arange(P) % 32 < 2)), wqT=att("Wq_w").T, wkT=att("Wk_w").T, wvT=att("Wv_w").T,
        cq=taps(att("convq_w")), ck=taps(att("convk_w")),
        qp1T=att("qproj_w")[:, :P].T, qp2T=att("qproj_w")[:, P:].T,
        kp1T=att("kproj_w")[:, :P].T, kp2T=att("kproj_w")[:, P:].T,
        tau1=att("tau1_w").reshape(P, 6), tau1b=att("tau1_b").reshape(P, 2),
        del1=att("del1_w").reshape(P, 6), del1b=att("del1_b").reshape(P, 2),
        tau2T=second(att("tau2_w")), del2T=second(att("del2_w")),
        bq=col(att("Wq_b")), bk=col(att("Wk_b")), cqb=col(att("convq_b")), ckb=col(att("convk_b")),
        qpb=col(att("qproj_b")), kpb=col(att("kproj_b")),
        tau2b=col(np.broadcast_to(att("tau2_b").reshape(H, 1), (H, DK))),
        woT=att("out_w").T, bv=row(att("Wv_b")), bo=row(att("out_b")), del2b=row(att("del2_b")))
    part_b = dict(wq=xat("Wq"), wk=xat("Wk"), wv=xat("Wv"), wo=xat("Wo"), bq=col(xat("bq")), bk=col(xat("bk")),
                  bv=row(xat("bv")), bo=row(xat("bo")), routerT=ffn("router_w").T, e_bias=row(ffn("e_bias")))
    gate = np.concatenate([ffn("SWg").reshape(P, 1, P), ffn("Wg").transpose(1, 0, 2).reshape(P, PAIRS, P)], 1)
    up = np.concatenate([ffn("SWu").reshape(P, 1, P), ffn("Wu").transpose(1, 0, 2).reshape(P, PAIRS, P)], 1)
    down = np.concatenate([ffn("SWd").reshape(P, 1, P), ffn("Wd").reshape(PAIRS, P, P).transpose(1, 0, 2)], 1)
    arrays = {
        "x": a["x"].reshape(T, P),
        "ctxT": a["ctx_1024"].reshape(T, P).T,
        "mask": a["mask_Bx1xSxS2_bk1"].reshape(B, P, P),
        "pack_a": np.concatenate([part_a[n] for n in PACK_A], axis=1),
        "pack_b": np.concatenate([part_b[n] for n in PACK_B], axis=1),
        "w3": np.stack([gate, up, down], axis=2).reshape(P, (PAIRS + 1) * 3 * P),
    }
    arrays = {k: np.ascontiguousarray(v) for k, v in arrays.items()}
    nc = bacc.Bacc("TRN2", target_bir_lowering=False, num_devices=1)
    args = [nc.dram_tensor(k, v.shape, mybir.dt.from_np(v.dtype), kind="ExternalInput").ap() for k, v in arrays.items()]
    outT = nc.dram_tensor("outT", (P, T), F32, kind="ExternalOutput").ap()
    rowsd = nc.dram_tensor("coefficient_rows", (2, E, HALF), F32, kind="Internal").ap()
    decoder_layer(nc, *args, rowsd, outT)
    r = run_bass_kernel_spmd(nc, [arrays], core_ids=[0])
    return np.ascontiguousarray(np.asarray(r.results[0]["outT"]).T).reshape(B, P, P)
```
